# Optimizing a Trainium2 kernel written in Bass

```python
import numpy as np
import jax
import jax.numpy as jnp

def _softmax(x, axis=-1):
    return jax.nn.softmax(x, axis=axis)

def _gelu(x):
    return jax.nn.gelu(x, approximate=True)

def _silu(x):
    return jax.nn.silu(x)

def _sigmoid(x):
    return jax.nn.sigmoid(x)

def _layernorm(x, axis=-1, eps=1e-05):
    m = jnp.mean(x, axis=axis, keepdims=True)
    v = jnp.var(x, axis=axis, keepdims=True)
    return (x - m) / jnp.sqrt(v + eps)

def _scatter_add(tgt, idx, src, axis=0):
    return tgt.at[idx].add(src)

def _segment_sum(src, seg, n):
    return jax.ops.segment_sum(src, seg, n)
kernel_name = 'mk_perceiver_d1_seqx_r2_4f5e55'

def setup_inputs(seed: int=0):
    np.random.seed(seed)
    _w = jnp.asarray

    def _rec_inputs():
        import jax
        import jax.numpy as jnp
        _rk = jax.random.key(seed)
        x = 0.0003765 + 1 * jax.random.normal(jax.random.fold_in(_rk, 1), (1, 256, 512), jnp.float32)
        _lenS = 256 - jax.random.randint(jax.random.fold_in(_rk, 7), (1,), 0, max(1, 256 // 4) + 1, jnp.int32)
        _lenS2 = 25088 - jax.random.randint(jax.random.fold_in(_rk, 8), (1,), 0, max(1, 25088 // 4) + 1, jnp.int32)
        _ctx_1024P = jax.random.normal(jax.random.fold_in(_rk, 11), (1, 16, 512), jnp.float32)
        _ctx_1024c = jax.random.dirichlet(jax.random.fold_in(_rk, 511), 0.3 * jnp.ones((16,), jnp.float32), (1, 25088))
        _ctx_1024t = jnp.einsum('bsk,bkd->bsd', _ctx_1024c, _ctx_1024P)
        _ctx_1024t = _ctx_1024t * jax.lax.rsqrt(jnp.mean(jnp.square(_ctx_1024t)) + 1e-12) * 0.953939
        ctx_1024 = -0.000292821 + 1.00034 * (_ctx_1024t + 0.3 * jax.random.normal(jax.random.fold_in(_rk, 611), (1, 25088, 512), jnp.float32))
        _validS = jnp.arange(256)[None, :] < _lenS[:, None]
        _validS2 = jnp.arange(25088)[None, :] < _lenS2[:, None]
        _causal = jnp.tril(jnp.ones((256, 256), dtype=bool))
        mask_Bx1xSxS2_ik1 = jnp.where(jnp.broadcast_to(_validS2[:, None, None, :], (1, 1, 256, 25088)), 1, 0).astype(jnp.int32)
        return (x, ctx_1024, mask_Bx1xSxS2_ik1)
    x, ctx_1024, mask_Bx1xSxS2_ik1 = _rec_inputs()

    def _L0_xattn_setup():
        import jax, jax.numpy as jnp
        import numpy as np
        EMBED = 512
        HEADS = 16
        HEAD_DIM = EMBED // HEADS
        key = jax.random.key(seed)
        ks = jax.random.split(key, 9)
        N, L = (2, 1024)
        inp = {'values': jax.random.normal(ks[0], (N, L, EMBED), dtype=jnp.float32), 'keys': jax.random.normal(ks[1], (N, L, EMBED), dtype=jnp.float32), 'query': jax.random.normal(ks[2], (N, L, EMBED), dtype=jnp.float32), 'mask': jax.random.randint(ks[3], (N, 1, L, L), 0, 2, dtype=jnp.int32), 'Wv': jax.random.normal(ks[4], (HEAD_DIM, HEAD_DIM), dtype=jnp.float32) / np.sqrt(HEAD_DIM), 'Wk': jax.random.normal(ks[5], (HEAD_DIM, HEAD_DIM), dtype=jnp.float32) / np.sqrt(HEAD_DIM), 'Wq': jax.random.normal(ks[6], (HEAD_DIM, HEAD_DIM), dtype=jnp.float32) / np.sqrt(HEAD_DIM), 'Wo': jax.random.normal(ks[7], (EMBED, EMBED), dtype=jnp.float32) / np.sqrt(EMBED), 'bo': jax.random.normal(ks[8], (EMBED,), dtype=jnp.float32) * 0.02}
        return inp
    _L0_xattn_all = _L0_xattn_setup()
    _L0_xattn_in = {k: v for k, v in _L0_xattn_all.items() if k in ('Wv', 'Wk', 'Wq', 'Wo', 'bo')}
    del _L0_xattn_all

    def _L0_attn_setup():
        import jax, jax.numpy as jnp
        import numpy as np
        B, S, H, NH, P = (1, 1024, 512, 16, 2)
        D = H // NH
        SCALE = 1.0 / np.sqrt(D).astype(np.float32)

        def _lin(x, W, b):
            return x @ W + b

        def _split_heads(x):
            return x.reshape(*x.shape[:-2], x.shape[-2], NH, D).swapaxes(-3, -2)

        def _merge_heads(x):
            return x.swapaxes(-3, -2).reshape(*x.shape[:-3], x.shape[-2], H)
        key = jax.random.key(seed)
        ks = jax.random.split(key, 20)
        w = lambda k, i, o: jax.random.normal(k, (i, o), jnp.float32) * 0.02
        inp = {'hidden_states': jax.random.normal(ks[0], (B, S, H), jnp.float32), 'past_states': jax.random.normal(ks[1], (P, B, S, H), jnp.float32), 'Wq': w(ks[2], H, H), 'bq': jnp.zeros((H,), jnp.float32), 'Wk': w(ks[3], H, H), 'bk': jnp.zeros((H,), jnp.float32), 'Wv': w(ks[4], H, H), 'bv': jnp.zeros((H,), jnp.float32), 'Wo': w(ks[5], H, H), 'bo': jnp.zeros((H,), jnp.float32), 'Wrq': w(ks[6], H, H), 'brq': jnp.zeros((H,), jnp.float32), 'Wrk': w(ks[7], H, H), 'brk': jnp.zeros((H,), jnp.float32), 'Wrv': w(ks[8], H, H), 'brv': jnp.zeros((H,), jnp.float32), 'Wg': w(ks[9], 2 * H, H), 'bg': jnp.zeros((H,), jnp.float32)}
        return inp
    _L0_attn_all = _L0_attn_setup()
    _L0_attn_in = {k: v for k, v in _L0_attn_all.items() if k in ('past_states', 'Wq', 'bq', 'Wk', 'bk', 'Wv', 'bv', 'Wo', 'bo', 'Wrq', 'brq', 'Wrk', 'brk', 'Wrv', 'brv', 'Wg', 'bg')}
    del _L0_attn_all

    def _L0_ffn_setup():
        import jax, jax.numpy as jnp
        import numpy as np
        B, S, D, E, F = (2, 512, 512, 14, 1024)
        key = jax.random.key(seed)
        k0, k1, k2, k3 = jax.random.split(key, 4)
        h = jax.random.normal(k0, (B, S, D), jnp.float32)
        gate_w = jax.random.normal(k1, (E, D), jnp.float32) * 0.02
        w1 = jax.random.normal(k2, (E, D, F), jnp.float32) * (1.0 / np.sqrt(D).astype(np.float32))
        b1 = jnp.zeros((E, F), jnp.float32)
        w2 = jax.random.normal(k3, (E, F, D), jnp.float32) * (1.0 / np.sqrt(F).astype(np.float32))
        b2 = jnp.zeros((E, D), jnp.float32)
        return {'h': h, 'gate_w': gate_w, 'w1': w1, 'b1': b1, 'w2': w2, 'b2': b2}
    _L0_ffn_all = _L0_ffn_setup()
    _L0_ffn_in = {k: v for k, v in _L0_ffn_all.items() if k in ('gate_w', 'w1', 'b1', 'w2', 'b2')}
    del _L0_ffn_all
    return {'x': x, 'ctx_1024': ctx_1024, 'mask_Bx1xSxS2_ik1': mask_Bx1xSxS2_ik1, 'L0_xattn_Wv': _L0_xattn_in['Wv'], 'L0_xattn_Wk': _L0_xattn_in['Wk'], 'L0_xattn_Wq': _L0_xattn_in['Wq'], 'L0_xattn_Wo': _L0_xattn_in['Wo'], 'L0_xattn_bo': _L0_xattn_in['bo'], 'L0_attn_past_states': _L0_attn_in['past_states'], 'L0_attn_Wq': _L0_attn_in['Wq'], 'L0_attn_bq': _L0_attn_in['bq'], 'L0_attn_Wk': _L0_attn_in['Wk'], 'L0_attn_bk': _L0_attn_in['bk'], 'L0_attn_Wv': _L0_attn_in['Wv'], 'L0_attn_bv': _L0_attn_in['bv'], 'L0_attn_Wo': _L0_attn_in['Wo'], 'L0_attn_bo': _L0_attn_in['bo'], 'L0_attn_Wrq': _L0_attn_in['Wrq'], 'L0_attn_brq': _L0_attn_in['brq'], 'L0_attn_Wrk': _L0_attn_in['Wrk'], 'L0_attn_brk': _L0_attn_in['brk'], 'L0_attn_Wrv': _L0_attn_in['Wrv'], 'L0_attn_brv': _L0_attn_in['brv'], 'L0_attn_Wg': _L0_attn_in['Wg'], 'L0_attn_bg': _L0_attn_in['bg'], 'L0_ffn_gate_w': _L0_ffn_in['gate_w'], 'L0_ffn_w1': _L0_ffn_in['w1'], 'L0_ffn_b1': _L0_ffn_in['b1'], 'L0_ffn_w2': _L0_ffn_in['w2'], 'L0_ffn_b2': _L0_ffn_in['b2']}

def reference(x, ctx_1024, mask_Bx1xSxS2_ik1, L0_xattn_Wv, L0_xattn_Wk, L0_xattn_Wq, L0_xattn_Wo, L0_xattn_bo, L0_attn_past_states, L0_attn_Wq, L0_attn_bq, L0_attn_Wk, L0_attn_bk, L0_attn_Wv, L0_attn_bv, L0_attn_Wo, L0_attn_bo, L0_attn_Wrq, L0_attn_brq, L0_attn_Wrk, L0_attn_brk, L0_attn_Wrv, L0_attn_brv, L0_attn_Wg, L0_attn_bg, L0_ffn_gate_w, L0_ffn_w1, L0_ffn_b1, L0_ffn_w2, L0_ffn_b2):
    import jax
    import jax.numpy as jnp

    def _L0_xattn_ref(values, keys, query, mask, Wv, Wk, Wq, Wo, bo):
        import jax, jax.numpy as jnp
        import numpy as np
        EMBED = 512
        HEADS = 16
        HEAD_DIM = EMBED // HEADS
        N, Lq = (query.shape[0], query.shape[1])
        Lk = keys.shape[1]
        v = values.reshape(N, Lk, HEADS, HEAD_DIM)
        k = keys.reshape(N, Lk, HEADS, HEAD_DIM)
        q = query.reshape(N, Lq, HEADS, HEAD_DIM)
        v = jnp.einsum('nlhd,ed->nlhe', v, Wv)
        k = jnp.einsum('nlhd,ed->nlhe', k, Wk)
        q = jnp.einsum('nqhd,ed->nqhe', q, Wq)
        energy = jnp.einsum('nqhd,nkhd->nhqk', q, k) / np.sqrt(HEAD_DIM).astype(np.float32)
        energy = jnp.where(mask == 0, jnp.float32(-1e+20), energy)
        attn = jax.nn.softmax(energy, axis=-1)
        out = jnp.einsum('nhql,nlhd->nqhd', attn, v).reshape(N, Lq, EMBED)
        return out @ Wo.T + bo

    def _L0_attn_ref(hidden_states, past_states, Wq, bq, Wk, bk, Wv, bv, Wo, bo, Wrq, brq, Wrk, brk, Wrv, brv, Wg, bg):
        import jax, jax.numpy as jnp
        import numpy as np
        B, S, H, NH, P = (1, 1024, 512, 16, 2)
        D = H // NH
        SCALE = 1.0 / np.sqrt(D).astype(np.float32)

        def _lin(x, W, b):
            return x @ W + b

        def _split_heads(x):
            return x.reshape(*x.shape[:-2], x.shape[-2], NH, D).swapaxes(-3, -2)

        def _merge_heads(x):
            return x.swapaxes(-3, -2).reshape(*x.shape[:-3], x.shape[-2], H)
        q = _split_heads(_lin(hidden_states, Wq, bq))
        k = _split_heads(_lin(hidden_states, Wk, bk))
        v = _split_heads(_lin(hidden_states, Wv, bv))
        scores = jnp.einsum('bhsd,bhtd->bhst', q, k) * SCALE
        attn = jax.nn.softmax(scores, axis=-1)
        ctx = jnp.einsum('bhst,bhtd->bhsd', attn, v)
        output = _lin(_merge_heads(ctx), Wo, bo)
        rq = _split_heads(_lin(output, Wrq, brq))
        rk = _split_heads(_lin(past_states, Wrk, brk))
        rv = _split_heads(_lin(past_states, Wrv, brv))
        rscores = jnp.einsum('bhsd,pbhtd->pbhst', rq, rk) * SCALE
        rattn = jax.nn.softmax(rscores, axis=-1)
        rctx = jnp.einsum('pbhst,pbhtd->pbhsd', rattn, rv)
        recursive_output = _merge_heads(rctx).mean(axis=0)
        gate = jax.nn.sigmoid(_lin(jnp.concatenate([output, recursive_output], axis=-1), Wg, bg))
        output = output * (1.0 - gate) + recursive_output * gate
        return output

    def _L0_ffn_ref(h, gate_w, w1, b1, w2, b2):
        import jax, jax.numpy as jnp
        import numpy as np
        B, S, D, E, F = (2, 512, 512, 14, 1024)
        Bb, Ss, Dd = h.shape
        x = h.reshape(Bb * Ss, Dd)
        logits = x @ gate_w.T
        probs = jax.nn.softmax(logits, axis=-1)
        top2_p, top2_i = jax.lax.top_k(probs, 2)
        w = top2_p / jnp.maximum(top2_p.sum(-1, keepdims=True), 1e-10)
        hh = jnp.einsum('nd,edf->nef', x, w1) + b1
        hh = jax.nn.gelu(hh, approximate=False)
        all_out = jnp.einsum('nef,efd->ned', hh, w2) + b2
        n = jnp.arange(x.shape[0])
        out0 = all_out[n, top2_i[:, 0]]
        out1 = all_out[n, top2_i[:, 1]]
        moe_out = w[:, 0:1] * out0 + w[:, 1:2] * out1
        result = jnp.clip(x + moe_out, -100.0, 100.0).reshape(Bb, Ss, Dd)
        return result
    x = x + _L0_xattn_ref(ctx_1024, ctx_1024, _layernorm(x, axis=-1), mask_Bx1xSxS2_ik1, L0_xattn_Wv, L0_xattn_Wk, L0_xattn_Wq, L0_xattn_Wo, L0_xattn_bo)
    x = x + _L0_attn_ref(_layernorm(x, axis=-1), L0_attn_past_states, L0_attn_Wq, L0_attn_bq, L0_attn_Wk, L0_attn_bk, L0_attn_Wv, L0_attn_bv, L0_attn_Wo, L0_attn_bo, L0_attn_Wrq, L0_attn_brq, L0_attn_Wrk, L0_attn_brk, L0_attn_Wrv, L0_attn_brv, L0_attn_Wg, L0_attn_bg)
    x = x + _L0_ffn_ref(_layernorm(x, axis=-1), L0_ffn_gate_w, L0_ffn_w1, L0_ffn_b1, L0_ffn_w2, L0_ffn_b2)
    return x

_drawn_inputs = setup_inputs


def setup_inputs(seed=0):
    import zlib

    import numpy as np

    out = dict(_drawn_inputs(seed))
    spreads = {'L0_attn_bq': (0.0, 0.8),
     'L0_attn_bk': (0.0, 2.0),
     'L0_attn_bv': (0.0, 0.1),
     'L0_attn_bo': (0.0, 0.1),
     'L0_attn_brq': (0.0, 0.8),
     'L0_attn_brk': (0.0, 2.0),
     'L0_attn_brv': (0.0, 0.1),
     'L0_attn_bg': (0.0, 0.385),
     'L0_ffn_b1': (0.0, 0.355),
     'L0_ffn_b2': (0.0, 0.487)}
    factors = {'L0_attn_past_states': 3.62,
     'L0_attn_Wq': 8.0,
     'L0_attn_Wk': 8.0,
     'L0_attn_Wrq': 8.0,
     'L0_attn_Wrk': 8.0,
     'L0_attn_Wrv': 4.736,
     'L0_attn_Wg': 3.119}
    for name, (base, spread) in spreads.items():
        noise = np.random.default_rng([zlib.crc32(name.encode()), seed]).standard_normal(out[name].shape)
        drawn = base * np.exp(spread * noise) if base else spread * noise
        out[name] = jnp.asarray(drawn.astype(out[name].dtype))
    for name, factor in factors.items():
        out[name] = (out[name] * factor).astype(out[name].dtype)
    return out
```

```python
from contextlib import ExitStack

import numpy as np

import concourse.bass as bass
from concourse import mybir

F32 = mybir.dt.float32
F32R = mybir.dt.float32r
I32 = mybir.dt.int32
U32 = mybir.dt.uint32
ALU = mybir.AluOpType
ACT = mybir.ActivationFunctionType
AX = mybir.AxisListType.X
AXY = mybir.AxisListType.XY
RMAX = bass.bass_isa.ReduceOp.max

P = 128
SQ = 256
D = 512
NH = 16
HD = D // NH
SK = 25088
NT = SK // P
U = 4
TURNS = NT // U
CT = D // P
HG = NH // CT
QT = SQ // P
STACK = 3 * HD
KROWS = STACK + 1
NP = 2
SP_ = 1024
NE = 14
FF = 1024
FT = FF // P
SCALE = 1.0 / float(np.sqrt(np.float32(HD)))
EPS = 1e-5
MASKED = -1e20
HIDE = -1e30
DEN_MIN, DEN_MAX = 1e-25, 1e30


def wait(eng, sem, value):
    if not isinstance(value, int) or value > 0:
        eng.wait_ge(sem, value)


class Chain:

    def __init__(self, eng, sem):
        self.eng, self.sem, self.n = eng, sem, 0

    def __call__(self, ins):
        self.n += 1
        ins.then_inc(self.sem, 1)
        self.eng.wait_ge(self.sem, self.n)


def build(nc, a, out):
    with ExitStack() as ctx:
        def sem(name):
            return ctx.enter_context(nc.semaphore(name))

        keep = Buffers(nc, ctx)
        ident = keep.sb("ident", [P, P])
        ones = keep.sb("ones", [P, P])
        xres = keep.sb("xres", [P, QT, D])
        weights = {n: keep.sb(f"w_{n}", [P, CT, D]) for n in ("q", "k", "v", "o")}
        w_ready = sem("w_ready")
        with ExitStack() as mem:
            cross_attention(nc, Buffers(nc, mem), sem, a, ident, ones, xres, weights, w_ready)
        with ExitStack() as mem:
            self_attention(nc, Buffers(nc, mem), sem, a, ident, ones, xres, weights, w_ready)
        with ExitStack() as mem:
            experts(nc, Buffers(nc, mem), sem, a, ident, ones, xres, out)


class Buffers:
    def __init__(self, nc, mem):
        self.nc, self.mem = nc, mem

    def sb(self, name, shape, dt=F32):
        return self.mem.enter_context(self.nc.sbuf_tensor(name, shape, dt))

    def ps(self, name, shape, dt=F32):
        return self.mem.enter_context(self.nc.psum_tensor(name, shape, dt))


class Norm:

    def __init__(self, name, mem, sem, xres, out):
        self.x, self.out = xres, out
        self.stats = mem.sb(f"{name}_stats", [P, QT, 6])
        self.mv = mem.sb(f"{name}_mv", [P, QT, 2])
        self.ve = mem.sb(f"{name}_ve", [P, QT])
        self.std = mem.sb(f"{name}_std", [P, QT])
        self.inv = mem.sb(f"{name}_inv", [P, QT])
        self.tmp = mem.sb(f"{name}_tmp", [P, QT])
        self.var_ready, self.std_ready = sem(f"{name}_var_ready"), sem(f"{name}_std_ready")
        self.ready = sem(f"{name}_ready")

    def vector(self, dve, link):
        for t in range(QT):
            link(dve.bn_stats(self.stats[:, t, :], self.x[:, t, :]))
            link(dve.bn_aggr(self.mv[:, t, :], self.stats[:, t, :]))
        dve.tensor_scalar(self.ve[:], self.mv[:, :, 1], EPS, None, ALU.add).then_inc(self.var_ready, 1)
        dve.wait_ge(self.std_ready, 1)
        link(dve.reciprocal(self.inv[:], self.std[:]))
        link(dve.tensor_tensor(self.tmp[:], self.inv[:], self.inv[:], ALU.mult))
        link(dve.tensor_tensor(self.tmp[:], self.tmp[:], self.ve[:], ALU.mult))
        link(dve.tensor_scalar(self.tmp[:], self.tmp[:], -0.5, 1.5, ALU.mult, ALU.add))
        link(dve.tensor_tensor(self.inv[:], self.inv[:], self.tmp[:], ALU.mult))
        for t in range(QT):
            dve.tensor_scalar(self.out[:, t, :], self.x[:, t, :], self.mv[:, t, 0:1], self.inv[:, t:t + 1],
                              ALU.subtract, ALU.mult).then_inc(self.ready, 1)

    def scalar(self, act):
        act.wait_ge(self.var_ready, 1)
        act.activation(self.std[:], self.ve[:], ACT.Sqrt).then_inc(self.std_ready, 1)


def transpose_tokens(pe, dst, src, ident):
    for t in range(CT):
        for m in range(QT):
            last = pe.transpose(dst[:, t, m * P:(m + 1) * P], src[:, m, t * P:(t + 1) * P], ident[:])
    return last


def cross_attention(nc, mem, sem, a, ident, ones, xres, weights, w_ready):
    xn = mem.sb("xn", [P, QT, D])
    bd_q = mem.sb("bd_q", [P, P])
    bd_k = mem.sb("bd_k", [P, HG, STACK])
    bd_v = mem.sb("bd_v", [P, P])
    wo = mem.sb("x_wo", [P, CT, D])
    bo = mem.sb("x_bo", [P, D])
    tok = mem.sb("x_tok", [P, CT, SQ])
    tok2 = mem.sb("x_tok2", [P, CT, SQ])
    nat = mem.sb("nat", [P, U, D])
    msk = mem.sb("msk", [P, U, SQ], I32)
    mask_min = mem.sb("mask_min", [P, NT])
    mask_max = mem.sb("mask_max", [P, NT])
    bias = mem.sb("bias", [P, U])
    split = mem.sb("split", [P, 2, NH, 3, HD])
    kst = mem.sb("kst", [KROWS, 2, NH, P], F32R)
    qst = mem.sb("qst", [KROWS, NH, SQ], F32R)
    probs = mem.sb("probs", [P, U, HG, SQ])
    den = mem.sb("den", [P, CT, HG, SQ])
    top = mem.sb("top", [P, CT, HG, SQ])
    tmp = mem.sb("x_tmp", [P, HG, SQ])
    mbias = mem.sb("mbias", [P, SQ])
    sums = mem.sb("sums", [P, 4])
    flag = mem.sb("flag", [1, 1], I32)
    sc = mem.ps("sc", [P, 2, HG, SQ])
    tr = mem.ps("tr", [P, 2, HG, P])
    acc = mem.ps("acc", [P, CT, SQ])

    norm = Norm("xnorm", mem, sem, xres, xn)
    S = {n: sem("x_" + n) for n in (
        "x_in", "small", "wo_in", "id0", "id", "ones", "dv", "tokT", "tokE", "q1", "q1E", "qr", "qrE", "qs",
        "split", "hi", "tr", "ks_dve", "ks_act", "probe_sc", "probe_cp", "shift", "shift_in", "score", "exp", "pv",
        "den_dve", "den_pool", "bias", "mask_used", "zero", "den_sum", "okrow", "oksum", "flag",
        "norm", "vp", "vpE", "proj", "done",
        "rows_set", "g_free", "g_row", "g_mask", "g_split", "g_tr", "g_ks", "g_sc", "g_arg", "g_exp", "g_pv", "g_max", "g_top",
        "g_fin", "g_dv", "g_zero", "g_den")}
    row_in = [sem(f"row_in{u}") for u in range(U)]
    mask_in = [sem(f"mask_in{u}") for u in range(U)]
    rows = a["ctx"].rearrange("(n p) c -> n p c", p=P)
    masks = a["mask_t"].rearrange("(n p) q -> n p q", p=P)

    def per_turn(body, eng):
        body(0)
        with eng.Fori(1, TURNS - 1) as i:
            body(i)
        body(TURNS - 1)

    def last_turn(i):
        return isinstance(i, int) and i == TURNS - 1

    with nc.Block() as block:
        @block.sync
        def _(sp):
            sp.dma_start(xres[:], a["x"].rearrange("(t p) c -> p t c", p=P)).then_inc(S["x_in"], 16)
            sp.dma_start(bd_q[:], a["bd_wq_t"]).then_inc(S["small"], 16)
            sp.dma_start(bd_k[:], a["bd_wk"]).then_inc(S["small"], 16)
            for u in range(U):
                sp.dma_start(nat[:, u, :], rows[u]).then_inc(row_in[u], 16)
                sp.dma_start(msk[:, u, :], masks[u]).then_inc(mask_in[u], 16)
            sp.dma_start(bd_v[:], a["bd_wv_t"]).then_inc(S["wo_in"], 16)
            sp.dma_start(wo[:], a["x_wo_t"].rearrange("(t p) o -> p t o", p=P)).then_inc(S["wo_in"], 16)
            sp.dma_start(bo[:], a["x_bo"].partition_broadcast(P)).then_inc(S["wo_in"], 16)
            with sp.Fori(1, TURNS) as i:
                for u in range(U):
                    sp.wait_ge(S["mask_used"], U * (i - 1) + u + 1)
                    sp.dma_start(msk[:, u, :], masks[U * i + u]).then_inc(mask_in[u], 16)
                    sp.wait_ge(S["pv"], CT * (U * (i - 1) + u + 1))
                    sp.dma_start(nat[:, u, :], rows[U * i + u]).then_inc(row_in[u], 16)
            for n in ("q", "k", "v", "o"):
                sp.dma_start(weights[n][:], a["w" + n].rearrange("(t p) o -> p t o", p=P)).then_inc(w_ready, 16)
            sp.wait_ge(S["flag"], 1)
            general = sp.value_load(flag[0:1, 0:1], min_val=0, max_val=1)
            with sp.If(general):
                for turn in range(2):
                    with sp.Fori(0, NT) as i:
                        sp.wait_ge(S["g_free"], NT * turn + i + 1)
                        sp.dma_start(nat[:, 0, :], rows[i]).then_inc(S["g_row"], 16)
                        sp.dma_start(msk[:, 0, :], masks[i]).then_inc(S["g_mask"], 16)
                sp.wait_ge(S["g_fin"], 1)
            with sp.Else():
                sp.nop()

        @block.gpsimd
        def _(pool):
            pool.memset(ident[:], 0.0).then_inc(S["id0"], 1)
            pool.wait_ge(S["id0"], 1)
            pool.affine_select(out=ident[:], in_=ident[:], compare_op=ALU.not_equal, fill=1.0, base=0,
                               pattern=[[-1, P]], channel_multiplier=1).then_inc(S["id"], 1)
            pool.memset(ones[:], 1.0).then_inc(S["ones"], 1)
            pool.wait_ge(S["probe_cp"], CT)
            pool.partition_all_reduce(den[:], probs[:], P, RMAX).then_inc(S["shift"], 1)
            pool.wait_ge(S["shift_in"], 1)
            pool.memset(den[:, 2:4], 0.0).then_inc(S["den_pool"], 1)

            def body(i):
                for u in range(U):
                    for g in (2, 3):
                        n = CT * (U * i + u) + g
                        pool.wait_ge(S["exp"], n + 1)
                        pool.wait_ge(S["den_pool"], 2 * (U * i + u) + g - 1)
                        pool.tensor_tensor(den[:, g], den[:, g], probs[:, g], ALU.add).then_inc(S["den_pool"], 1)

            per_turn(body, pool)
            pool.wait_ge(S["flag"], 1)
            general = pool.value_load(flag[0:1, 0:1], min_val=0, max_val=1)
            with pool.If(general):
                pool.wait_ge(S["g_max"], 1)
                pool.partition_all_reduce(den[:], top[:], P, RMAX).then_inc(S["g_top"], 1)
                pool.wait_ge(S["g_fin"], 1)
            with pool.Else():
                pool.nop()

        @block.scalar
        def _(act):
            norm.scalar(act)

            def evacuate(i, u, g, tile):
                m = CT * tile + g
                act.wait_ge(S["tr"], m + 1)
                wait(act, S["score"], m - 2 * CT + 1)
                act.activation(kst[0:STACK, (u + 1) % 2, HG * g:HG * (g + 1), :], tr[0:STACK, g % 2],
                               ACT.Copy).then_inc(S["ks_act"], 1)

            evacuate(0, -1, 1, 0)
            evacuate(0, -1, 3, 0)

            def body(i):
                for u in range(U):
                    tile = U * i + u
                    for g in range(CT):
                        n = CT * tile + g
                        if g % 2 and not (last_turn(i) and u == U - 1):
                            evacuate(i, u, g, tile + 1)
                        act.wait_ge(S["bias"], tile + 1)
                        act.wait_ge(S["score"], n + 1)
                        wait(act, S["pv"], n - CT + 1)
                        if g < 2:
                            wait(act, S["den_dve"], 2 * tile + g)
                        else:
                            wait(act, S["den_pool"], 2 * tile + g - 2)
                        act.activation(probs[:, g], sc[:, g % 2], ACT.Exp,
                                       bias=bias[:, u:u + 1]).then_inc(S["exp"], 1)

            per_turn(body, act)
            act.wait_ge(S["flag"], 1)
            general = act.value_load(flag[0:1, 0:1], min_val=0, max_val=1)
            with act.If(general):
                with act.Fori(0, NT) as i:
                    for g in range(CT):
                        act.wait_ge(S["g_arg"], CT * i + g + 1)
                        act.activation(probs[:, 0], tmp[:], ACT.Exp).then_inc(S["g_exp"], 1)
                act.wait_ge(S["g_fin"], 1)
            with act.Else():
                act.nop()

        def general_vector(dve):
            link = Chain(dve, S["g_dv"])
            link(dve.memset(top[:], -3.0e38))
            link(dve.tensor_scalar(qst[STACK:KROWS].rearrange("p h q -> p (h q)"),
                                   ones[STACK:KROWS, 0:1].to_broadcast([1, NH * SQ]), 0.0, None, ALU.mult))
            dve.sem_inc(S["g_free"], 1)
            base = link.n
            for turn in range(2):
                if turn:
                    dve.sem_inc(S["g_max"], 1)
                    dve.wait_ge(S["g_top"], 1)
                    dve.tensor_copy(top[:], den[:]).then_inc(S["g_zero"], 1)
                    dve.wait_ge(S["g_zero"], 1)
                    dve.memset(den[:], 0.0).then_inc(S["g_zero"], 1)
                    dve.memset(acc[:], 0.0).then_inc(S["g_zero"], 1)
                steps = 3 + 2 * CT if turn == 0 else 3 + 3 * CT
                with dve.Fori(0, NT) as i:
                    seen = NT * turn + i
                    n = base + steps * i
                    dve.wait_ge(S["g_row"], 16 * (seen + 1))
                    dve.wait_ge(S["g_mask"], 16 * (seen + 1))
                    dve.tensor_copy(split[:, 0, :, 0:3:2, :].bitcast(F32R),
                                    nat[:, 0, :].rearrange("p (h c) -> p h c", c=HD).unsqueeze(2)
                                    .to_broadcast([P, NH, 2, HD])).then_inc(S["g_dv"], 1)
                    dve.wait_ge(S["g_dv"], n + 1)
                    dve.tensor_tensor(split[:, 0, :, 1, :], nat[:, 0, :].rearrange("p (h c) -> p h c", c=HD),
                                      split[:, 0, :, 0, :], ALU.subtract).then_inc(S["g_dv"], 1)
                    dve.wait_ge(S["g_dv"], n + 2)
                    dve.tensor_scalar(mbias[:], msk[:, 0, :], 0, MASKED, ALU.is_equal, ALU.mult)\
                       .then_inc(S["g_dv"], 1)
                    dve.wait_ge(S["g_dv"], n + 3)
                    dve.sem_inc(S["g_split"], 1)
                    k = n + 3
                    for g in range(CT):
                        dve.wait_ge(S["g_tr"], CT * seen + g + 1)
                        dve.tensor_copy(kst[0:STACK, 0, HG * g:HG * (g + 1), :], tr[0:STACK, 0])\
                           .then_inc(S["g_ks"], 1)
                        dve.wait_ge(S["g_sc"], CT * seen + g + 1)
                        if turn and g:
                            dve.wait_ge(S["g_exp"], CT * i + g)
                        dve.tensor_tensor(tmp[:], sc[:, 0], mbias[:].unsqueeze(1).to_broadcast([P, HG, SQ]),
                                          ALU.add).then_inc(S["g_dv"], 1)
                        dve.wait_ge(S["g_dv"], k + 1)
                        if turn == 0:
                            dve.tensor_tensor(top[:, g], top[:, g], tmp[:], ALU.max).then_inc(S["g_dv"], 1)
                            dve.wait_ge(S["g_dv"], k + 2)
                            k = k + 2
                        else:
                            dve.tensor_tensor(tmp[:], tmp[:], top[:, g], ALU.subtract).then_inc(S["g_dv"], 1)
                            dve.wait_ge(S["g_dv"], k + 2)
                            dve.sem_inc(S["g_arg"], 1)
                            dve.wait_ge(S["g_exp"], CT * i + g + 1)
                            dve.tensor_tensor(den[:, g], den[:, g], probs[:, 0], ALU.add).then_inc(S["g_dv"], 1)
                            dve.wait_ge(S["g_dv"], k + 3)
                            k = k + 3
                    if turn:
                        dve.wait_ge(S["g_pv"], CT * (i + 1))
                    dve.sem_inc(S["g_free"], 1)
                base = base + steps * NT
            dve.wait_ge(S["g_fin"], 1)

        @block.vector
        def _(dve):
            link = Chain(dve, S["dv"])
            dve.memset(acc[:], 0.0).then_inc(S["zero"], 1)
            dve.wait_ge(S["x_in"], 16)
            norm.vector(dve, link)
            dve.wait_ge(S["tokT"], 1)
            dve.tensor_copy(tok[:], sc[:, 0]).then_inc(S["tokE"], 1)
            dve.wait_ge(S["q1"], 1)
            dve.tensor_copy(tok2[:], sc[:, 1]).then_inc(S["q1E"], 1)
            for t in range(CT):
                heads = slice(HG * t, HG * (t + 1))
                dve.wait_ge(S["qr"], t + 1)
                link(dve.tensor_scalar(qst[0:STACK, heads, :], sc[0:STACK, t % 2], SCALE, None, ALU.mult))
                dve.scalar_tensor_tensor(qst[2 * HD:STACK, heads, :], sc[2 * HD:STACK, t % 2], SCALE,
                                         qst[2 * HD:STACK, heads, :].bitcast(F32), ALU.mult,
                                         ALU.subtract).then_inc(S["qs"], 1)
            dve.wait_ge(S["ones"], 1)
            for b in range(2):
                link(dve.tensor_copy(kst[STACK:KROWS, b].rearrange("p h k -> p (h k)"),
                                     ones[STACK:KROWS, 0:1].to_broadcast([1, NH * P])))
            link(dve.tensor_scalar(qst[STACK:KROWS].rearrange("p h q -> p (h q)"),
                                   ones[STACK:KROWS, 0:1].to_broadcast([1, NH * SQ]), 0.0, None, ALU.mult))
            dve.sem_inc(S["rows_set"], 1)

            def row_hi(u, b, seen):
                dve.wait_ge(row_in[u], seen)
                dve.tensor_copy(split[:, b, :, 0:3:2, :].bitcast(F32R),
                                nat[:, u, :].rearrange("p (h c) -> p h c", c=HD).unsqueeze(2)
                                .to_broadcast([P, NH, 2, HD])).then_inc(S["hi"], 1)

            def row_lo(u, b, tile):
                dve.wait_ge(S["hi"], tile + 1)
                dve.tensor_tensor(split[:, b, :, 1, :], nat[:, u, :].rearrange("p (h c) -> p h c", c=HD),
                                  split[:, b, :, 0, :], ALU.subtract).then_inc(S["split"], 1)

            def evacuate(b, g, tile):
                m = CT * tile + g
                dve.wait_ge(S["tr"], m + 1)
                wait(dve, S["score"], m - 2 * CT + 1)
                dve.tensor_copy(kst[0:STACK, b, HG * g:HG * (g + 1), :], tr[0:STACK, g % 2])\
                   .then_inc(S["ks_dve"], 1)

            def look_at_mask(u, tile, seen):
                dve.wait_ge(mask_in[u], seen)
                wait(dve, S["exp"], CT * (tile - U + 1))
                dve.tensor_reduce(mask_min[:, bass.ds(tile, 1)], msk[:, u, :], AX, ALU.min)\
                   .then_inc(S["dv"], 1)
                dve.tensor_reduce(mask_max[:, bass.ds(tile, 1)], msk[:, u, :], AX, ALU.max)\
                   .then_inc(S["mask_used"], 1)

            def set_bias(u, tile, before):
                dve.wait_ge(S["dv"], before)
                dve.tensor_scalar(bias[:, u:u + 1], mask_min[:, bass.ds(tile, 1)], 0.0, HIDE,
                                  ALU.is_le, ALU.mult).then_inc(S["bias"], 1)

            for tile in range(2):
                row_hi(tile, tile, 16)
                row_lo(tile, tile, tile)
            evacuate(0, 0, 0)
            evacuate(0, 2, 0)
            for g in range(CT):
                dve.wait_ge(S["probe_sc"], g + 1)
                dve.tensor_copy(probs[:, g], sc[:, g % 2]).then_inc(S["probe_cp"], 1)
            dve.wait_ge(S["shift"], 1)
            link(dve.tensor_scalar(qst[STACK:KROWS].rearrange("p h q -> p (h q)"),
                                   den[STACK:KROWS].rearrange("p g h q -> p (g h q)"), -1.0, None, ALU.mult))
            dve.sem_inc(S["shift_in"], 1)
            dve.memset(den[:, 0:2], 0.0).then_inc(S["den_dve"], 1)
            base = link.n
            for tile in range(2):
                look_at_mask(tile, tile, 16)
                set_bias(tile, tile, base + tile + 1)

            def add(tile, g):
                dve.wait_ge(S["exp"], CT * tile + g + 1)
                dve.wait_ge(S["den_dve"], 2 * tile + g + 1)
                dve.tensor_tensor(den[:, g], den[:, g], probs[:, g], ALU.add).then_inc(S["den_dve"], 1)

            def body(i):
                for u in range(U):
                    tile = U * i + u
                    b2, seen2 = (u + 2) % U, 16 * (i + 1 + (u + 2) // U)
                    more1 = not (last_turn(i) and u >= U - 1)
                    more2 = not (last_turn(i) and u >= U - 2)
                    if more1:
                        evacuate((u + 1) % 2, 0, tile + 1)
                    if more2:
                        dve.wait_ge(S["tr"], CT * (tile + 1))
                        row_hi(b2, u % 2, seen2)
                    add(tile, 0)
                    if more2:
                        row_lo(b2, u % 2, tile + 2)
                    if more1:
                        evacuate((u + 1) % 2, 2, tile + 1)
                    if more2:
                        look_at_mask(b2, tile + 2, seen2)
                    add(tile, 1)
                    if more2:
                        set_bias(b2, tile + 2, base + 1 + tile + 2)

            per_turn(body, dve)
            dve.wait_ge(S["den_sum"], 1)
            count = Chain(dve, S["okrow"])
            count(dve.tensor_tensor(mask_max[:], mask_max[:], mask_min[:], ALU.subtract))
            count(dve.scalar_tensor_tensor(mask_max[:], mask_min[:], 0.0, mask_max[:], ALU.is_le, ALU.mult))
            count(dve.tensor_reduce(sums[:, 0:1], mask_max[:], AX, ALU.max))
            count(dve.tensor_scalar(sums[:, 0:1], sums[:, 0:1], 0.0, None, ALU.is_gt))
            count(dve.tensor_scalar(tmp[:], sc[:, 0], DEN_MIN, None, ALU.is_ge))
            count(dve.scalar_tensor_tensor(tmp[:], sc[:, 0], DEN_MAX, tmp[:], ALU.is_le, ALU.mult))
            count(dve.tensor_reduce(sums[:, 1:2], tmp[:], AXY, ALU.min))
            count(dve.tensor_scalar(sums[:, 2:3], sums[:, 1:2], 1.0, None, ALU.is_lt))
            count(dve.tensor_tensor(sums[:, 3:4], sums[:, 0:1], sums[:, 2:3], ALU.add))
            dve.wait_ge(S["oksum"], 1)
            dve.tensor_scalar(flag[:], tr[0:1, 0, 0, 0:1], 0.5, None, ALU.is_gt).then_inc(S["flag"], 1)
            dve.wait_ge(S["flag"], 1)
            general = dve.value_load(flag[0:1, 0:1], min_val=0, max_val=1)
            with dve.If(general):
                general_vector(dve)
            with dve.Else():
                dve.nop()
            dve.wait_ge(S["den_sum"], 1)
            tail = Chain(dve, S["norm"])
            tail(dve.reciprocal(tmp[:], sc[:, 0]))
            tail(dve.tensor_tensor(tok[:], acc[:], tmp[:], ALU.mult))
            dve.wait_ge(S["vp"], 1)
            dve.tensor_copy(tok2[:], sc[:, 1]).then_inc(S["vpE"], 1)
            dve.wait_ge(S["wo_in"], 48)
            dve.wait_ge(S["proj"], 1)
            for m in range(QT):
                tail(dve.tensor_tensor(xres[:, m, :], xres[:, m, :], bo[:], ALU.add))
                tail(dve.tensor_tensor(xres[:, m, :], xres[:, m, :],
                                       sc[:, 0].rearrange("p h q -> p (h q)")[:, m * D:(m + 1) * D], ALU.add))

        @block.tensor
        def _(pe):
            scf = sc[:].rearrange("p s h q -> p s (h q)")
            pe.wait_ge(S["id"], 1)
            pe.wait_ge(norm.ready, QT)
            transpose_tokens(pe, sc[:, 0], xn, ident).then_inc(S["tokT"], 1)
            pe.wait_ge(S["small"], 32)
            pe.wait_ge(S["tokE"], 1)
            for t in range(CT):
                last = pe.matmul(sc[:, 1, t], bd_q[:], tok[:, t], start=True, stop=True)
            last.then_inc(S["q1"], 1)
            pe.wait_ge(S["q1E"], 1)
            for t in range(CT):
                wait(pe, S["qs"], t - 1)
                for j in range(HG):
                    last = pe.matmul(sc[0:STACK, t % 2, j], bd_k[:, j], tok2[:, t], start=True, stop=True)
                last.then_inc(S["qr"], 1)

            def transposes(b, g, tile):
                pe.wait_ge(S["split"], tile + 1)
                wait(pe, S["ks_act"] if g % 2 else S["ks_dve"], 2 * tile + g // 2)
                for j in range(HG):
                    last = pe.transpose(tr[0:STACK, g % 2, j],
                                        split[:, b, HG * g + j].rearrange("p s c -> p (s c)"), ident[:])
                last.then_inc(S["tr"], 1)

            def scores(b, g, tile, signal):
                pe.wait_ge(S["ks_act"] if g % 2 else S["ks_dve"], 2 * tile + g // 2 + 1)
                for j in range(HG):
                    h = HG * g + j
                    last = pe.matmul(sc[:, g % 2, j], kst[:, b, h], qst[:, h], start=True, stop=True)
                last.then_inc(signal, 1)

            def weighted(u, g, signal, src):
                for j in range(HG):
                    last = pe.matmul(acc[HD * j:HD * (j + 1), g], nat[:, u, (HG * g + j) * HD:(HG * g + j + 1) * HD],
                                     src[:, j], start=False, stop=True, skip_group_check=True,
                                     tile_position=(0, HD * j))
                last.then_inc(signal, 1)

            for g in range(CT):
                transposes(0, g, 0)
            pe.wait_ge(S["qs"], CT)
            pe.wait_ge(S["rows_set"], 1)
            for g in range(CT):
                wait(pe, S["probe_cp"], g - 1)
                scores(0, g, 0, S["probe_sc"])
            pe.wait_ge(S["probe_cp"], CT)
            pe.wait_ge(S["shift_in"], 1)
            pe.wait_ge(S["zero"], 1)

            def body(i):
                for u in range(U):
                    tile = U * i + u
                    for g in range(CT):
                        n = CT * tile + g
                        if not (last_turn(i) and u == U - 1):
                            transposes((u + 1) % 2, g, tile + 1)
                        wait(pe, S["exp"], n - 1)
                        scores(u % 2, g, tile, S["score"])
                        if not (isinstance(i, int) and n < 2):
                            weighted((u if g >= 2 else u - 1) % U, (g - 2) % CT, S["pv"], probs[:, (g - 2) % CT])

            per_turn(body, pe)
            for g in (2, 3):
                pe.wait_ge(S["exp"], NT * CT - 3 + g)
                weighted(U - 1, g, S["pv"], probs[:, g])
            pe.wait_ge(S["den_dve"], 2 * NT + 1)
            pe.wait_ge(S["den_pool"], 2 * NT + 1)
            pe.wait_ge(S["exp"], NT * CT)

            def total(signal):
                for g in range(CT):
                    for j in range(HG):
                        last = pe.matmul(sc[HD * j:HD * (j + 1), 0, g], ones[:, 0:HD], den[:, g, j],
                                         start=True, stop=True, tile_position=(0, HD * j))
                last.then_inc(signal, 1)

            total(S["den_sum"])
            pe.wait_ge(S["okrow"], 9)
            pe.matmul(tr[0:1, 0, 0, 0:1], sums[:, 3:4], ones[:, 0:1], start=True, stop=True).then_inc(S["oksum"], 1)
            pe.wait_ge(S["flag"], 1)
            general = pe.value_load(flag[0:1, 0:1], min_val=0, max_val=1)
            with pe.If(general):
                for turn in range(2):
                    if turn:
                        pe.wait_ge(S["g_zero"], 3)
                    with pe.Fori(0, NT) as i:
                        seen = NT * turn + i
                        pe.wait_ge(S["g_split"], seen + 1)
                        for g in range(CT):
                            for j in range(HG):
                                last = pe.transpose(tr[0:STACK, 0, j],
                                                    split[:, 0, HG * g + j].rearrange("p s c -> p (s c)"), ident[:])
                            last.then_inc(S["g_tr"], 1)
                            pe.wait_ge(S["g_ks"], CT * seen + g + 1)
                            for j in range(HG):
                                h = HG * g + j
                                last = pe.matmul(sc[:, 0, j], kst[:, 0, h], qst[:, h], start=True, stop=True)
                            last.then_inc(S["g_sc"], 1)
                            if turn:
                                pe.wait_ge(S["g_exp"], CT * i + g + 1)
                                weighted(0, g, S["g_pv"], probs[:, 0])
                            else:
                                pe.wait_ge(S["g_dv"], 2 + (3 + 2 * CT) * i + 3 + 2 * (g + 1))
                pe.wait_ge(S["g_dv"], 2 + (6 + 5 * CT) * NT)
                total(S["g_den"])
                pe.wait_ge(S["g_den"], 1)
                pe.sem_inc(S["g_fin"], 1)
            with pe.Else():
                pe.nop()
            pe.wait_ge(S["norm"], 2)
            pe.wait_ge(S["wo_in"], 48)
            for t in range(CT):
                last = pe.matmul(sc[:, 1, t], bd_v[:], tok[:, t], start=True, stop=True)
            last.then_inc(S["vp"], 1)
            pe.wait_ge(S["vpE"], 1)
            for m in range(QT):
                for t in range(CT):
                    last = pe.matmul(scf[:, 0, m * D:(m + 1) * D], tok2[:, t, m * P:(m + 1) * P], wo[:, t],
                                     start=t == 0, stop=t == CT - 1)
            last.then_inc(S["proj"], 1)


def self_attention(nc, mem, sem, a, ident, ones, xres, weights, w_ready):
    NU_SELF, NU_PAST = CT * QT, NH * QT * NP
    KT = NP * SP_ // P
    past = mem.sb("past", [P, CT, SP_])
    wrk = mem.sb("wrk", [P, CT, D])
    wrv = mem.sb("wrv", [P, CT, D])
    wrq = mem.sb("wrq", [P, CT, D])
    brk_c, brq_c, bq_c, bk_c, bo_c = (mem.sb(n, [P, CT]) for n in ("brk_c", "brq_c", "bq_c", "bk_c", "bo_c"))
    rk = mem.sb("rk", [P, CT, NP * SP_])
    rv = mem.sb("rv", [P, KT, D])
    row_bias = mem.sb("row_bias", [P, 4, D])
    h = mem.sb("b_h", [P, QT, D])
    ht = mem.sb("b_ht", [P, CT, SQ])
    qpad = mem.sb("qpad", [P, CT, HG, SQ])
    kt = mem.sb("b_kt", [P, CT, SQ])
    v = mem.sb("b_v", [P, QT, D])
    pr = mem.sb("pr", [P, 2, 1024])
    pt = mem.sb("pt", [P, 2, 8, P])
    ct = mem.sb("b_ct", [P, CT, SQ])
    nmax = mem.sb("nmax", [P, NU_SELF + NU_PAST, HG])
    tot = mem.sb("tot", [P, NU_SELF + NU_PAST, HG])
    inv = mem.sb("b_inv", [P, NU_SELF + NU_PAST, HG])
    sc = mem.ps("b_sc", [P, 2, 1024])
    tr = mem.ps("b_tr", [P, 8, P])
    acc = mem.ps("b_acc", [P, CT, SQ])
    wg = past
    o_t, o_nat = kt, v
    r_t, r_nat, gate = ct, h, pr

    norm = Norm("bnorm", mem, sem, xres, h)
    S = {n: sem("b_" + n) for n in (
        "past_in", "wr_in", "bias_in", "wg_in", "pmm", "pev_act", "pev_dve", "dv", "hT", "hE", "q", "qE", "k", "kE", "v", "vE",
        "sc", "max", "exp", "norm", "tr", "ev_dve", "ev_act", "pv", "accE", "o", "oT", "oE", "oTE", "rq", "rqE",
        "rT", "rE", "gmm", "z", "ez", "done")}
    with nc.Block() as block:
        @block.sync
        def _(sp):
            pastv = [a["past_t"][p].rearrange("(t p) k -> p t k", p=P) for p in range(NP)]
            sp.dma_start(wrk[:], a["wrk"].rearrange("(t p) o -> p t o", p=P)).then_inc(S["wr_in"], 16)
            sp.dma_start(past[:], pastv[0]).then_inc(S["past_in"], 16)
            sp.dma_start(wrv[:], a["wrv"].rearrange("(t p) o -> p t o", p=P)).then_inc(S["wr_in"], 16)
            for dst, name in ((brk_c, "brk"), (brq_c, "brq"), (bq_c, "bq"), (bk_c, "bk"), (bo_c, "bo")):
                sp.dma_start(dst[:], a[name + "_c"]).then_inc(S["bias_in"], 16)
            for n, name in enumerate(("brv", "bv", "bo", "bg")):
                sp.dma_start(row_bias[:, n], a[name].partition_broadcast(P)).then_inc(S["bias_in"], 16)
            sp.dma_start(wrq[:], a["wrq"].rearrange("(t p) o -> p t o", p=P)).then_inc(S["wr_in"], 16)
            sp.wait_ge(S["pmm"], 16)
            sp.dma_start(past[:], pastv[1]).then_inc(S["past_in"], 16)
            sp.wait_ge(S["pmm"], 32)
            for n in range(2):
                sp.dma_start(wg[:, :, n * D:(n + 1) * D],
                             a["wg"][n * D:(n + 1) * D].rearrange("(t p) o -> p t o", p=P)).then_inc(S["wg_in"], 16)

        slots = [sc[:, n // 2, (n % 2) * D:(n % 2 + 1) * D] for n in range(4)]

        @block.scalar
        def _(act):
            act.wait_ge(S["bias_in"], 9 * 16)
            for n in range(16):
                mt, c = (n % 8) % CT, 2 * (n // 8) + (n % 8) // CT
                act.wait_ge(S["pmm"], 2 * n + 1)
                act.activation(rk[:, mt, c * D:(c + 1) * D], slots[(2 * n) % 4], ACT.Identity,
                               bias=brk_c[:, mt:mt + 1]).then_inc(S["pev_act"], 1)
            norm.scalar(act)
            act.wait_ge(S["k"], 1)
            for t in range(CT):
                last = act.activation(kt[:, t], sc[:, 1, t * SQ:(t + 1) * SQ], ACT.Identity, bias=bk_c[:, t:t + 1])
            last.then_inc(S["kE"], 1)

            def evacuate(u):
                act.wait_ge(S["tr"], u + 1)
                wait(act, S["pv"], u - 1)
                act.activation(pt[:, u % 2, 4:8], tr[:, 4:8], ACT.Copy).then_inc(S["ev_act"], 1)

            def units(first, n, groups):
                for u in range(first, first + n + 2):
                    if u < first + n:
                        act.wait_ge(S["max"], u + 1)
                        wait(act, S["tr"], u - 1)
                        w = 1024 // groups
                        for g in range(groups):
                            last = act.activation(pr[:, u % 2, g * w:(g + 1) * w], sc[:, u % 2, g * w:(g + 1) * w],
                                                  ACT.Exp, bias=nmax[:, u, g:g + 1], accum_out=tot[:, u, g:g + 1])
                        last.then_inc(S["exp"], 1)
                    if u >= first + 2:
                        evacuate(u - 2)

            units(0, NU_SELF, HG)
            act.wait_ge(S["oT"], 1)
            for t in range(CT):
                last = act.activation(o_t[:, t], sc[:, 1, t * SQ:(t + 1) * SQ], ACT.Identity, bias=bo_c[:, t:t + 1])
            last.then_inc(S["oTE"], 1)
            units(NU_SELF, NU_PAST, 1)
            act.wait_ge(S["z"], 1)
            act.activation(gate[:, 1], gate[:, 0], ACT.Exp, scale=-1.0).then_inc(S["ez"], 1)

        @block.vector
        def _(dve):
            link = Chain(dve, S["dv"])
            dve.wait_ge(S["bias_in"], 9 * 16)
            for n in range(16):
                dve.wait_ge(S["pmm"], 2 * n + 2)
                dve.tensor_tensor(rv[:, n], slots[(2 * n + 1) % 4], row_bias[:, 0], ALU.add).then_inc(S["pev_dve"], 1)
            norm.vector(dve, link)
            link(dve.memset(qpad[:], 0.0))
            dve.wait_ge(S["hT"], 1)
            dve.tensor_copy(ht[:].rearrange("p t q -> p (t q)"), tr[:].rearrange("p a b -> p (a b)"))\
               .then_inc(S["hE"], 1)

            def pad(bias, src):
                for t in range(CT):
                    for j in range(HG):
                        part = slice(HD * j, HD * (j + 1))
                        last = dve.tensor_scalar(qpad[part, t, j], src[part, t * SQ:(t + 1) * SQ],
                                                 bias[part, t:t + 1], SCALE, ALU.add, ALU.mult)
                return last

            dve.wait_ge(S["q"], 1)
            pad(bq_c, sc[:, 0]).then_inc(S["qE"], 1)
            dve.wait_ge(S["v"], 1)
            for m in range(QT):
                last = dve.tensor_tensor(v[:, m], tr[:, 4 * m:4 * m + 4].rearrange("p a b -> p (a b)"),
                                         row_bias[:, 1], ALU.add)
            last.then_inc(S["vE"], 1)

            def units(first, n, groups, factor):
                w = 1024 // groups
                for u in range(first, first + n + 2):
                    if u < first + n:
                        dve.wait_ge(S["sc"], u + 1)
                        dve.tensor_reduce(nmax[:, u, 0:groups], sc[:, u % 2].rearrange("p (g k) -> p g k", g=groups),
                                          AX, ALU.max, negate=True).then_inc(S["max"], 1)
                    if first < u <= first + n:
                        x = u - 1
                        dve.wait_ge(S["exp"], x + 1)
                        link(dve.reciprocal(inv[:, x, 0:groups], tot[:, x, 0:groups]))
                        if groups == 1:
                            last = dve.tensor_scalar(pr[:, x % 2], pr[:, x % 2], inv[:, x, 0:1], factor,
                                                     ALU.mult, ALU.mult)
                        else:
                            for g in range(groups):
                                last = dve.tensor_scalar(pr[:, x % 2, g * w:(g + 1) * w],
                                                         pr[:, x % 2, g * w:(g + 1) * w],
                                                         inv[:, x, g:g + 1], factor, ALU.mult, ALU.mult)
                        last.then_inc(S["norm"], 1)
                    if u >= first + 2:
                        x = u - 2
                        dve.wait_ge(S["tr"], x + 1)
                        wait(dve, S["pv"], x - 1)
                        dve.tensor_copy(pt[:, x % 2, 0:4], tr[:, 0:4]).then_inc(S["ev_dve"], 1)

            units(0, NU_SELF, HG, 1.0)
            dve.wait_ge(S["pv"], NU_SELF)
            dve.tensor_copy(ct[:], acc[:]).then_inc(S["accE"], 1)
            dve.wait_ge(S["o"], 1)
            for m in range(QT):
                last = dve.tensor_tensor(o_nat[:, m], sc[:, 0, m * D:(m + 1) * D], row_bias[:, 2], ALU.add)
            last.then_inc(S["oE"], 1)
            dve.wait_ge(S["rq"], 1)
            pad(brq_c, tr[:].rearrange("p a b -> p (a b)")).then_inc(S["rqE"], 1)
            units(NU_SELF, NU_PAST, 1, 1.0 / NP)
            dve.wait_ge(S["pv"], NU_SELF + NU_PAST)
            dve.tensor_copy(r_t[:], acc[:]).then_inc(S["accE"], 1)
            dve.wait_ge(S["rT"], 1)
            for m in range(QT):
                last = dve.tensor_copy(r_nat[:, m], tr[:, 4 * m:4 * m + 4].rearrange("p a b -> p (a b)"))
            last.then_inc(S["rE"], 1)
            dve.wait_ge(S["gmm"], 1)
            for m in range(QT):
                link(dve.tensor_tensor(gate[:, 0, m * D:(m + 1) * D], sc[:, 0, m * D:(m + 1) * D], row_bias[:, 3],
                                       ALU.add))
            dve.sem_inc(S["z"], 1)
            g = gate[:, 1].rearrange("p (m c) -> p m c", m=QT)
            dve.wait_ge(S["ez"], 1)
            link(dve.tensor_scalar(g, g, 1.0, None, ALU.add))
            link(dve.reciprocal(g, g))
            link(dve.tensor_tensor(r_nat[:], r_nat[:], o_nat[:], ALU.subtract))
            link(dve.tensor_tensor(r_nat[:], r_nat[:], g, ALU.mult))
            link(dve.tensor_tensor(r_nat[:], r_nat[:], o_nat[:], ALU.add))
            link(dve.tensor_tensor(xres[:], xres[:], r_nat[:], ALU.add))

        @block.tensor
        def _(pe):
            pe.wait_ge(S["wr_in"], 48)
            for n in range(32):
                state, k = n // 16, (n % 16) // 2
                if n % 16 == 0:
                    pe.wait_ge(S["past_in"], 16 * (state + 1))
                wait(pe, S["pev_dve"] if n % 2 else S["pev_act"], n // 2 - 1)
                for c in range(CT):
                    if n % 2:
                        lhs, rhs = past[:, c, k * P:(k + 1) * P], wrv[:, c]
                    else:
                        lhs, rhs = wrk[:, c, (k % CT) * P:(k % CT + 1) * P], past[:, c, (k // CT) * D:(k // CT + 1) * D]
                    last = pe.matmul(slots[n % 4], lhs, rhs, start=c == 0, stop=c == CT - 1)
                last.then_inc(S["pmm"], 1)
            pe.wait_ge(norm.ready, QT)
            transpose_tokens(pe, tr[:].rearrange("p a b -> p (a b)").rearrange("p (t q) -> p t q", q=SQ), h, ident)\
                .then_inc(S["hT"], 1)
            pe.wait_ge(w_ready, 64)
            pe.wait_ge(S["hE"], 1)
            pe.wait_ge(S["pev_dve"], 16)
            pe.wait_ge(S["pev_act"], 16)

            def project_t(dst, w, src):
                for mt in range(CT):
                    for c in range(CT):
                        last = pe.matmul(dst[:, mt * SQ:(mt + 1) * SQ], w[:, c, mt * P:(mt + 1) * P], src[:, c],
                                         start=c == 0, stop=c == CT - 1)
                return last

            def project(dst, w, src):
                for m in range(QT):
                    for c in range(CT):
                        last = pe.matmul(dst[:, m * D:(m + 1) * D], src[:, c, m * P:(m + 1) * P], w[:, c],
                                         start=c == 0, stop=c == CT - 1)
                return last

            trf = tr[:].rearrange("p a b -> p (a b)")
            project_t(sc[:, 0], weights["q"], ht).then_inc(S["q"], 1)
            project_t(sc[:, 1], weights["k"], ht).then_inc(S["k"], 1)
            project(trf, weights["v"], ht).then_inc(S["v"], 1)
            pe.wait_ge(S["qE"], 1)
            pe.wait_ge(S["kE"], 1)
            pe.wait_ge(S["vE"], 1)

            def units(first, n, scores, weighted):
                for u in range(first, first + n + 2):
                    if u < first + n:
                        wait(pe, S["exp"], u - 1)
                        scores(u - first, sc[:, u % 2]).then_inc(S["sc"], 1)
                    if first < u <= first + n:
                        x = u - 1
                        pe.wait_ge(S["norm"], x + 1)
                        wait(pe, S["ev_dve"], x)
                        wait(pe, S["ev_act"], x)
                        for b in range(8):
                            last = pe.transpose(tr[:, b], pr[:, x % 2, b * P:(b + 1) * P], ident[:])
                        last.then_inc(S["tr"], 1)
                    if u >= first + 2:
                        x = u - 2
                        pe.wait_ge(S["ev_dve"], x + 1)
                        pe.wait_ge(S["ev_act"], x + 1)
                        weighted(x - first, pt[:, x % 2]).then_inc(S["pv"], 1)

            def self_scores(u, dst):
                t, m = u // QT, u % QT
                for j in range(HG):
                    last = pe.matmul(dst[:, j * SQ:(j + 1) * SQ], qpad[:, t, j, m * P:(m + 1) * P], kt[:, t],
                                     start=True, stop=True)
                return last

            def self_weighted(u, src):
                t, m = u // QT, u % QT
                for k in range(QT):
                    for j in range(HG):
                        last = pe.matmul(acc[HD * j:HD * (j + 1), t, m * P:(m + 1) * P],
                                         v[:, k, (HG * t + j) * HD:(HG * t + j + 1) * HD], src[:, QT * j + k],
                                         start=k == 0, stop=k == QT - 1, skip_group_check=True,
                                         tile_position=(0, HD * j))
                return last

            units(0, NU_SELF, self_scores, self_weighted)
            pe.wait_ge(S["accE"], 1)
            project(sc[:, 0], weights["o"], ct).then_inc(S["o"], 1)
            project_t(sc[:, 1], weights["o"], ct).then_inc(S["oT"], 1)
            pe.wait_ge(S["oTE"], 1)
            project_t(trf, wrq, o_t).then_inc(S["rq"], 1)
            pe.wait_ge(S["rqE"], 1)
            pe.wait_ge(S["oE"], 1)

            def past_scores(u, dst):
                head, m, state = u // (QT * NP), u // NP % QT, u % NP
                for n in range(SP_ // D):
                    at = state * SP_ + n * D
                    last = pe.matmul(dst[:, n * D:(n + 1) * D], qpad[:, head // HG, head % HG, m * P:(m + 1) * P],
                                     rk[:, head // HG, at:at + D], start=True, stop=True)
                return last

            def past_weighted(u, src):
                head, m, state = u // (QT * NP), u // NP % QT, u % NP
                t, j = head // HG, head % HG
                for k in range(8):
                    last = pe.matmul(acc[HD * j:HD * (j + 1), t, m * P:(m + 1) * P],
                                     rv[:, 8 * state + k, head * HD:(head + 1) * HD], src[:, k],
                                     start=state == 0 and k == 0, stop=state == NP - 1 and k == 7,
                                     tile_position=(0, HD * j))
                return last

            units(NU_SELF, NU_PAST, past_scores, past_weighted)
            pe.wait_ge(S["accE"], 2)
            for m in range(QT):
                for t in range(CT):
                    last = pe.transpose(tr[:, 4 * m + t], r_t[:, t, m * P:(m + 1) * P], ident[:])
            last.then_inc(S["rT"], 1)
            pe.wait_ge(S["wg_in"], 32)
            for m in range(QT):
                for c in range(2 * CT):
                    src = (o_t if c < CT else r_t)[:, c % CT, m * P:(m + 1) * P]
                    last = pe.matmul(sc[:, 0, m * D:(m + 1) * D], src, wg[:, c % CT, (c // CT) * D:(c // CT + 1) * D],
                                     start=c == 0, stop=c == 2 * CT - 1)
            last.then_inc(S["gmm"], 1)


def experts(nc, mem, sem, a, ident, ones, xres, out):
    w1 = mem.sb("w1", [P, 2, CT, FF])
    w2 = mem.sb("w2", [P, 2, FT, D])
    h = mem.sb("c_h", [P, QT, D])
    ht = mem.sb("c_ht", [P, CT, SQ])
    gw = mem.sb("gw", [P, CT, NE])
    b1 = mem.sb("b1", [P, NE, FT])
    b2 = mem.sb("b2", [NE, D])
    iota = mem.sb("iota", [P, NE])
    prob = mem.sb("prob", [P, QT, NE])
    share = mem.sb("share", [P, QT, NE])
    share_t = mem.sb("share_t", [NE, SQ])
    best = mem.sb("best", [P, QT, 8])
    which = mem.sb("which", [P, QT, 8], U32)
    whichf = mem.sb("whichf", [P, QT, 8])
    pick = mem.sb("pick", [P, NE])
    one = mem.sb("one", [P, QT, 4])
    hid = mem.sb("hid", [P, 2, FT, SQ])
    total = mem.sb("total", [P, QT, D])
    up = mem.ps("up", [P, 2, 4, SQ])
    down = mem.ps("down", [P, 2, D])
    small = mem.ps("c_small", [P, 2, D])

    norm = Norm("cnorm", mem, sem, xres, h)
    S = {n: sem("c_" + n) for n in (
        "gate_in", "b_in", "iota", "iotaf", "dv", "hT", "hE", "logit", "nmax", "p", "share", "shT", "shE", "b2",
        "up", "gelu", "down", "added", "out", "done")}
    w1_in = [sem(f"w1_in{b}") for b in range(2)]
    w2_in = [sem(f"w2_in{b}") for b in range(2)]
    w1v = a["w1"].rearrange("e (t p) f -> e p t f", p=P)
    w2v = a["w2"].rearrange("e (t p) f -> e p t f", p=P)
    PAIRS = NE // 2
    with nc.Block() as block:
        @block.sync
        def _(sp):
            sp.dma_start(gw[:], a["gate_t"].rearrange("(t p) e -> p t e", p=P)).then_inc(S["gate_in"], 16)
            for b in range(2):
                sp.dma_start(w1[:, b], w1v[b]).then_inc(w1_in[b], 16)
                sp.dma_start(w2[:, b], w2v[b]).then_inc(w2_in[b], 16)
            sp.dma_start(b1[:], a["b1_c"]).then_inc(S["b_in"], 16)
            sp.dma_start(b2[:], a["b2"]).then_inc(S["b_in"], 16)
            with sp.Fori(1, PAIRS) as i:
                for b in range(2):
                    e = 2 * i + b
                    sp.wait_ge(S["up"], 2 * (e - 1))
                    sp.dma_start(w1[:, b], w1v[e]).then_inc(w1_in[b], 16)
                    sp.wait_ge(S["down"], e - 1)
                    sp.dma_start(w2[:, b], w2v[e]).then_inc(w2_in[b], 16)
            sp.wait_ge(S["out"], 1)
            sp.dma_start(out.rearrange("(t p) c -> p t c", p=P), total[:]).then_inc(S["done"], 16)
            sp.wait_ge(S["done"], 16)

        @block.gpsimd
        def _(pool):
            pool.iota(iota[:], [[1, NE]], base=0, channel_multiplier=0,
                      allow_small_or_imprecise_dtypes=True).then_inc(S["iota"], 1)

        @block.scalar
        def _(act):
            norm.scalar(act)
            for m in range(QT):
                act.wait_ge(S["nmax"], QT)
                act.activation(prob[:, m], small[:, 0, m * NE:(m + 1) * NE], ACT.Exp, bias=one[:, m, 0:1],
                               accum_out=one[:, m, 1:2]).then_inc(S["p"], 1)
            act.wait_ge(S["b_in"], 32)

            def body(i):
                for b in range(2):
                    e = 2 * i + b
                    for s in range(2):
                        act.wait_ge(S["up"], 2 * e + s + 1)
                        wait(act, S["down"], e - 1)
                        for f in range(4):
                            last = act.activation(hid[:, b, 4 * s + f], up[:, s, f], ACT.Gelu,
                                                  bias=b1[:, bass.ds(e, 1), 4 * s + f])
                        last.then_inc(S["gelu"], 1)

            body(0)
            with act.Fori(1, PAIRS) as i:
                body(i)

        @block.vector
        def _(dve):
            link = Chain(dve, S["dv"])
            norm.vector(dve, link)
            dve.wait_ge(S["hT"], 1)
            dve.tensor_copy(ht[:], up[:, 0]).then_inc(S["hE"], 1)
            dve.wait_ge(S["logit"], 1)
            for m in range(QT):
                dve.tensor_reduce(one[:, m, 0:1], small[:, 0, m * NE:(m + 1) * NE], AX, ALU.max,
                                  negate=True).then_inc(S["nmax"], 1)
            dve.wait_ge(S["iota"], 1)
            for m in range(QT):
                dve.wait_ge(S["p"], m + 1)
                link(dve.reciprocal(one[:, m, 2:3], one[:, m, 1:2]))
                link(dve.tensor_scalar(prob[:, m], prob[:, m], one[:, m, 2:3], None, ALU.mult))
                link(dve.max(best[:, m], prob[:, m]))
                link(dve.max_index(which[:, m], best[:, m], prob[:, m]))
                link(dve.tensor_copy(whichf[:, m], which[:, m]))
                link(dve.tensor_tensor(one[:, m, 3:4], best[:, m, 0:1], best[:, m, 1:2], ALU.add))
                link(dve.tensor_scalar(one[:, m, 3:4], one[:, m, 3:4], 1e-10, None, ALU.max))
                link(dve.reciprocal(one[:, m, 3:4], one[:, m, 3:4]))
                link(dve.tensor_scalar(best[:, m], best[:, m], one[:, m, 3:4], None, ALU.mult))
                link(dve.tensor_scalar(share[:, m], iota[:], whichf[:, m, 0:1], best[:, m, 0:1],
                                       ALU.is_equal, ALU.mult))
                link(dve.tensor_scalar(pick[:], iota[:], whichf[:, m, 1:2], best[:, m, 1:2],
                                       ALU.is_equal, ALU.mult))
                link(dve.tensor_tensor(share[:, m], share[:, m], pick[:], ALU.add))
            dve.sem_inc(S["share"], 1)
            dve.wait_ge(S["shT"], 1)
            dve.tensor_copy(share_t[:], small[0:NE, 0, 64:64 + SQ]).then_inc(S["shE"], 1)
            dve.wait_ge(S["b2"], 1)
            for m in range(QT):
                dve.tensor_tensor(total[:, m], h[:, m], down[:, m], ALU.add).then_inc(S["added"], 1)

            def body(i):
                for b in range(2):
                    e = 2 * i + b
                    dve.wait_ge(S["down"], e + 1)
                    dve.wait_ge(S["added"], QT * (e + 1))
                    for m in range(QT):
                        dve.scalar_tensor_tensor(total[:, m], down[:, m], share[:, m, bass.ds(e, 1)], total[:, m],
                                                 ALU.mult, ALU.add).then_inc(S["added"], 1)

            body(0)
            with dve.Fori(1, PAIRS) as i:
                body(i)
            dve.wait_ge(S["added"], QT * (NE + 1))
            link(dve.tensor_scalar(total[:], total[:], -100.0, 100.0, ALU.max, ALU.min))
            dve.tensor_tensor(total[:], total[:], xres[:], ALU.add).then_inc(S["out"], 1)

        @block.tensor
        def _(pe):
            pe.wait_ge(norm.ready, QT)
            transpose_tokens(pe, up[:, 0], h, ident).then_inc(S["hT"], 1)
            pe.wait_ge(S["gate_in"], 16)
            pe.wait_ge(S["hE"], 1)
            for m in range(QT):
                for c in range(CT):
                    last = pe.matmul(small[:, 0, m * NE:(m + 1) * NE], ht[:, c, m * P:(m + 1) * P], gw[:, c],
                                     start=c == 0, stop=c == CT - 1)
            last.then_inc(S["logit"], 1)
            pe.wait_ge(S["share"], 1)
            for m in range(QT):
                last = pe.transpose(small[0:NE, 0, 64 + m * P:64 + (m + 1) * P], share[:, m], ident[:])
            last.then_inc(S["shT"], 1)
            pe.wait_ge(S["b_in"], 32)
            pe.wait_ge(S["shE"], 1)
            for m in range(QT):
                last = pe.matmul(down[:, m], share_t[:, m * P:(m + 1) * P], b2[:], start=True, stop=True)
            last.then_inc(S["b2"], 1)

            def body(i):
                for b in range(2):
                    e = 2 * i + b
                    pe.wait_ge(w1_in[b], 16 * (i + 1))
                    for s in range(2):
                        wait(pe, S["gelu"], 2 * e + s - 1)
                        for f in range(4):
                            for c in range(CT):
                                last = pe.matmul(up[:, s, f], w1[:, b, c, (4 * s + f) * P:(4 * s + f + 1) * P],
                                                 ht[:, c], start=c == 0, stop=c == CT - 1)
                        last.then_inc(S["up"], 1)
                    pe.wait_ge(w2_in[b], 16 * (i + 1))
                    pe.wait_ge(S["gelu"], 2 * e + 2)
                    pe.wait_ge(S["added"], QT * (e + 1))
                    for m in range(QT):
                        for f in range(FT):
                            last = pe.matmul(down[:, m], hid[:, b, f, m * P:(m + 1) * P], w2[:, b, f],
                                             start=f == 0, stop=f == FT - 1)
                    last.then_inc(S["down"], 1)

            body(0)
            with pe.Fori(1, PAIRS) as i:
                body(i)


INPUTS = {"x": [SQ, D], "ctx": [SK, D], "mask_t": [SK, SQ], "bd_wq_t": [P, P], "bd_wk": [P, HG, STACK],
          "bd_wv_t": [P, P], "x_wo_t": [D, D], "x_bo": [D], "wq": [D, D], "wk": [D, D], "wv": [D, D], "wo": [D, D],
          "past_t": [NP, D, SP_], "wrk": [D, D], "wrv": [D, D], "wrq": [D, D], "wg": [2 * D, D],
          "brk_c": [P, CT], "brq_c": [P, CT], "bq_c": [P, CT], "bk_c": [P, CT], "bo_c": [P, CT],
          "brv": [D], "bv": [D], "bo": [D], "bg": [D],
          "gate_t": [D, NE], "w1": [NE, D, FF], "w2": [NE, FF, D], "b1_c": [P, NE, FT], "b2": [NE, D]}


def kernel(**inputs):
    import concourse.bacc as bacc
    from concourse.bass_utils import run_bass_kernel_spmd

    given = {k: np.asarray(v) for k, v in inputs.items()}

    def blocks(w):
        m = np.zeros((P, P), w.dtype)
        for j in range(HG):
            m[HD * j:HD * (j + 1), HD * j:HD * (j + 1)] = w
        return m

    arrays = {
        "x": given["x"][0], "ctx": given["ctx_1024"][0], "mask_t": given["mask_Bx1xSxS2_ik1"][0, 0].T,
        "bd_wq_t": blocks(given["L0_xattn_Wq"].T), "bd_wv_t": blocks(given["L0_xattn_Wv"].T),
        "bd_wk": np.concatenate([blocks(given["L0_xattn_Wk"]).reshape(P, HG, HD)] * 3, axis=2),
        "x_wo_t": given["L0_xattn_Wo"].T, "x_bo": given["L0_xattn_bo"],
        "past_t": given["L0_attn_past_states"][:, 0, :SP_].transpose(0, 2, 1),
        "gate_t": given["L0_ffn_gate_w"].T, "w1": given["L0_ffn_w1"], "w2": given["L0_ffn_w2"],
        "b1_c": given["L0_ffn_b1"].reshape(NE, FT, P).transpose(2, 0, 1), "b2": given["L0_ffn_b2"],
        "wq": given["L0_attn_Wq"], "wk": given["L0_attn_Wk"], "wv": given["L0_attn_Wv"], "wo": given["L0_attn_Wo"],
    }
    arrays |= {n.lower(): given["L0_attn_" + n] for n in ("Wrk", "Wrv", "Wrq", "Wg", "brv", "bv", "bo", "bg")}
    arrays |= {n + "_c": given["L0_attn_" + n].reshape(CT, P).T for n in ("brk", "brq", "bq", "bk", "bo")}
    arrays = {"in_" + k: np.ascontiguousarray(v) for k, v in arrays.items()}
    nc = bacc.Bacc("TRN2", target_bir_lowering=False, num_devices=1)
    aps = {}
    for name, shape in INPUTS.items():
        assert list(arrays["in_" + name].shape) == shape, name
        aps[name] = nc.dram_tensor("in_" + name, shape, mybir.dt.from_np(arrays["in_" + name].dtype), kind="ExternalInput").ap()
    out = nc.dram_tensor("out", [SQ, D], F32, kind="ExternalOutput").ap()
    build(nc, aps, out)
    result = run_bass_kernel_spmd(nc, [arrays], core_ids=[0])
    return result.results[0]["out"][None]
```

```python
from contextlib import ExitStack

import numpy as np

import concourse.bass as bass
from concourse import mybir

F32 = mybir.dt.float32
F32R = mybir.dt.float32r
I32 = mybir.dt.int32
U32 = mybir.dt.uint32
ALU = mybir.AluOpType
ACT = mybir.ActivationFunctionType
AX = mybir.AxisListType.X
AXY = mybir.AxisListType.XY
RMAX = bass.bass_isa.ReduceOp.max

P = 128
SQ = 256
D = 512
NH = 16
HD = D // NH
SK = 25088
NT = SK // P
U = 4
TURNS = NT // U
CT = D // P
HG = NH // CT
QT = SQ // P
STACK = 3 * HD
KROWS = STACK + 1
NP = 2
SP_ = 1024
NE = 14
FF = 1024
FT = FF // P
SCALE = 1.0 / float(np.sqrt(np.float32(HD)))
EPS = 1e-5
MASKED = -1e20
HIDE = -1e30
DEN_MIN, DEN_MAX = 1e-25, 1e30


def wait(eng, sem, value):
    if not isinstance(value, int) or value > 0:
        eng.wait_ge(sem, value)


class Chain:

    def __init__(self, eng, sem):
        self.eng, self.sem, self.n = eng, sem, 0

    def __call__(self, ins):
        self.n += 1
        ins.then_inc(self.sem, 1)
        self.eng.wait_ge(self.sem, self.n)


def build(nc, a, out):
    with ExitStack() as ctx:
        def sem(name):
            return ctx.enter_context(nc.semaphore(name))

        keep = Buffers(nc, ctx)
        ident = keep.sb("ident", [P, P])
        ones = keep.sb("ones", [P, P])
        xres = keep.sb("xres", [P, QT, D])
        weights = {n: keep.sb(f"w_{n}", [P, CT, D]) for n in ("q", "k", "v", "o")}
        w_ready = sem("w_ready")
        with ExitStack() as mem:
            cross_attention(nc, Buffers(nc, mem), sem, a, ident, ones, xres, weights, w_ready)
        with ExitStack() as mem:
            self_attention(nc, Buffers(nc, mem), sem, a, ident, ones, xres, weights, w_ready)
        with ExitStack() as mem:
            experts(nc, Buffers(nc, mem), sem, a, ident, ones, xres, out)


class Buffers:
    def __init__(self, nc, mem):
        self.nc, self.mem = nc, mem

    def sb(self, name, shape, dt=F32):
        return self.mem.enter_context(self.nc.sbuf_tensor(name, shape, dt))

    def ps(self, name, shape, dt=F32):
        return self.mem.enter_context(self.nc.psum_tensor(name, shape, dt))


class Norm:

    def __init__(self, name, mem, sem, xres, out):
        self.x, self.out = xres, out
        self.stats = mem.sb(f"{name}_stats", [P, QT, 6])
        self.mv = mem.sb(f"{name}_mv", [P, QT, 2])
        self.ve = mem.sb(f"{name}_ve", [P, QT])
        self.std = mem.sb(f"{name}_std", [P, QT])
        self.inv = mem.sb(f"{name}_inv", [P, QT])
        self.tmp = mem.sb(f"{name}_tmp", [P, QT])
        self.var_ready, self.std_ready = sem(f"{name}_var_ready"), sem(f"{name}_std_ready")
        self.ready = sem(f"{name}_ready")

    def vector(self, dve, link):
        for t in range(QT):
            link(dve.bn_stats(self.stats[:, t, :], self.x[:, t, :]))
            link(dve.bn_aggr(self.mv[:, t, :], self.stats[:, t, :]))
        dve.tensor_scalar(self.ve[:], self.mv[:, :, 1], EPS, None, ALU.add).then_inc(self.var_ready, 1)
        dve.wait_ge(self.std_ready, 1)
        link(dve.reciprocal(self.inv[:], self.std[:]))
        link(dve.tensor_tensor(self.tmp[:], self.inv[:], self.inv[:], ALU.mult))
        link(dve.tensor_tensor(self.tmp[:], self.tmp[:], self.ve[:], ALU.mult))
        link(dve.tensor_scalar(self.tmp[:], self.tmp[:], -0.5, 1.5, ALU.mult, ALU.add))
        link(dve.tensor_tensor(self.inv[:], self.inv[:], self.tmp[:], ALU.mult))
        for t in range(QT):
            dve.tensor_scalar(self.out[:, t, :], self.x[:, t, :], self.mv[:, t, 0:1], self.inv[:, t:t + 1],
                              ALU.subtract, ALU.mult).then_inc(self.ready, 1)

    def scalar(self, act):
        act.wait_ge(self.var_ready, 1)
        act.activation(self.std[:], self.ve[:], ACT.Sqrt).then_inc(self.std_ready, 1)


def transpose_tokens(pe, dst, src, ident):
    for t in range(CT):
        for m in range(QT):
            last = pe.transpose(dst[:, t, m * P:(m + 1) * P], src[:, m, t * P:(t + 1) * P], ident[:])
    return last


def cross_attention(nc, mem, sem, a, ident, ones, xres, weights, w_ready):
    xn = mem.sb("xn", [P, QT, D])
    bd_q = mem.sb("bd_q", [P, P])
    bd_k = mem.sb("bd_k", [P, HG, STACK])
    bd_v = mem.sb("bd_v", [P, P])
    wo = mem.sb("x_wo", [P, CT, D])
    bo = mem.sb("x_bo", [P, D])
    tok = mem.sb("x_tok", [P, CT, SQ])
    tok2 = mem.sb("x_tok2", [P, CT, SQ])
    nat = mem.sb("nat", [P, U, D])
    msk = mem.sb("msk", [P, U, SQ], I32)
    steps_up = mem.sb("steps_up", [P, 2])
    steps_down = mem.sb("steps_down", [P, 2])
    bias = mem.sb("bias", [P, U])
    split = mem.sb("split", [P, 2, NH, 3, HD], F32R)
    ident_r = mem.sb("ident_r", [P, P], F32R)
    kst = mem.sb("kst", [KROWS, 2, NH, P], F32R)
    qst = mem.sb("qst", [KROWS, NH, SQ], F32R)
    probs = mem.sb("probs", [P, U, HG, SQ])
    den = mem.sb("den", [P, CT, HG, SQ])
    dsum = mem.sb("dsum", [P, CT, SQ])
    top = mem.sb("top", [P, CT, HG, SQ])
    tmp = mem.sb("x_tmp", [P, HG, SQ])
    mbias = mem.sb("mbias", [P, SQ])
    sums = mem.sb("sums", [P, 4])
    flag = mem.sb("flag", [1, 1], I32)
    sc = mem.ps("sc", [P, 2, HG, SQ])
    tr = mem.ps("tr", [P, HG, P])
    psum = mem.ps("psum", [P, SQ])
    acc = mem.ps("acc", [P, CT, SQ])

    norm = Norm("xnorm", mem, sem, xres, xn)
    S = {n: sem("x_" + n) for n in (
        "x_in", "small", "wo_in", "id0", "id", "ones", "dv", "tokT", "tokE", "q1", "q1E", "qr", "qs", "split",
        "hi", "tr", "ks_dve", "ks_act", "probe_sc", "probe_cp", "shift", "shift_in", "score", "exp", "pv",
        "den_dve", "bias", "steps", "zero", "den_sum", "okrow", "oksum", "flag", "norm", "vp", "vpE", "proj",
        "rows_set", "ident_r", "g_free", "g_row", "g_mask", "g_split", "g_tr", "g_ks", "g_sc", "g_arg", "g_exp",
        "g_pv", "g_max", "g_top", "g_fin", "g_dv", "g_zero", "g_den")}
    row_in = [sem(f"row_in{u}") for u in range(U)]
    mask_in = [sem(f"mask_in{u}") for u in range(U)]
    rows = a["ctx"].rearrange("(n p) c -> n p c", p=P)
    masks = a["mask_t"].rearrange("(n p) q -> n p q", p=P)

    def per_turn(body, eng):
        body(0)
        with eng.Fori(1, TURNS - 1) as i:
            body(i)
        body(TURNS - 1)

    def last_turn(i):
        return isinstance(i, int) and i == TURNS - 1

    with nc.Block() as block:
        @block.sync
        def _(sp):
            sp.dma_start(xres[:], a["x"].rearrange("(t p) c -> p t c", p=P)).then_inc(S["x_in"], 16)
            sp.dma_start(bd_q[:], a["bd_wq_t"]).then_inc(S["small"], 16)
            sp.dma_start(bd_k[:], a["bd_wk"]).then_inc(S["small"], 16)
            for u in range(U):
                sp.dma_start(nat[:, u, :], rows[u]).then_inc(row_in[u], 16)
                sp.dma_start(msk[:, u, :], masks[u]).then_inc(mask_in[u], 16)
            sp.dma_start(bd_v[:], a["bd_wv_t"]).then_inc(S["wo_in"], 16)
            sp.dma_start(wo[:], a["x_wo_t"].rearrange("(t p) o -> p t o", p=P)).then_inc(S["wo_in"], 16)
            sp.dma_start(bo[:], a["x_bo"].partition_broadcast(P)).then_inc(S["wo_in"], 16)
            with sp.Fori(1, TURNS) as i:
                for u in range(U):
                    sp.wait_ge(S["steps"], 2 * (U * (i - 1) + u + 2))
                    sp.dma_start(msk[:, u, :], masks[U * i + u]).then_inc(mask_in[u], 16)
                    sp.wait_ge(S["pv"], CT * (U * (i - 1) + u + 1))
                    sp.dma_start(nat[:, u, :], rows[U * i + u]).then_inc(row_in[u], 16)
            for n in ("q", "k", "v", "o"):
                sp.dma_start(weights[n][:], a["w" + n].rearrange("(t p) o -> p t o", p=P)).then_inc(w_ready, 16)
            sp.wait_ge(S["flag"], 1)
            general = sp.value_load(flag[0:1, 0:1], min_val=0, max_val=1)
            with sp.If(general):
                for turn in range(2):
                    with sp.Fori(0, NT) as i:
                        sp.wait_ge(S["g_free"], NT * turn + i + 1)
                        sp.dma_start(nat[:, 0, :], rows[i]).then_inc(S["g_row"], 16)
                        sp.dma_start(msk[:, 0, :], masks[i]).then_inc(S["g_mask"], 16)
                sp.wait_ge(S["g_fin"], 1)
            with sp.Else():
                sp.nop()

        @block.gpsimd
        def _(pool):
            pool.memset(ident[:], 0.0).then_inc(S["id0"], 1)
            pool.wait_ge(S["id0"], 1)
            pool.affine_select(out=ident[:], in_=ident[:], compare_op=ALU.not_equal, fill=1.0, base=0,
                               pattern=[[-1, P]], channel_multiplier=1).then_inc(S["id"], 1)
            pool.memset(ones[:], 1.0).then_inc(S["ones"], 1)
            pool.wait_ge(S["probe_cp"], CT)
            pool.partition_all_reduce(den[:], probs[:], P, RMAX).then_inc(S["shift"], 1)
            pool.wait_ge(S["flag"], 1)
            general = pool.value_load(flag[0:1, 0:1], min_val=0, max_val=1)
            with pool.If(general):
                pool.wait_ge(S["g_max"], 1)
                pool.partition_all_reduce(den[:], top[:], P, RMAX).then_inc(S["g_top"], 1)
                pool.wait_ge(S["g_fin"], 1)
            with pool.Else():
                pool.nop()

        @block.scalar
        def _(act):
            norm.scalar(act)

            def evacuate(i, u, g, tile):
                m = CT * tile + g
                act.wait_ge(S["tr"], m + 1)
                wait(act, S["score"], m - 2 * CT + 1)
                act.activation(kst[0:STACK, (u + 1) % 2, HG * g:HG * (g + 1), :], tr[0:STACK],
                               ACT.Copy).then_inc(S["ks_act"], 1)

            for g in range(1, CT):
                evacuate(0, -1, g, 0)

            def body(i):
                for u in range(U):
                    tile = U * i + u
                    for g in range(CT):
                        n = CT * tile + g
                        if g and not (last_turn(i) and u == U - 1):
                            evacuate(i, u, g, tile + 1)
                        act.wait_ge(S["bias"], tile + 1)
                        act.wait_ge(S["score"], n + 1)
                        wait(act, S["pv"], n - CT + 1)
                        if g < 3:
                            wait(act, S["den_dve"], 3 * (tile - 1) + g + 2)
                        act.activation(probs[:, g], sc[:, g % 2], ACT.Exp,
                                       bias=bias[:, u:u + 1]).then_inc(S["exp"], 1)

            per_turn(body, act)
            act.wait_ge(S["flag"], 1)
            general = act.value_load(flag[0:1, 0:1], min_val=0, max_val=1)
            with act.If(general):
                with act.Fori(0, NT) as i:
                    for g in range(CT):
                        act.wait_ge(S["g_arg"], CT * i + g + 1)
                        act.activation(probs[:, 0], tmp[:], ACT.Exp).then_inc(S["g_exp"], 1)
                act.wait_ge(S["g_fin"], 1)
            with act.Else():
                act.nop()

        def general_vector(dve):
            link = Chain(dve, S["g_dv"])
            link(dve.memset(top[:], -3.0e38))
            link(dve.tensor_scalar(qst[STACK:KROWS].rearrange("p h q -> p (h q)"),
                                   ones[STACK:KROWS, 0:1].to_broadcast([1, NH * SQ]), 0.0, None, ALU.mult))
            dve.sem_inc(S["g_free"], 1)
            base = link.n
            for turn in range(2):
                if turn:
                    dve.sem_inc(S["g_max"], 1)
                    dve.wait_ge(S["g_top"], 1)
                    dve.tensor_copy(top[:], den[:]).then_inc(S["g_zero"], 1)
                    dve.wait_ge(S["g_zero"], 1)
                    dve.memset(den[:], 0.0).then_inc(S["g_zero"], 1)
                    dve.memset(acc[:], 0.0).then_inc(S["g_zero"], 1)
                steps = 3 + 2 * CT if turn == 0 else 3 + 3 * CT
                with dve.Fori(0, NT) as i:
                    seen = NT * turn + i
                    n = base + steps * i
                    dve.wait_ge(S["g_row"], 16 * (seen + 1))
                    dve.wait_ge(S["g_mask"], 16 * (seen + 1))
                    dve.tensor_copy(split[:, 0, :, 0:3:2, :],
                                    nat[:, 0, :].rearrange("p (h c) -> p h c", c=HD).unsqueeze(2)
                                    .to_broadcast([P, NH, 2, HD])).then_inc(S["g_dv"], 1)
                    dve.wait_ge(S["g_dv"], n + 1)
                    dve.tensor_tensor(split[:, 0, :, 1, :], nat[:, 0, :].rearrange("p (h c) -> p h c", c=HD),
                                      split[:, 0, :, 0, :].bitcast(F32), ALU.subtract).then_inc(S["g_dv"], 1)
                    dve.wait_ge(S["g_dv"], n + 2)
                    dve.tensor_scalar(mbias[:], msk[:, 0, :], 0, MASKED, ALU.is_equal, ALU.mult)\
                       .then_inc(S["g_dv"], 1)
                    dve.wait_ge(S["g_dv"], n + 3)
                    dve.sem_inc(S["g_split"], 1)
                    k = n + 3
                    for g in range(CT):
                        dve.wait_ge(S["g_tr"], CT * seen + g + 1)
                        dve.tensor_copy(kst[0:STACK, 0, HG * g:HG * (g + 1), :], tr[0:STACK])\
                           .then_inc(S["g_ks"], 1)
                        dve.wait_ge(S["g_sc"], CT * seen + g + 1)
                        if turn and g:
                            dve.wait_ge(S["g_exp"], CT * i + g)
                        dve.tensor_tensor(tmp[:], sc[:, 0], mbias[:].unsqueeze(1).to_broadcast([P, HG, SQ]),
                                          ALU.add).then_inc(S["g_dv"], 1)
                        dve.wait_ge(S["g_dv"], k + 1)
                        if turn == 0:
                            dve.tensor_tensor(top[:, g], top[:, g], tmp[:], ALU.max).then_inc(S["g_dv"], 1)
                            dve.wait_ge(S["g_dv"], k + 2)
                            k = k + 2
                        else:
                            dve.tensor_tensor(tmp[:], tmp[:], top[:, g], ALU.subtract).then_inc(S["g_dv"], 1)
                            dve.wait_ge(S["g_dv"], k + 2)
                            dve.sem_inc(S["g_arg"], 1)
                            dve.wait_ge(S["g_exp"], CT * i + g + 1)
                            dve.tensor_tensor(den[:, g], den[:, g], probs[:, 0], ALU.add).then_inc(S["g_dv"], 1)
                            dve.wait_ge(S["g_dv"], k + 3)
                            k = k + 3
                    if turn:
                        dve.wait_ge(S["g_pv"], CT * (i + 1))
                    dve.sem_inc(S["g_free"], 1)
                base = base + steps * NT
            dve.wait_ge(S["g_fin"], 1)
            dve.tensor_copy(dsum[:], sc[:, 0]).then_inc(S["g_zero"], 1)
            dve.wait_ge(S["g_zero"], 4)

        @block.vector
        def _(dve):
            link = Chain(dve, S["dv"])
            dve.memset(acc[:], 0.0).then_inc(S["zero"], 1)
            dve.memset(psum[:], 0.0).then_inc(S["zero"], 1)
            dve.wait_ge(S["x_in"], 16)
            norm.vector(dve, link)
            dve.wait_ge(S["tokT"], 1)
            dve.tensor_copy(tok[:], sc[:, 0]).then_inc(S["tokE"], 1)
            dve.wait_ge(S["q1"], 1)
            dve.tensor_copy(tok2[:], sc[:, 1]).then_inc(S["q1E"], 1)
            for t in range(CT):
                heads = slice(HG * t, HG * (t + 1))
                dve.wait_ge(S["qr"], t + 1)
                link(dve.tensor_scalar(qst[0:STACK, heads, :], sc[0:STACK, t % 2], SCALE, None, ALU.mult))
                dve.scalar_tensor_tensor(qst[2 * HD:STACK, heads, :], sc[2 * HD:STACK, t % 2], SCALE,
                                         qst[2 * HD:STACK, heads, :].bitcast(F32), ALU.mult,
                                         ALU.subtract).then_inc(S["qs"], 1)
            dve.wait_ge(S["ones"], 1)
            link(dve.tensor_copy(ident_r[:], ident[:]))
            dve.sem_inc(S["ident_r"], 1)
            for b in range(2):
                link(dve.tensor_copy(kst[STACK:KROWS, b].rearrange("p h k -> p (h k)"),
                                     ones[STACK:KROWS, 0:1].to_broadcast([1, NH * P])))
            link(dve.tensor_scalar(qst[STACK:KROWS].rearrange("p h q -> p (h q)"),
                                   ones[STACK:KROWS, 0:1].to_broadcast([1, NH * SQ]), 0.0, None, ALU.mult))
            dve.sem_inc(S["rows_set"], 1)

            def row_hi(u, b, seen):
                dve.wait_ge(row_in[u], seen)
                dve.tensor_copy(split[:, b, :, 0:3:2, :],
                                nat[:, u, :].rearrange("p (h c) -> p h c", c=HD).unsqueeze(2)
                                .to_broadcast([P, NH, 2, HD])).then_inc(S["hi"], 1)

            def row_lo(u, b, tile):
                dve.wait_ge(S["hi"], tile + 1)
                dve.tensor_tensor(split[:, b, :, 1, :], nat[:, u, :].rearrange("p (h c) -> p h c", c=HD),
                                  split[:, b, :, 0, :].bitcast(F32), ALU.subtract).then_inc(S["split"], 1)

            def evacuate(b, g, tile):
                m = CT * tile + g
                dve.wait_ge(S["tr"], m + 1)
                wait(dve, S["score"], m - 2 * CT + 1)
                dve.tensor_copy(kst[0:STACK, b, HG * g:HG * (g + 1), :], tr[0:STACK])\
                   .then_inc(S["ks_dve"], 1)

            def look_at_mask(u, tile, seen):
                now, then = u % 2, (u + 1) % 2
                dve.wait_ge(mask_in[u], seen)
                wait(dve, S["exp"], CT * (tile - U + 1))
                dve.wait_ge(S["steps"], 2 * tile + 2)
                dve.tensor_scalar(bias[:, u:u + 1], msk[:, u, 0:1], 0.0, HIDE, ALU.is_equal, ALU.mult)\
                   .then_inc(S["bias"], 1)
                dve.scalar_tensor_tensor(steps_up[:, now:now + 1], msk[:, u, SQ - 1:SQ], msk[:, u, 0:1],
                                         steps_up[:, then:then + 1], ALU.subtract, ALU.max).then_inc(S["steps"], 1)
                dve.tensor_tensor_reduce(out=mbias[:, 1:SQ], in0=msk[:, u, 0:SQ - 1], in1=msk[:, u, 1:SQ],
                                         scale=1.0, scalar=steps_down[:, then:then + 1], op0=ALU.subtract,
                                         op1=ALU.max, accum_out=steps_down[:, now:now + 1])\
                   .then_inc(S["steps"], 1)

            for tile in range(2):
                row_hi(tile, tile, 16)
                row_lo(tile, tile, tile)
            evacuate(0, 0, 0)
            for g in range(CT):
                dve.wait_ge(S["probe_sc"], g + 1)
                dve.tensor_copy(probs[:, g], sc[:, g % 2]).then_inc(S["probe_cp"], 1)
            dve.wait_ge(S["shift"], 1)
            link(dve.tensor_scalar(qst[STACK:KROWS].rearrange("p h q -> p (h q)"),
                                   den[STACK:KROWS].rearrange("p g h q -> p (g h q)"), -1.0, None, ALU.mult))
            dve.sem_inc(S["shift_in"], 1)
            dve.memset(den[:, 0:3], 0.0).then_inc(S["den_dve"], 1)
            dve.memset(steps_up[:], 0.0).then_inc(S["steps"], 1)
            dve.memset(steps_down[:], 0.0).then_inc(S["steps"], 1)
            for tile in range(2):
                look_at_mask(tile, tile, 16)

            def add(tile, g):
                dve.wait_ge(S["exp"], CT * tile + g + 1)
                dve.wait_ge(S["den_dve"], 3 * tile + g + 1)
                dve.tensor_tensor(den[:, g], den[:, g], probs[:, g], ALU.add).then_inc(S["den_dve"], 1)

            def body(i):
                for u in range(U):
                    tile = U * i + u
                    b2, seen2 = (u + 2) % U, 16 * (i + 1 + (u + 2) // U)
                    more1 = not (last_turn(i) and u >= U - 1)
                    more2 = not (last_turn(i) and u >= U - 2)
                    if more1:
                        evacuate((u + 1) % 2, 0, tile + 1)
                    if more2:
                        dve.wait_ge(S["tr"], CT * (tile + 1))
                        row_hi(b2, u % 2, seen2)
                    add(tile, 0)
                    if more2:
                        row_lo(b2, u % 2, tile + 2)
                    add(tile, 1)
                    if more2:
                        look_at_mask(b2, tile + 2, seen2)
                    add(tile, 2)

            per_turn(body, dve)
            dve.wait_ge(S["den_sum"], 1)
            dve.wait_ge(S["pv"], NT * CT)
            count = Chain(dve, S["okrow"])
            count(dve.tensor_copy(dsum[:, 0:3], sc[:, 0, 0:3]))
            count(dve.tensor_copy(dsum[:, 3], psum[:]))
            count(dve.tensor_tensor(sums[:, 0:1], steps_up[:, 1:2], steps_down[:, 1:2], ALU.max))
            count(dve.tensor_scalar(sums[:, 0:1], sums[:, 0:1], 0.0, None, ALU.is_gt))
            count(dve.tensor_scalar(tmp[:], dsum[:], DEN_MIN, None, ALU.is_ge))
            count(dve.scalar_tensor_tensor(tmp[:], dsum[:], DEN_MAX, tmp[:], ALU.is_le, ALU.mult))
            count(dve.tensor_reduce(sums[:, 1:2], tmp[:], AXY, ALU.min))
            count(dve.tensor_scalar(sums[:, 2:3], sums[:, 1:2], 1.0, None, ALU.is_lt))
            count(dve.tensor_tensor(sums[:, 3:4], sums[:, 0:1], sums[:, 2:3], ALU.add))
            dve.wait_ge(S["oksum"], 1)
            dve.tensor_scalar(flag[:], tr[0:1, 0, 0:1], 0.5, None, ALU.is_gt).then_inc(S["flag"], 1)
            dve.wait_ge(S["flag"], 1)
            general = dve.value_load(flag[0:1, 0:1], min_val=0, max_val=1)
            with dve.If(general):
                general_vector(dve)
            with dve.Else():
                dve.nop()
            tail = Chain(dve, S["norm"])
            tail(dve.reciprocal(tmp[:], dsum[:]))
            tail(dve.tensor_tensor(tok[:], acc[:], tmp[:], ALU.mult))
            dve.wait_ge(S["vp"], 1)
            dve.tensor_copy(tok2[:], sc[:, 1]).then_inc(S["vpE"], 1)
            dve.wait_ge(S["wo_in"], 48)
            dve.wait_ge(S["proj"], 1)
            for m in range(QT):
                tail(dve.tensor_tensor(xres[:, m, :], xres[:, m, :], bo[:], ALU.add))
                tail(dve.tensor_tensor(xres[:, m, :], xres[:, m, :],
                                       sc[:, 0].rearrange("p h q -> p (h q)")[:, m * D:(m + 1) * D], ALU.add))

        @block.tensor
        def _(pe):
            scf = sc[:].rearrange("p s h q -> p s (h q)")
            pe.wait_ge(S["id"], 1)
            pe.wait_ge(norm.ready, QT)
            transpose_tokens(pe, sc[:, 0], xn, ident).then_inc(S["tokT"], 1)
            pe.wait_ge(S["small"], 32)
            pe.wait_ge(S["tokE"], 1)
            for t in range(CT):
                last = pe.matmul(sc[:, 1, t], bd_q[:], tok[:, t], start=True, stop=True)
            last.then_inc(S["q1"], 1)
            pe.wait_ge(S["q1E"], 1)
            for t in range(CT):
                wait(pe, S["qs"], t - 1)
                for j in range(HG):
                    last = pe.matmul(sc[0:STACK, t % 2, j], bd_k[:, j], tok2[:, t], start=True, stop=True)
                last.then_inc(S["qr"], 1)

            def transposes(b, g, tile):
                pe.wait_ge(S["split"], tile + 1)
                if g == 1:
                    pe.wait_ge(S["ks_dve"], tile + 1)
                else:
                    wait(pe, S["ks_act"], 3 * tile + max(g - 1, 0))
                for j in range(HG):
                    last = pe.matmul(tr[0:STACK, j], split[:, b, HG * g + j].rearrange("p s c -> p (s c)"),
                                     ident_r[:], start=True, stop=True)
                last.then_inc(S["tr"], 1)

            def scores(b, g, tile, signal):
                if g == 0:
                    pe.wait_ge(S["ks_dve"], tile + 1)
                else:
                    pe.wait_ge(S["ks_act"], 3 * tile + g)
                for j in range(HG):
                    h = HG * g + j
                    last = pe.matmul(sc[:, g % 2, j], kst[:, b, h], qst[:, h], start=True, stop=True)
                last.then_inc(signal, 1)

            def weighted(u, g, signal, src):
                for j in range(HG):
                    last = pe.matmul(acc[HD * j:HD * (j + 1), g], nat[:, u, (HG * g + j) * HD:(HG * g + j + 1) * HD],
                                     src[:, j], start=False, stop=True, skip_group_check=True,
                                     tile_position=(0, HD * j))
                if signal is S["pv"] and g == 3:
                    for j in range(HG):
                        last = pe.matmul(psum[HD * j:HD * (j + 1)], ones[:, 0:HD], src[:, j], start=False,
                                         stop=True, skip_group_check=True, tile_position=(0, HD * j))
                last.then_inc(signal, 1)

            pe.wait_ge(S["ident_r"], 1)
            for g in range(CT):
                transposes(0, g, 0)
            pe.wait_ge(S["qs"], CT)
            pe.wait_ge(S["rows_set"], 1)
            for g in range(CT):
                wait(pe, S["probe_cp"], g - 1)
                scores(0, g, 0, S["probe_sc"])
            pe.wait_ge(S["probe_cp"], CT)
            pe.wait_ge(S["shift_in"], 1)
            pe.wait_ge(S["zero"], 2)

            def body(i):
                for u in range(U):
                    tile = U * i + u
                    for g in range(CT):
                        n = CT * tile + g
                        if not (last_turn(i) and u == U - 1):
                            transposes((u + 1) % 2, g, tile + 1)
                        wait(pe, S["exp"], n - 1)
                        scores(u % 2, g, tile, S["score"])
                        if not (isinstance(i, int) and n < 2):
                            weighted((u if g >= 2 else u - 1) % U, (g - 2) % CT, S["pv"], probs[:, (g - 2) % CT])

            per_turn(body, pe)
            for g in (2, 3):
                pe.wait_ge(S["exp"], NT * CT - 3 + g)
                weighted(U - 1, g, S["pv"], probs[:, g])
            pe.wait_ge(S["den_dve"], 3 * NT + 1)
            pe.wait_ge(S["exp"], NT * CT)

            def total(groups, signal):
                for g in groups:
                    for j in range(HG):
                        last = pe.matmul(sc[HD * j:HD * (j + 1), 0, g], ones[:, 0:HD], den[:, g, j],
                                         start=True, stop=True, tile_position=(0, HD * j))
                last.then_inc(signal, 1)

            total(range(3), S["den_sum"])
            pe.wait_ge(S["okrow"], 9)
            pe.matmul(tr[0:1, 0, 0:1], sums[:, 3:4], ones[:, 0:1], start=True, stop=True).then_inc(S["oksum"], 1)
            pe.wait_ge(S["flag"], 1)
            general = pe.value_load(flag[0:1, 0:1], min_val=0, max_val=1)
            with pe.If(general):
                for turn in range(2):
                    if turn:
                        pe.wait_ge(S["g_zero"], 3)
                    with pe.Fori(0, NT) as i:
                        seen = NT * turn + i
                        pe.wait_ge(S["g_split"], seen + 1)
                        for g in range(CT):
                            for j in range(HG):
                                last = pe.matmul(tr[0:STACK, j],
                                                 split[:, 0, HG * g + j].rearrange("p s c -> p (s c)"),
                                                 ident_r[:], start=True, stop=True)
                            last.then_inc(S["g_tr"], 1)
                            pe.wait_ge(S["g_ks"], CT * seen + g + 1)
                            for j in range(HG):
                                h = HG * g + j
                                last = pe.matmul(sc[:, 0, j], kst[:, 0, h], qst[:, h], start=True, stop=True)
                            last.then_inc(S["g_sc"], 1)
                            if turn:
                                pe.wait_ge(S["g_exp"], CT * i + g + 1)
                                weighted(0, g, S["g_pv"], probs[:, 0])
                            else:
                                pe.wait_ge(S["g_dv"], 2 + (3 + 2 * CT) * i + 3 + 2 * (g + 1))
                pe.wait_ge(S["g_dv"], 2 + (6 + 5 * CT) * NT)
                total(range(CT), S["g_den"])
                pe.wait_ge(S["g_den"], 1)
                pe.sem_inc(S["g_fin"], 1)
            with pe.Else():
                pe.nop()
            pe.wait_ge(S["norm"], 2)
            pe.wait_ge(S["wo_in"], 48)
            for t in range(CT):
                last = pe.matmul(sc[:, 1, t], bd_v[:], tok[:, t], start=True, stop=True)
            last.then_inc(S["vp"], 1)
            pe.wait_ge(S["vpE"], 1)
            for m in range(QT):
                for t in range(CT):
                    last = pe.matmul(scf[:, 0, m * D:(m + 1) * D], tok2[:, t, m * P:(m + 1) * P], wo[:, t],
                                     start=t == 0, stop=t == CT - 1)
            last.then_inc(S["proj"], 1)


def self_attention(nc, mem, sem, a, ident, ones, xres, weights, w_ready):
    PAIRS = NH // 2
    NU_SELF = PAIRS
    UP = SP_ // P // 2
    NU_PAST = NP * PAIRS * UP
    NU_EXACT = NH * QT * NP
    KT = NP * SP_ // P
    past = mem.sb("past", [P, CT, SP_])
    wr = mem.sb("wr", [P, 2 * CT, D])
    wrk, wrv = wr[:, 0:CT], wr[:, CT:2 * CT]
    wrq = mem.sb("wrq", [P, CT, D])
    brk_c, brq_c, bq_c, bk_c, bo_c = (mem.sb(n, [P, CT]) for n in ("brk_c", "brq_c", "bq_c", "bk_c", "bo_c"))
    rk = mem.sb("rk", [P, CT, NP * SP_])
    rv = mem.sb("rv", [P, KT, D])
    row_bias = mem.sb("row_bias", [P, 4, D])
    h = mem.sb("b_h", [P, QT, D])
    ht = mem.sb("b_ht", [P, CT, SQ])
    qpad = mem.sb("qpad", [P, CT, HG, SQ])
    kt = mem.sb("b_kt", [P, CT, SQ])
    v = mem.sb("b_v", [P, QT, D])
    ex = mem.sb("b_ex", [P, 3, 1024])
    ct = mem.sb("b_ct", [P, CT, SQ])
    inv = mem.sb("b_inv", [P, CT, NP, SQ])
    term = mem.sb("b_term", [P, SQ])
    flag = mem.sb("b_flag", [1, 1], I32)
    few = mem.sb("b_few", [P, 2])
    nmax = mem.sb("nmax", [P, NU_EXACT])
    tot = mem.sb("tot", [P, NU_EXACT])
    sc = mem.ps("b_sc", [P, 2, 1024])
    tr = mem.ps("b_tr", [P, 8, P])
    acc = mem.ps("b_acc", [P, 2, D])
    accq = acc[:].rearrange("p b (t q) -> p (b t) q", q=SQ)
    shift = [wr[:].rearrange("p t c -> p (t c)"),
             past[:].rearrange("p t c -> p (t c)")]
    top = h
    pr, pt = ex[:, 0:2], inv[:].rearrange("p t s (k q) -> p (t s k) q", q=P).rearrange("p (b n) q -> p b n q", b=2)
    wg = wr[:].rearrange("p (t n) c -> p t (n c)", n=2)
    o_t, o_nat = kt, v
    r_t, r_nat, gate = ct, h, ex

    norm = Norm("bnorm", mem, sem, xres, h)
    S = {n: sem("b_" + n) for n in (
        "past_in", "wr_in", "bias_in", "wg_in", "pmm", "pev_act", "pev_dve", "dv", "hT", "hE", "q", "qE", "k",
        "kE", "v", "vE", "filled", "read", "shift", "exp", "pv", "acc_free", "okrow", "oksum", "flag", "g_dv",
        "g_sc", "g_max", "g_exp", "g_norm", "g_tr", "g_ev_dve", "g_ev_act", "g_pv", "accE", "o", "oT", "oE",
        "oTE", "rq", "rqE", "rT", "rE", "gmm", "z", "ez")}

    self_units = [(pair, 0, (0, 1), 0, 1) for pair in range(PAIRS)]
    past_units = [(pair, state, (2 * UP * state + 2 * c, 2 * UP * state + 2 * c + 1), c, UP)
                  for state in range(NP) for pair in range(PAIRS) for c in range(UP)]
    all_units = self_units + past_units
    SELF, PAST = range(NU_SELF), range(NU_SELF, NU_SELF + NU_PAST)

    def filling(u):
        return u + PAIRS * (1 if u < NU_SELF else 1 + NP)

    def group(u):
        return all_units[u][0] + (0 if u < NU_SELF else PAIRS * (1 + all_units[u][1]))

    def probes():
        for n in range(PAIRS * (1 + NP)):
            yield n, n if n < PAIRS else n + NU_SELF, n % PAIRS, max(0, n // PAIRS - 1)

    with nc.Block() as block:
        @block.sync
        def _(sp):
            pastv = [a["past_t"][p].rearrange("(t p) k -> p t k", p=P) for p in range(NP)]
            sp.dma_start(wrk[:], a["wrk"].rearrange("(t p) o -> p t o", p=P)).then_inc(S["wr_in"], 16)
            sp.dma_start(past[:], pastv[0]).then_inc(S["past_in"], 16)
            sp.dma_start(wrv[:], a["wrv"].rearrange("(t p) o -> p t o", p=P)).then_inc(S["wr_in"], 16)
            for dst, name in ((brk_c, "brk"), (brq_c, "brq"), (bq_c, "bq"), (bk_c, "bk"), (bo_c, "bo")):
                sp.dma_start(dst[:], a[name + "_c"]).then_inc(S["bias_in"], 16)
            for n, name in enumerate(("brv", "bv", "bo", "bg")):
                sp.dma_start(row_bias[:, n], a[name].partition_broadcast(P)).then_inc(S["bias_in"], 16)
            sp.dma_start(wrq[:], a["wrq"].rearrange("(t p) o -> p t o", p=P)).then_inc(S["wr_in"], 16)
            sp.wait_ge(S["pmm"], 16)
            sp.dma_start(past[:], pastv[1]).then_inc(S["past_in"], 16)
            sp.wait_ge(S["read"], filling(PAST[NU_PAST // 2 - 1]) + 1)
            for n in range(2):
                sp.dma_start(wg[:, :, n * D:(n + 1) * D],
                             a["wg"][n * D:(n + 1) * D].rearrange("(t p) o -> p t o", p=P)).then_inc(S["wg_in"], 16)

        slots = [sc[:, n // 2, (n % 2) * D:(n % 2 + 1) * D] for n in range(4)]

        @block.gpsimd
        def _(pool):
            for n, fill, pair, state in probes():
                if n == PAIRS:
                    pool.wait_ge(S["accE"], 1)
                pool.wait_ge(S["read"], fill + 1)
                pool.partition_all_reduce(shift[state][:, pair * 2 * SQ:(pair + 1) * 2 * SQ], top[:, n % 2], P,
                                          RMAX).then_inc(S["shift"], 1)

        @block.scalar
        def _(act):
            act.wait_ge(S["bias_in"], 9 * 16)
            for n in range(16):
                mt, c = (n % 8) % CT, 2 * (n // 8) + (n % 8) // CT
                act.wait_ge(S["pmm"], 2 * n + 1)
                act.activation(rk[:, mt, c * D:(c + 1) * D], slots[(2 * n) % 4], ACT.Identity,
                               bias=brk_c[:, mt:mt + 1]).then_inc(S["pev_act"], 1)
            norm.scalar(act)
            act.wait_ge(S["k"], 1)
            for t in range(CT):
                last = act.activation(kt[:, t], sc[:, 1, t * SQ:(t + 1) * SQ], ACT.Identity, bias=bk_c[:, t:t + 1])
            last.then_inc(S["kE"], 1)

            def attend(units):
                for u in units:
                    act.wait_ge(S["read"], filling(u) + 1)
                    act.activation(ex[:, u % 3], ex[:, u % 3], ACT.Exp).then_inc(S["exp"], 1)

            attend(SELF)
            act.wait_ge(S["oT"], 1)
            for t in range(CT):
                last = act.activation(o_t[:, t], sc[:, 1, t * SQ:(t + 1) * SQ], ACT.Identity, bias=bo_c[:, t:t + 1])
            last.then_inc(S["oTE"], 1)
            attend(PAST)
            act.wait_ge(S["flag"], 1)
            general = act.value_load(flag[0:1, 0:1], min_val=0, max_val=1)
            with act.If(general):
                for u in range(NU_EXACT + 2):
                    if u < NU_EXACT:
                        act.wait_ge(S["g_max"], u + 1)
                        wait(act, S["g_tr"], u - 1)
                        act.activation(pr[:, u % 2], sc[:, u % 2], ACT.Exp, bias=nmax[:, u:u + 1],
                                       accum_out=tot[:, u:u + 1]).then_inc(S["g_exp"], 1)
                    if u >= 2:
                        act.wait_ge(S["g_tr"], u - 1)
                        wait(act, S["g_pv"], u - 3)
                        act.activation(pt[:, u % 2, 4:8], tr[:, 4:8], ACT.Copy).then_inc(S["g_ev_act"], 1)
            with act.Else():
                act.nop()
            act.wait_ge(S["z"], 1)
            act.activation(gate[:, 1], gate[:, 0], ACT.Exp, scale=-1.0).then_inc(S["ez"], 1)

        @block.vector
        def _(dve):
            link = Chain(dve, S["dv"])
            dve.wait_ge(S["bias_in"], 9 * 16)
            for n in range(16):
                dve.wait_ge(S["pmm"], 2 * n + 2)
                dve.tensor_tensor(rv[:, n], slots[(2 * n + 1) % 4], row_bias[:, 0], ALU.add).then_inc(S["pev_dve"], 1)
            norm.vector(dve, link)
            link(dve.memset(qpad[:], 0.0))
            dve.wait_ge(S["hT"], 1)
            dve.tensor_copy(ht[:].rearrange("p t q -> p (t q)"), tr[:].rearrange("p a b -> p (a b)"))\
               .then_inc(S["hE"], 1)

            def pad(bias, src):
                for t in range(CT):
                    for j in range(HG):
                        part = slice(HD * j, HD * (j + 1))
                        last = dve.tensor_scalar(qpad[part, t, j], src[part, t * SQ:(t + 1) * SQ],
                                                 bias[part, t:t + 1], SCALE, ALU.add, ALU.mult)
                return last

            dve.wait_ge(S["q"], 1)
            pad(bq_c, sc[:, 0]).then_inc(S["qE"], 1)
            dve.wait_ge(S["v"], 1)
            for m in range(QT):
                last = dve.tensor_tensor(v[:, m], tr[:, 4 * m:4 * m + 4].rearrange("p a b -> p (a b)"),
                                         row_bias[:, 1], ALU.add)
            last.then_inc(S["vE"], 1)

            def probe(n, fill):
                dve.wait_ge(S["filled"], fill + 1)
                wait(dve, S["shift"], n - 1)
                dve.tensor_reduce(top[:, n % 2], sc[:, n % 2].rearrange("p (k c) -> p c k", k=2), AX,
                                  ALU.max).then_inc(S["read"], 1)

            def take(g, x):
                pair, state, _, _, count = all_units[x]
                t = pair // 2
                dve.wait_ge(S["pv"], x + 1)
                for hh in range(2):
                    j = 2 * (pair % 2) + hh
                    dst = slice(HD * j, HD * (j + 1))
                    num, den = (acc[64 * hh + HD * n:64 * hh + HD * (n + 1), g % 2, 0:SQ] for n in range(2))
                    rec = inv[dst, t, state]
                    link(dve.reciprocal(rec, den))
                    if state == 0:
                        last = dve.scalar_tensor_tensor(ct[dst, t], num, 1.0 if count == 1 else 1.0 / NP, rec,
                                                        ALU.mult, ALU.mult)
                    else:
                        link(dve.scalar_tensor_tensor(term[dst], num, 1.0 / NP, rec, ALU.mult, ALU.mult))
                        last = dve.tensor_tensor(r_t[dst, t], r_t[dst, t], term[dst], ALU.add)
                    if hh == 0:
                        link(last)
                last.then_inc(S["acc_free"], 1)

            def attend(units):
                for u in range(units.start, units.stop + 3):
                    if u < units.stop:
                        pair, state, _, c, _ = all_units[u]
                        if c == 0:
                            dve.wait_ge(S["shift"], group(u) + 1)
                        dve.wait_ge(S["filled"], filling(u) + 1)
                        wait(dve, S["pv"], u - 2)
                        dve.tensor_tensor(ex[:, u % 3].rearrange("p (k c) -> p k c", k=2),
                                          sc[:, u % 2].rearrange("p (k c) -> p k c", k=2),
                                          shift[state][:, None, pair * 2 * SQ:(pair + 1) * 2 * SQ]
                                          .to_broadcast([P, 2, 2 * SQ]), ALU.subtract).then_inc(S["read"], 1)
                    x = u - 3
                    if x >= units.start and all_units[x][3] == all_units[x][4] - 1:
                        take(group(x), x)

            for n, fill, pair, state in probes():
                if n < PAIRS:
                    probe(n, fill)
            attend(SELF)
            dve.wait_ge(S["acc_free"], PAIRS)
            dve.sem_inc(S["accE"], 1)
            dve.wait_ge(S["o"], 1)
            for m in range(QT):
                last = dve.tensor_tensor(o_nat[:, m], sc[:, 0, m * D:(m + 1) * D], row_bias[:, 2], ALU.add)
            last.then_inc(S["oE"], 1)
            dve.wait_ge(S["rq"], 1)
            pad(brq_c, tr[:].rearrange("p a b -> p (a b)")).then_inc(S["rqE"], 1)
            for n, fill, pair, state in probes():
                if n >= PAIRS:
                    probe(n, fill)
            attend(PAST)
            dve.wait_ge(S["acc_free"], PAIRS * (1 + NP))
            ok = ex[:, 0:2].rearrange("p a b -> p (a b)")
            invf = inv[:].rearrange("p t s q -> p (t s q)")
            count = Chain(dve, S["okrow"])
            count(dve.tensor_scalar(ok, invf, 1.0 / DEN_MAX, None, ALU.is_ge))
            count(dve.scalar_tensor_tensor(ok, invf, 1.0 / DEN_MIN, ok, ALU.is_le, ALU.mult))
            count(dve.tensor_reduce(few[:, 0:1], ok, AX, ALU.min))
            count(dve.tensor_scalar(few[:, 1:2], few[:, 0:1], 1.0, None, ALU.is_lt))
            dve.wait_ge(S["oksum"], 1)
            dve.tensor_scalar(flag[:], tr[0:1, 0, 0:1], 0.5, None, ALU.is_gt).then_inc(S["flag"], 1)
            dve.wait_ge(S["flag"], 1)
            general = dve.value_load(flag[0:1, 0:1], min_val=0, max_val=1)
            with dve.If(general):
                here = Chain(dve, S["g_dv"])
                for u in range(NU_EXACT + 2):
                    if u < NU_EXACT:
                        dve.wait_ge(S["g_sc"], u + 1)
                        dve.tensor_reduce(nmax[:, u:u + 1], sc[:, u % 2], AX, ALU.max, negate=True)\
                           .then_inc(S["g_max"], 1)
                    if 0 < u <= NU_EXACT:
                        x = u - 1
                        dve.wait_ge(S["g_exp"], x + 1)
                        here(dve.reciprocal(tot[:, x:x + 1], tot[:, x:x + 1]))
                        dve.tensor_scalar(pr[:, x % 2], pr[:, x % 2], tot[:, x:x + 1], 1.0 / NP, ALU.mult,
                                          ALU.mult).then_inc(S["g_norm"], 1)
                    if u >= 2:
                        dve.wait_ge(S["g_tr"], u - 1)
                        wait(dve, S["g_pv"], u - 3)
                        dve.tensor_copy(pt[:, u % 2, 0:4], tr[:, 0:4]).then_inc(S["g_ev_dve"], 1)
                dve.wait_ge(S["g_pv"], NU_EXACT)
                here(dve.tensor_copy(r_t[:], accq))
            with dve.Else():
                dve.nop()
            dve.sem_inc(S["accE"], 1)
            dve.wait_ge(S["rT"], 1)
            for m in range(QT):
                last = dve.tensor_copy(r_nat[:, m], tr[:, 4 * m:4 * m + 4].rearrange("p a b -> p (a b)"))
            last.then_inc(S["rE"], 1)
            dve.wait_ge(S["gmm"], 1)
            for m in range(QT):
                link(dve.tensor_tensor(gate[:, 0, m * D:(m + 1) * D], sc[:, 0, m * D:(m + 1) * D], row_bias[:, 3],
                                       ALU.add))
            dve.sem_inc(S["z"], 1)
            g = gate[:, 1].rearrange("p (m c) -> p m c", m=QT)
            dve.wait_ge(S["ez"], 1)
            link(dve.tensor_scalar(g, g, 1.0, None, ALU.add))
            link(dve.reciprocal(g, g))
            link(dve.tensor_tensor(r_nat[:], r_nat[:], o_nat[:], ALU.subtract))
            link(dve.tensor_tensor(r_nat[:], r_nat[:], g, ALU.mult))
            link(dve.tensor_tensor(r_nat[:], r_nat[:], o_nat[:], ALU.add))
            link(dve.tensor_tensor(xres[:], xres[:], r_nat[:], ALU.add))

        @block.tensor
        def _(pe):
            pe.wait_ge(S["wr_in"], 48)
            for n in range(32):
                state, k = n // 16, (n % 16) // 2
                if n % 16 == 0:
                    pe.wait_ge(S["past_in"], 16 * (state + 1))
                wait(pe, S["pev_dve"] if n % 2 else S["pev_act"], n // 2 - 1)
                for c in range(CT):
                    if n % 2:
                        lhs, rhs = past[:, c, k * P:(k + 1) * P], wrv[:, c]
                    else:
                        lhs, rhs = wrk[:, c, (k % CT) * P:(k % CT + 1) * P], past[:, c, (k // CT) * D:(k // CT + 1) * D]
                    last = pe.matmul(slots[n % 4], lhs, rhs, start=c == 0, stop=c == CT - 1)
                last.then_inc(S["pmm"], 1)
            pe.wait_ge(norm.ready, QT)
            transpose_tokens(pe, tr[:].rearrange("p a b -> p (a b)").rearrange("p (t q) -> p t q", q=SQ), h, ident)\
                .then_inc(S["hT"], 1)
            pe.wait_ge(w_ready, 64)
            pe.wait_ge(S["hE"], 1)
            pe.wait_ge(S["pev_dve"], 16)
            pe.wait_ge(S["pev_act"], 16)

            def project_t(dst, w, src):
                for mt in range(CT):
                    for c in range(CT):
                        last = pe.matmul(dst[:, mt * SQ:(mt + 1) * SQ], w[:, c, mt * P:(mt + 1) * P], src[:, c],
                                         start=c == 0, stop=c == CT - 1)
                return last

            def project(dst, w, src):
                for m in range(QT):
                    for c in range(CT):
                        last = pe.matmul(dst[:, m * D:(m + 1) * D], src[:, c, m * P:(m + 1) * P], w[:, c],
                                         start=c == 0, stop=c == CT - 1)
                return last

            trf = tr[:].rearrange("p a b -> p (a b)")
            project_t(sc[:, 0], weights["q"], ht).then_inc(S["q"], 1)
            project_t(sc[:, 1], weights["k"], ht).then_inc(S["k"], 1)
            project(trf, weights["v"], ht).then_inc(S["v"], 1)
            pe.wait_ge(S["qE"], 1)
            pe.wait_ge(S["kE"], 1)
            pe.wait_ge(S["vE"], 1)

            def fill(n, keys, pair, tiles):
                wait(pe, S["read"], n - 1)
                for k in range(2):
                    last = pe.matmul(sc[:, n % 2, k * D:(k + 1) * D],
                                     keys[:, pair // 2, tiles[k] * P:(tiles[k] + 1) * P],
                                     qpad[:, pair // 2, 2 * (pair % 2):2 * (pair % 2) + 2], start=True, stop=True)
                last.then_inc(S["filled"], 1)

            def attend(units, keys, values):
                for u in range(units.start, units.stop + 2):
                    if u < units.stop:
                        pair, _, tiles, _, _ = all_units[u]
                        fill(filling(u), keys, pair, tiles)
                    if u < units.start + 2:
                        continue
                    x = u - 2
                    pair, _, tiles, c, count = all_units[x]
                    g = group(x)
                    pe.wait_ge(S["exp"], x + 1)
                    if c == 0:
                        wait(pe, S["acc_free"], g - 1)
                    for k in range(2):
                        for hh in range(2):
                            head = 2 * pair + hh
                            for n, lhs in enumerate((values[:, tiles[k], head * HD:(head + 1) * HD], ones[:, 0:HD])):
                                at = 64 * hh + HD * n
                                last = pe.matmul(acc[at:at + HD, g % 2, 0:SQ], lhs,
                                                 ex[:, x % 3, k * D + hh * SQ:k * D + (hh + 1) * SQ],
                                                 start=c == 0 and k == 0, stop=c == count - 1 and k == 1,
                                                 skip_group_check=True, tile_position=(0, at))
                    last.then_inc(S["pv"], 1)

            for n, at, pair, state in probes():
                if n < PAIRS:
                    fill(at, kt, pair, (0, 1))
            attend(SELF, kt, v)
            pe.wait_ge(S["accE"], 1)
            project(sc[:, 0], weights["o"], ct).then_inc(S["o"], 1)
            project_t(sc[:, 1], weights["o"], ct).then_inc(S["oT"], 1)
            pe.wait_ge(S["oTE"], 1)
            project_t(trf, wrq, o_t).then_inc(S["rq"], 1)
            pe.wait_ge(S["rqE"], 1)
            pe.wait_ge(S["oE"], 1)

            for n, at, pair, state in probes():
                if n >= PAIRS:
                    fill(at, rk, pair, (2 * UP * state, 2 * UP * state + 1))
            attend(PAST, rk, rv)
            pe.wait_ge(S["okrow"], 4)
            pe.matmul(tr[0:1, 0, 0:1], few[:, 1:2], ones[:, 0:1], start=True, stop=True).then_inc(S["oksum"], 1)
            pe.wait_ge(S["flag"], 1)
            general = pe.value_load(flag[0:1, 0:1], min_val=0, max_val=1)
            with pe.If(general):
                for u in range(NU_EXACT + 2):
                    if u < NU_EXACT:
                        head, m, state = u // (QT * NP), u // NP % QT, u % NP
                        wait(pe, S["g_exp"], u - 1)
                        for n in range(SP_ // D):
                            at = state * SP_ + n * D
                            last = pe.matmul(sc[:, u % 2, n * D:(n + 1) * D],
                                             qpad[:, head // HG, head % HG, m * P:(m + 1) * P],
                                             rk[:, head // HG, at:at + D], start=True, stop=True)
                        last.then_inc(S["g_sc"], 1)
                    if 0 < u <= NU_EXACT:
                        pe.wait_ge(S["g_norm"], u)
                        wait(pe, S["g_ev_dve"], u - 1)
                        wait(pe, S["g_ev_act"], u - 1)
                        for b in range(8):
                            last = pe.transpose(tr[:, b], pr[:, (u - 1) % 2, b * P:(b + 1) * P], ident[:])
                        last.then_inc(S["g_tr"], 1)
                    if u >= 2:
                        x = u - 2
                        head, m, state = x // (QT * NP), x // NP % QT, x % NP
                        t, j = head // HG, head % HG
                        pe.wait_ge(S["g_ev_dve"], x + 1)
                        pe.wait_ge(S["g_ev_act"], x + 1)
                        for k in range(8):
                            last = pe.matmul(accq[HD * j:HD * (j + 1), t, m * P:(m + 1) * P],
                                             rv[:, 8 * state + k, head * HD:(head + 1) * HD], pt[:, x % 2, k],
                                             start=state == 0 and k == 0, stop=state == NP - 1 and k == 7,
                                             skip_group_check=True, tile_position=(0, HD * j))
                        last.then_inc(S["g_pv"], 1)
            with pe.Else():
                pe.nop()
            pe.wait_ge(S["accE"], 2)
            for m in range(QT):
                for t in range(CT):
                    last = pe.transpose(tr[:, 4 * m + t], r_t[:, t, m * P:(m + 1) * P], ident[:])
            last.then_inc(S["rT"], 1)
            pe.wait_ge(S["wg_in"], 32)
            for m in range(QT):
                for c in range(2 * CT):
                    src = (o_t if c < CT else r_t)[:, c % CT, m * P:(m + 1) * P]
                    last = pe.matmul(sc[:, 0, m * D:(m + 1) * D], src, wg[:, c % CT, (c // CT) * D:(c // CT + 1) * D],
                                     start=c == 0, stop=c == 2 * CT - 1)
            last.then_inc(S["gmm"], 1)


def experts(nc, mem, sem, a, ident, ones, xres, out):
    MORE = (2 * SQ - NE) // P
    w1 = mem.sb("w1", [P, 2, CT, FF])
    w2 = mem.sb("w2", [P, 2, FT, D])
    h = mem.sb("c_h", [P, QT, D])
    ht = mem.sb("c_ht", [P, CT, SQ])
    gw = mem.sb("gw", [P, CT, NE])
    b1 = mem.sb("b1", [P, NE, FT])
    b2 = mem.sb("b2", [NE, D])
    iota = mem.sb("iota", [P, NE])
    prob = mem.sb("prob", [P, QT, NE])
    share = mem.sb("share", [P, QT, NE])
    share_t = mem.sb("share_t", [NE, SQ])
    best = mem.sb("best", [P, QT, 8])
    which = mem.sb("which", [P, QT, 8], U32)
    whichf = mem.sb("whichf", [P, QT, 8])
    pick = mem.sb("pick", [P, NE])
    one = mem.sb("one", [P, QT, 4])
    hid = mem.sb("hid", [P, 2, FT, P])
    count_to = mem.sb("count_to", [P, P])
    row_no = mem.sb("row_no", [P, 1])
    before = mem.sb("before", [P, P])
    chosen = mem.sb("chosen", [P, QT, NE])
    place = mem.sb("place", [P, QT, NE])
    place2 = mem.sb("place2", [P, QT, NE])
    over = mem.sb("over", [NE, 2])
    second = mem.sb("second", [NE, MORE])
    extra = mem.sb("extra", [1, 2 * MORE], I32)
    ident_r = mem.sb("c_ident_r", [P, P], F32R)
    h_hi = mem.sb("h_hi", [P, QT, D], F32R)
    h_lo = mem.sb("h_lo", [P, QT, D], F32R)
    to_place = mem.sb("to_place", [P, 2, QT, P], F32R)
    from_place = mem.sb("from_place", [P, 2, SQ], F32R)
    mine = mem.sb("mine", [P, 2, CT, P])
    y_hi = mem.sb("y_hi", [P, D], F32R)
    y_lo = mem.sb("y_lo", [P, D], F32R)
    total = mem.sb("total", [P, QT, D])
    up = mem.ps("up", [P, 2, 4 * P])
    mine_ps = mem.ps("mine_ps", [P, CT * P])
    back_ps = mem.ps("back_ps", [P, D])
    down = mem.ps("down", [P, 2, D])
    small = mem.ps("c_small", [P, D])
    y = mem.ps("c_y", [P, D])

    norm = Norm("cnorm", mem, sem, xres, h)
    S = {n: sem("c_" + n) for n in (
        "gate_in", "b_in", "iota", "dv", "hT", "hE", "logit", "nmax", "p", "share", "chosen", "counted", "over",
        "extra", "split", "sel", "gathered", "mine", "back", "y", "y_hi", "y_lo", "scattered", "shT", "shE",
        "b2", "up", "gelu", "down", "added", "out", "done")}
    w1_in = [sem(f"w1_in{b}") for b in range(2)]
    w2_in = [sem(f"w2_in{b}") for b in range(2)]
    w1v = a["w1"].rearrange("e (t p) f -> e p t f", p=P)
    w2v = a["w2"].rearrange("e (t p) f -> e p t f", p=P)
    PAIRS = NE // 2
    C_SHARE = 64
    C_PLACE = C_SHARE + SQ
    C_EXTRA = 2

    def second_jobs(eng):
        eng.wait_ge(S["extra"], 1)
        for n in range(MORE):
            yield (NE + n, n % 2, eng.value_load(extra[0:1, n:n + 1], min_val=0, max_val=NE - 1),
                   eng.value_load(extra[0:1, MORE + n:MORE + n + 1], min_val=0, max_val=1))

    def last_pair(i):
        return isinstance(i, int) and i == PAIRS - 1

    with nc.Block() as block:
        @block.sync
        def _(sp):
            sp.dma_start(gw[:], a["gate_t"].rearrange("(t p) e -> p t e", p=P)).then_inc(S["gate_in"], 16)
            for b in range(2):
                sp.dma_start(w1[:, b], w1v[b]).then_inc(w1_in[b], 16)
                sp.dma_start(w2[:, b], w2v[b]).then_inc(w2_in[b], 16)
            sp.dma_start(b1[:], a["b1_c"]).then_inc(S["b_in"], 16)
            sp.dma_start(b2[:], a["b2"]).then_inc(S["b_in"], 16)

            def load(job, e, b):
                sp.wait_ge(S["up"], 2 * (job - 1))
                sp.dma_start(w1[:, b], w1v[e]).then_inc(w1_in[b], 16)
                sp.wait_ge(S["y"], job - 1)
                sp.dma_start(w2[:, b], w2v[e]).then_inc(w2_in[b], 16)

            with sp.Fori(1, PAIRS) as i:
                for b in range(2):
                    load(2 * i + b, 2 * i + b, b)
            for job, b, e, wanted in second_jobs(sp):
                with sp.If(wanted):
                    load(job, e, b)
                with sp.Else():
                    sp.nop()
            sp.wait_ge(S["out"], 1)
            sp.dma_start(out.rearrange("(t p) c -> p t c", p=P), total[:]).then_inc(S["done"], 16)
            sp.wait_ge(S["done"], 16)

        @block.gpsimd
        def _(pool):
            pool.iota(iota[:], [[1, NE]], base=0, channel_multiplier=0,
                      allow_small_or_imprecise_dtypes=True).then_inc(S["iota"], 1)
            pool.iota(count_to[:], [[1, P]], base=0, channel_multiplier=0,
                      allow_small_or_imprecise_dtypes=True).then_inc(S["iota"], 1)
            pool.iota(row_no[:], [[0, 1]], base=0, channel_multiplier=1,
                      allow_small_or_imprecise_dtypes=True).then_inc(S["iota"], 1)

        @block.scalar
        def _(act):
            norm.scalar(act)
            for m in range(QT):
                act.wait_ge(S["nmax"], QT)
                act.activation(prob[:, m], small[:, m * NE:(m + 1) * NE], ACT.Exp, bias=one[:, m, 0:1],
                               accum_out=one[:, m, 1:2]).then_inc(S["p"], 1)
            act.wait_ge(S["b_in"], 32)

            def own_tokens(e, b):
                act.wait_ge(S["gathered"], e + 1)
                wait(act, S["up"], 2 * (e - 1))
                act.activation(mine[:, b], mine_ps[:].rearrange("p (c k) -> p c k", k=P), ACT.Copy)\
                   .then_inc(S["mine"], 1)

            def job(n, e, b):
                for s in range(2):
                    act.wait_ge(S["up"], 2 * n + s + 1)
                    wait(act, S["y"], n - 1)
                    for f in range(4):
                        last = act.activation(hid[:, b, 4 * s + f], up[:, s, f * P:(f + 1) * P], ACT.Gelu,
                                              bias=b1[:, bass.ds(e, 1), 4 * s + f])
                    last.then_inc(S["gelu"], 1)

            def result(n):
                act.wait_ge(S["y"], n + 1)
                act.activation(y_hi[:], y[:], ACT.Copy).then_inc(S["y_hi"], 1)

            def pair(i):
                for b in range(2):
                    e = 2 * i + b
                    job(e, e, b)
                    if not last_pair(i) or b == 0:
                        own_tokens(e + 1, 1 - b)
                    result(e)

            own_tokens(0, 0)
            pair(0)
            with act.Fori(1, PAIRS - 1) as i:
                pair(i)
            pair(PAIRS - 1)
            for n, b, e, wanted in second_jobs(act):
                with act.If(wanted):
                    own_tokens(n, b)
                    job(n, e, b)
                    result(n)
                with act.Else():
                    act.nop()

        @block.vector
        def _(dve):
            link = Chain(dve, S["dv"])
            norm.vector(dve, link)
            dve.wait_ge(S["hT"], 1)
            dve.tensor_copy(ht[:], down[:].rearrange("p m (t q) -> p (m t) q", q=SQ)).then_inc(S["hE"], 1)
            dve.wait_ge(S["logit"], 1)
            for m in range(QT):
                dve.tensor_reduce(one[:, m, 0:1], small[:, m * NE:(m + 1) * NE], AX, ALU.max,
                                  negate=True).then_inc(S["nmax"], 1)
            link(dve.tensor_copy(ident_r[:], ident[:]))
            link(dve.tensor_copy(h_hi[:], h[:]))
            link(dve.tensor_tensor(h_lo[:], h[:], h_hi[:].bitcast(F32), ALU.subtract))
            dve.wait_ge(S["iota"], 3)
            link(dve.tensor_scalar(before[:], count_to[:], row_no[:, 0:1], None, ALU.is_gt))
            dve.sem_inc(S["split"], 1)
            for m in range(QT):
                dve.wait_ge(S["p"], m + 1)
                link(dve.reciprocal(one[:, m, 2:3], one[:, m, 1:2]))
                link(dve.tensor_scalar(prob[:, m], prob[:, m], one[:, m, 2:3], None, ALU.mult))
                link(dve.max(best[:, m], prob[:, m]))
                link(dve.max_index(which[:, m], best[:, m], prob[:, m]))
                link(dve.tensor_copy(whichf[:, m], which[:, m]))
                link(dve.tensor_tensor(one[:, m, 3:4], best[:, m, 0:1], best[:, m, 1:2], ALU.add))
                link(dve.tensor_scalar(one[:, m, 3:4], one[:, m, 3:4], 1e-10, None, ALU.max))
                link(dve.reciprocal(one[:, m, 3:4], one[:, m, 3:4]))
                link(dve.tensor_scalar(best[:, m], best[:, m], one[:, m, 3:4], None, ALU.mult))
                link(dve.tensor_scalar(share[:, m], iota[:], whichf[:, m, 0:1], best[:, m, 0:1],
                                       ALU.is_equal, ALU.mult))
                link(dve.tensor_scalar(pick[:], iota[:], whichf[:, m, 1:2], best[:, m, 1:2],
                                       ALU.is_equal, ALU.mult))
                link(dve.tensor_tensor(share[:, m], share[:, m], pick[:], ALU.add))
                link(dve.tensor_scalar(chosen[:, m], iota[:], whichf[:, m, 0:1], None, ALU.is_equal))
                link(dve.tensor_scalar(pick[:], iota[:], whichf[:, m, 1:2], None, ALU.is_equal))
                link(dve.tensor_tensor(chosen[:, m], chosen[:, m], pick[:], ALU.add))
            dve.sem_inc(S["share"], 1)
            dve.wait_ge(S["shT"], 1)
            dve.tensor_copy(share_t[:], small[0:NE, C_SHARE:C_SHARE + SQ]).then_inc(S["shE"], 1)
            dve.wait_ge(S["counted"], 1)
            over_jobs = Chain(dve, S["over"])
            over_jobs(dve.tensor_scalar(over[:, 0:1], y[0:NE, 0:1], P + 0.5, None, ALU.is_gt))
            for m in range(QT):
                link(dve.tensor_scalar(place[:, m], chosen[:, m], -2.0 * SQ, 2.0 * SQ, ALU.mult, ALU.add))
                link(dve.tensor_tensor(place[:, m], place[:, m], small[:, C_PLACE + m * NE:C_PLACE + (m + 1) * NE],
                                       ALU.add))
                link(dve.tensor_scalar(place2[:, m], place[:, m], -float(P), None, ALU.add))
            dve.wait_ge(S["counted"], 2)
            over_jobs(dve.tensor_copy(over[:, 1:2], y[0:NE, 1:2]))
            dve.tensor_scalar(second[:], count_to[0:NE, 0:MORE], over[:, 1:2], over[:, 0:1], ALU.is_equal,
                              ALU.mult).then_inc(S["over"], 1)
            dve.wait_ge(S["counted"], 3)
            dve.tensor_copy(extra[:], y[0:1, C_EXTRA:C_EXTRA + 2 * MORE]).then_inc(S["extra"], 1)
            dve.wait_ge(S["b2"], 1)
            for m in range(QT):
                dve.tensor_tensor(total[:, m], h[:, m], down[:, m], ALU.add).then_inc(S["added"], 1)

            def select(n, e, b, place=place):
                wait(dve, S["gathered"], n - 1)
                for m in range(QT):
                    last = dve.tensor_scalar(to_place[:, b, m], count_to[:], place[:, m, bass.ds(e, 1)], None,
                                             ALU.is_equal)
                last.then_inc(S["sel"], 1)

            def back(e, b):
                dve.wait_ge(S["gathered"], e + 1)
                wait(dve, S["scattered"], e - 1)
                dve.tensor_copy(from_place[:, b], back_ps[:, 0:SQ]).then_inc(S["back"], 1)

            def add(n, e):
                dve.wait_ge(S["scattered"], n + 1)
                dve.wait_ge(S["added"], QT * (n + 1))
                for m in range(QT):
                    dve.scalar_tensor_tensor(total[:, m], down[:, m], share[:, m, bass.ds(e, 1)], total[:, m],
                                             ALU.mult, ALU.add).then_inc(S["added"], 1)

            def result(n):
                dve.wait_ge(S["y_hi"], n + 1)
                dve.tensor_tensor(y_lo[:], y[:], y_hi[:].bitcast(F32), ALU.subtract).then_inc(S["y_lo"], 1)

            def pair(i):
                for b in range(2):
                    e = 2 * i + b
                    if not last_pair(i) or b == 0:
                        select(e + 1, e + 1, 1 - b)
                        back(e + 1, 1 - b)
                    if not (isinstance(e, int) and e == 0):
                        add(e - 1, e - 1)
                    result(e)

            select(0, 0, 0)
            back(0, 0)
            pair(0)
            with dve.Fori(1, PAIRS - 1) as i:
                pair(i)
            pair(PAIRS - 1)
            add(NE - 1, NE - 1)
            dve.wait_ge(S["added"], QT * (NE + 1))
            for n, b, e, wanted in second_jobs(dve):
                with dve.If(wanted):
                    select(n, e, b, place2)
                    back(n, b)
                    result(n)
                    add(n, e)
                    dve.wait_ge(S["added"], QT * (n + 2))
                with dve.Else():
                    dve.nop()
            link(dve.tensor_scalar(total[:], total[:], -100.0, 100.0, ALU.max, ALU.min))
            dve.tensor_tensor(total[:], total[:], xres[:], ALU.add).then_inc(S["out"], 1)

        @block.tensor
        def _(pe):
            pe.wait_ge(norm.ready, QT)
            transpose_tokens(pe, down[:].rearrange("p m (t q) -> p (m t) q", q=SQ), h, ident).then_inc(S["hT"], 1)
            pe.wait_ge(S["gate_in"], 16)
            pe.wait_ge(S["hE"], 1)
            for m in range(QT):
                for c in range(CT):
                    last = pe.matmul(small[:, m * NE:(m + 1) * NE], ht[:, c, m * P:(m + 1) * P], gw[:, c],
                                     start=c == 0, stop=c == CT - 1)
            last.then_inc(S["logit"], 1)
            pe.wait_ge(S["share"], 1)
            for m in range(QT):
                last = pe.transpose(small[0:NE, C_SHARE + m * P:C_SHARE + (m + 1) * P], share[:, m], ident[:])
            last.then_inc(S["shT"], 1)
            pe.wait_ge(S["split"], 1)
            pe.wait_ge(S["shE"], 1)
            for m in range(QT):
                at = C_PLACE + m * NE
                last = pe.matmul(small[:, at:at + NE], before[:], chosen[:, m], start=True, stop=m == 0)
                if m:
                    pe.matmul(small[:, at:at + NE], ones[:], chosen[:, 0], start=False, stop=True)
            for m in range(QT):
                last = pe.matmul(y[0:NE, 0:1], chosen[:, m], ones[:, 0:1], start=m == 0,
                                 stop=m == QT - 1)
            last.then_inc(S["counted"], 1)
            pe.wait_ge(S["over"], 1)
            pe.matmul(y[0:NE, 1:2], before[0:NE, 0:NE], over[:, 0:1], start=True, stop=True)\
              .then_inc(S["counted"], 1)
            pe.wait_ge(S["over"], 3)
            for n, lhs in enumerate((row_no, ones)):
                last = pe.matmul(y[0:1, C_EXTRA + n * MORE:C_EXTRA + (n + 1) * MORE], lhs[0:NE, 0:1], second[:],
                                 start=True, stop=True)
            last.then_inc(S["counted"], 1)
            pe.wait_ge(S["b_in"], 32)
            pe.wait_ge(S["shE"], 1)
            for m in range(QT):
                last = pe.matmul(down[:, m], share_t[:, m * P:(m + 1) * P], b2[:], start=True, stop=True)
            last.then_inc(S["b2"], 1)


            def gather(e, b):
                pe.wait_ge(S["sel"], e + 1)
                wait(pe, S["mine"], e)
                wait(pe, S["back"], e)
                for c in range(CT):
                    for m in range(QT):
                        for part in (h_hi, h_lo):
                            pe.matmul(mine_ps[:, c * P:(c + 1) * P], part[:, m, c * P:(c + 1) * P], to_place[:, b, m],
                                      start=m == 0 and part is h_hi, stop=m == QT - 1 and part is h_lo)
                for m in range(QT):
                    last = pe.matmul(back_ps[:, m * P:(m + 1) * P], to_place[:, b, m], ident_r[:],
                                     start=True, stop=True)
                last.then_inc(S["gathered"], 1)

            def scatter(e, b):
                pe.wait_ge(S["y_lo"], e + 1)
                pe.wait_ge(S["back"], e + 1)
                pe.wait_ge(S["added"], QT * (e + 1))
                for m in range(QT):
                    for part in (y_hi, y_lo):
                        last = pe.matmul(down[:, m], from_place[:, b, m * P:(m + 1) * P], part[:],
                                         start=part is y_hi, stop=part is y_lo)
                last.then_inc(S["scattered"], 1)

            def first_product(n, b, seen):
                pe.wait_ge(w1_in[b], seen)
                pe.wait_ge(S["mine"], n + 1)
                for s in range(2):
                    wait(pe, S["gelu"], 2 * n + s - 1)
                    for f in range(4):
                        for c in range(CT):
                            last = pe.matmul(up[:, s, f * P:(f + 1) * P],
                                             w1[:, b, c, (4 * s + f) * P:(4 * s + f + 1) * P],
                                             mine[:, b, c], start=c == 0, stop=c == CT - 1)
                    last.then_inc(S["up"], 1)

            def second_product(n, b, seen):
                pe.wait_ge(w2_in[b], seen)
                pe.wait_ge(S["gelu"], 2 * n + 2)
                for f in range(FT):
                    last = pe.matmul(y[:], hid[:, b, f], w2[:, b, f], start=f == 0, stop=f == FT - 1)
                last.then_inc(S["y"], 1)

            def pair(i):
                for b in range(2):
                    e = 2 * i + b
                    first_product(e, b, 16 * (i + 1))
                    if not last_pair(i) or b == 0:
                        gather(e + 1, 1 - b)
                    if not (isinstance(e, int) and e == 0):
                        scatter(e - 1, 1 - b)
                    second_product(e, b, 16 * (i + 1))

            gather(0, 0)
            pair(0)
            with pe.Fori(1, PAIRS - 1) as i:
                pair(i)
            pair(PAIRS - 1)
            scatter(NE - 1, 1)
            for n, b, e, wanted in second_jobs(pe):
                with pe.If(wanted):
                    gather(n, b)
                    first_product(n, b, 16 * (n // 2 + 1))
                    second_product(n, b, 16 * (n // 2 + 1))
                    scatter(n, b)
                with pe.Else():
                    pe.nop()


INPUTS = {"x": [SQ, D], "ctx": [SK, D], "mask_t": [SK, SQ], "bd_wq_t": [P, P], "bd_wk": [P, HG, STACK],
          "bd_wv_t": [P, P], "x_wo_t": [D, D], "x_bo": [D], "wq": [D, D], "wk": [D, D], "wv": [D, D], "wo": [D, D],
          "past_t": [NP, D, SP_], "wrk": [D, D], "wrv": [D, D], "wrq": [D, D], "wg": [2 * D, D],
          "brk_c": [P, CT], "brq_c": [P, CT], "bq_c": [P, CT], "bk_c": [P, CT], "bo_c": [P, CT],
          "brv": [D], "bv": [D], "bo": [D], "bg": [D],
          "gate_t": [D, NE], "w1": [NE, D, FF], "w2": [NE, FF, D], "b1_c": [P, NE, FT], "b2": [NE, D]}


def kernel(**inputs):
    import concourse.bacc as bacc
    from concourse.bass_utils import run_bass_kernel_spmd

    given = {k: np.asarray(v) for k, v in inputs.items()}

    def blocks(w):
        m = np.zeros((P, P), w.dtype)
        for j in range(HG):
            m[HD * j:HD * (j + 1), HD * j:HD * (j + 1)] = w
        return m

    arrays = {
        "x": given["x"][0], "ctx": given["ctx_1024"][0], "mask_t": given["mask_Bx1xSxS2_ik1"][0, 0].T,
        "bd_wq_t": blocks(given["L0_xattn_Wq"].T), "bd_wv_t": blocks(given["L0_xattn_Wv"].T),
        "bd_wk": np.concatenate([blocks(given["L0_xattn_Wk"]).reshape(P, HG, HD)] * 3, axis=2),
        "x_wo_t": given["L0_xattn_Wo"].T, "x_bo": given["L0_xattn_bo"],
        "past_t": given["L0_attn_past_states"][:, 0, :SP_].transpose(0, 2, 1),
        "gate_t": given["L0_ffn_gate_w"].T, "w1": given["L0_ffn_w1"], "w2": given["L0_ffn_w2"],
        "b1_c": given["L0_ffn_b1"].reshape(NE, FT, P).transpose(2, 0, 1), "b2": given["L0_ffn_b2"],
        "wq": given["L0_attn_Wq"], "wk": given["L0_attn_Wk"], "wv": given["L0_attn_Wv"], "wo": given["L0_attn_Wo"],
    }
    arrays |= {n.lower(): given["L0_attn_" + n] for n in ("Wrk", "Wrv", "Wrq", "Wg", "brv", "bv", "bo", "bg")}
    arrays |= {n + "_c": given["L0_attn_" + n].reshape(CT, P).T for n in ("brk", "brq", "bq", "bk", "bo")}
    arrays = {"in_" + k: np.ascontiguousarray(v) for k, v in arrays.items()}
    nc = bacc.Bacc("TRN2", target_bir_lowering=False, num_devices=1)
    aps = {}
    for name, shape in INPUTS.items():
        assert list(arrays["in_" + name].shape) == shape, name
        aps[name] = nc.dram_tensor("in_" + name, shape, mybir.dt.from_np(arrays["in_" + name].dtype), kind="ExternalInput").ap()
    out = nc.dram_tensor("out", [SQ, D], F32, kind="ExternalOutput").ap()
    build(nc, aps, out)
    result = run_bass_kernel_spmd(nc, [arrays], core_ids=[0])
    return result.results[0]["out"][None]
```

```python
from contextlib import ExitStack

import numpy as np

import concourse.bass as bass
from concourse import mybir

F32 = mybir.dt.float32
F32R = mybir.dt.float32r
I32 = mybir.dt.int32
U32 = mybir.dt.uint32
ALU = mybir.AluOpType
ACT = mybir.ActivationFunctionType
AX = mybir.AxisListType.X
AXY = mybir.AxisListType.XY
RMAX = bass.bass_isa.ReduceOp.max

P = 128
SQ = 256
D = 512
NH = 16
HD = D // NH
SK = 25088
NT = SK // P
U = 4
TURNS = NT // U
CT = D // P
HG = NH // CT
QT = SQ // P
STACK = 3 * HD
KROWS = STACK + 1
NP = 2
SP_ = 1024
NE = 14
FF = 1024
FT = FF // P
SCALE = 1.0 / float(np.sqrt(np.float32(HD)))
EPS = 1e-5
MASKED = -1e20
HIDE = -1e30
DEN_MIN, DEN_MAX = 1e-25, 1e30


def wait(eng, sem, value):
    if not isinstance(value, int) or value > 0:
        eng.wait_ge(sem, value)


class Chain:

    def __init__(self, eng, sem):
        self.eng, self.sem, self.n = eng, sem, 0

    def __call__(self, ins):
        self.n += 1
        ins.then_inc(self.sem, 1)
        self.eng.wait_ge(self.sem, self.n)


def build(nc, a, out):
    with ExitStack() as ctx:
        def sem(name):
            return ctx.enter_context(nc.semaphore(name))

        keep = Buffers(nc, ctx)
        ident = keep.sb("ident", [P, P])
        ones = keep.sb("ones", [P, P])
        xres = keep.sb("xres", [P, QT, D])
        wr = keep.sb("wr", [P, 2 * CT, D])
        past = keep.sb("past", [P, CT, SP_])
        past_ready = sem("past_ready")
        with ExitStack() as mem:
            cross_attention(nc, Buffers(nc, mem), sem, a, ident, ones, xres, wr, past, past_ready)
        with ExitStack() as mem:
            self_attention(nc, Buffers(nc, mem), sem, a, ident, ones, xres, wr, past, past_ready)
        with ExitStack() as mem:
            experts(nc, Buffers(nc, mem), sem, a, ident, ones, xres, out)


class Buffers:
    def __init__(self, nc, mem):
        self.nc, self.mem = nc, mem

    def sb(self, name, shape, dt=F32):
        return self.mem.enter_context(self.nc.sbuf_tensor(name, shape, dt))

    def ps(self, name, shape, dt=F32):
        return self.mem.enter_context(self.nc.psum_tensor(name, shape, dt))


class Norm:

    def __init__(self, name, mem, sem, xres, out):
        self.x, self.out = xres, out
        self.stats = mem.sb(f"{name}_stats", [P, QT, 6])
        self.mv = mem.sb(f"{name}_mv", [P, QT, 2])
        self.ve = mem.sb(f"{name}_ve", [P, QT])
        self.std = mem.sb(f"{name}_std", [P, QT])
        self.inv = mem.sb(f"{name}_inv", [P, QT])
        self.tmp = mem.sb(f"{name}_tmp", [P, QT])
        self.var_ready, self.std_ready = sem(f"{name}_var_ready"), sem(f"{name}_std_ready")
        self.ready = sem(f"{name}_ready")

    def vector(self, dve, link):
        for t in range(QT):
            link(dve.bn_stats(self.stats[:, t, :], self.x[:, t, :]))
            link(dve.bn_aggr(self.mv[:, t, :], self.stats[:, t, :]))
        dve.tensor_scalar(self.ve[:], self.mv[:, :, 1], EPS, None, ALU.add).then_inc(self.var_ready, 1)
        dve.wait_ge(self.std_ready, 1)
        link(dve.reciprocal(self.inv[:], self.std[:]))
        link(dve.tensor_tensor(self.tmp[:], self.inv[:], self.inv[:], ALU.mult))
        link(dve.tensor_tensor(self.tmp[:], self.tmp[:], self.ve[:], ALU.mult))
        link(dve.tensor_scalar(self.tmp[:], self.tmp[:], -0.5, 1.5, ALU.mult, ALU.add))
        link(dve.tensor_tensor(self.inv[:], self.inv[:], self.tmp[:], ALU.mult))
        for t in range(QT):
            dve.tensor_scalar(self.out[:, t, :], self.x[:, t, :], self.mv[:, t, 0:1], self.inv[:, t:t + 1],
                              ALU.subtract, ALU.mult).then_inc(self.ready, 1)

    def scalar(self, act):
        act.wait_ge(self.var_ready, 1)
        act.activation(self.std[:], self.ve[:], ACT.Sqrt).then_inc(self.std_ready, 1)


def transpose_tokens(pe, dst, src, ident):
    for t in range(CT):
        for m in range(QT):
            last = pe.transpose(dst[:, t, m * P:(m + 1) * P], src[:, m, t * P:(t + 1) * P], ident[:])
    return last


def cross_attention(nc, mem, sem, a, ident, ones, xres, wr, past, past_ready):
    xn = mem.sb("xn", [P, QT, D])
    bd_q = mem.sb("bd_q", [P, P])
    bd_k = mem.sb("bd_k", [P, HG, STACK])
    bd_v = mem.sb("bd_v", [P, P])
    wo = mem.sb("x_wo", [P, CT, D])
    bo = mem.sb("x_bo", [P, D])
    tok = mem.sb("x_tok", [P, CT, SQ])
    tok2 = mem.sb("x_tok2", [P, CT, SQ])
    nat = mem.sb("nat", [P, U, D])
    msk = mem.sb("msk", [P, U, SQ], I32)
    steps_up = mem.sb("steps_up", [P, 2])
    steps_down = mem.sb("steps_down", [P, 2])
    bias = mem.sb("bias", [P, U])
    split = mem.sb("split", [P, 2, NH, 3, HD], F32R)
    ident_r = mem.sb("ident_r", [P, P], F32R)
    kst = mem.sb("kst", [KROWS, 2, NH, P], F32R)
    qst = mem.sb("qst", [KROWS, NH, SQ], F32R)
    probs = mem.sb("probs", [P, U, HG, SQ])
    den = mem.sb("den", [P, CT, HG, SQ])
    dsum = mem.sb("dsum", [P, CT, SQ])
    top = mem.sb("top", [P, CT, HG, SQ])
    tmp = mem.sb("x_tmp", [P, HG, SQ])
    mbias = mem.sb("mbias", [P, SQ])
    sums = mem.sb("sums", [P, 4])
    flag = mem.sb("flag", [1, 1], I32)
    sc = mem.ps("sc", [P, 2, HG, SQ])
    tr = mem.ps("tr", [P, HG, P])
    psum = mem.ps("psum", [P, SQ])
    acc = mem.ps("acc", [P, CT, SQ])

    norm = Norm("xnorm", mem, sem, xres, xn)
    S = {n: sem("x_" + n) for n in (
        "x_in", "small", "wo_in", "id0", "id", "ones", "dv", "tokT", "tokE", "q1", "q1E", "qr", "qs", "split",
        "hi", "tr", "ks_dve", "ks_act", "probe_sc", "probe_cp", "shift", "shift_in", "score", "exp", "pv",
        "den_dve", "bias", "steps", "zero", "den_sum", "okrow", "oksum", "flag", "norm", "vp", "vpE", "proj",
        "rows_set", "ident_r", "g_free", "g_row", "g_mask", "g_split", "g_tr", "g_ks", "g_sc", "g_arg", "g_exp",
        "g_pv", "g_max", "g_top", "g_fin", "g_dv", "g_zero", "g_den")}
    row_in = [sem(f"row_in{u}") for u in range(U)]
    mask_in = [sem(f"mask_in{u}") for u in range(U)]
    rows = a["ctx"].rearrange("(n p) c -> n p c", p=P)
    masks = a["mask_t"].rearrange("(n p) q -> n p q", p=P)

    def per_turn(body, eng):
        body(0)
        with eng.Fori(1, TURNS - 1) as i:
            body(i)
        body(TURNS - 1)

    def last_turn(i):
        return isinstance(i, int) and i == TURNS - 1

    with nc.Block() as block:
        @block.sync
        def _(sp):
            sp.dma_start(xres[:], a["x"].rearrange("(t p) c -> p t c", p=P)).then_inc(S["x_in"], 16)
            sp.dma_start(bd_q[:], a["bd_wq_t"]).then_inc(S["small"], 16)
            sp.dma_start(bd_k[:], a["bd_wk"]).then_inc(S["small"], 16)
            for u in range(U):
                sp.dma_start(nat[:, u, :], rows[u]).then_inc(row_in[u], 16)
                sp.dma_start(msk[:, u, :], masks[u]).then_inc(mask_in[u], 16)
            sp.dma_start(bd_v[:], a["bd_wv_t"]).then_inc(S["wo_in"], 16)
            sp.dma_start(wo[:], a["x_wo_t"].rearrange("(t p) o -> p t o", p=P)).then_inc(S["wo_in"], 16)
            sp.dma_start(bo[:], a["x_bo"].partition_broadcast(P)).then_inc(S["wo_in"], 16)
            with sp.Fori(1, TURNS) as i:
                for u in range(U):
                    sp.wait_ge(S["steps"], 2 * (U * (i - 1) + u + 2))
                    sp.dma_start(msk[:, u, :], masks[U * i + u]).then_inc(mask_in[u], 16)
                    sp.wait_ge(S["pv"], CT * (U * (i - 1) + u + 1))
                    sp.dma_start(nat[:, u, :], rows[U * i + u]).then_inc(row_in[u], 16)
            for n, name in enumerate(("wrk", "wrv")):
                sp.dma_start(wr[:, n * CT:(n + 1) * CT], a[name].rearrange("(t p) o -> p t o", p=P))\
                  .then_inc(past_ready, 16)
            sp.dma_start(past[:], a["past_t"][0].rearrange("(t p) k -> p t k", p=P)).then_inc(past_ready, 16)
            sp.wait_ge(S["flag"], 1)
            general = sp.value_load(flag[0:1, 0:1], min_val=0, max_val=1)
            with sp.If(general):
                for turn in range(2):
                    with sp.Fori(0, NT) as i:
                        sp.wait_ge(S["g_free"], NT * turn + i + 1)
                        sp.dma_start(nat[:, 0, :], rows[i]).then_inc(S["g_row"], 16)
                        sp.dma_start(msk[:, 0, :], masks[i]).then_inc(S["g_mask"], 16)
                sp.wait_ge(S["g_fin"], 1)
            with sp.Else():
                sp.nop()

        @block.gpsimd
        def _(pool):
            pool.memset(ident[:], 0.0).then_inc(S["id0"], 1)
            pool.wait_ge(S["id0"], 1)
            pool.affine_select(out=ident[:], in_=ident[:], compare_op=ALU.not_equal, fill=1.0, base=0,
                               pattern=[[-1, P]], channel_multiplier=1).then_inc(S["id"], 1)
            pool.memset(ones[:], 1.0).then_inc(S["ones"], 1)
            pool.wait_ge(S["probe_cp"], CT)
            pool.partition_all_reduce(den[:], probs[:], P, RMAX).then_inc(S["shift"], 1)
            pool.wait_ge(S["flag"], 1)
            general = pool.value_load(flag[0:1, 0:1], min_val=0, max_val=1)
            with pool.If(general):
                pool.wait_ge(S["g_max"], 1)
                pool.partition_all_reduce(den[:], top[:], P, RMAX).then_inc(S["g_top"], 1)
                pool.wait_ge(S["g_fin"], 1)
            with pool.Else():
                pool.nop()

        @block.scalar
        def _(act):
            norm.scalar(act)

            def evacuate(i, u, g, tile):
                m = CT * tile + g
                act.wait_ge(S["tr"], m + 1)
                wait(act, S["score"], m - 2 * CT + 1)
                act.activation(kst[0:STACK, (u + 1) % 2, HG * g:HG * (g + 1), :], tr[0:STACK],
                               ACT.Copy).then_inc(S["ks_act"], 1)

            for g in range(1, CT):
                evacuate(0, -1, g, 0)

            def body(i):
                for u in range(U):
                    tile = U * i + u
                    for g in range(CT):
                        n = CT * tile + g
                        if g and not (last_turn(i) and u == U - 1):
                            evacuate(i, u, g, tile + 1)
                        act.wait_ge(S["bias"], tile + 1)
                        act.wait_ge(S["score"], n + 1)
                        wait(act, S["pv"], n - CT + 1)
                        if g < 3:
                            wait(act, S["den_dve"], 3 * (tile - 1) + g + 2)
                        act.activation(probs[:, g], sc[:, g % 2], ACT.Exp,
                                       bias=bias[:, u:u + 1]).then_inc(S["exp"], 1)

            per_turn(body, act)
            act.wait_ge(S["flag"], 1)
            general = act.value_load(flag[0:1, 0:1], min_val=0, max_val=1)
            with act.If(general):
                with act.Fori(0, NT) as i:
                    for g in range(CT):
                        act.wait_ge(S["g_arg"], CT * i + g + 1)
                        act.activation(probs[:, 0], tmp[:], ACT.Exp).then_inc(S["g_exp"], 1)
                act.wait_ge(S["g_fin"], 1)
            with act.Else():
                act.nop()

        def general_vector(dve):
            link = Chain(dve, S["g_dv"])
            link(dve.memset(top[:], -3.0e38))
            link(dve.tensor_scalar(qst[STACK:KROWS].rearrange("p h q -> p (h q)"),
                                   ones[STACK:KROWS, 0:1].to_broadcast([1, NH * SQ]), 0.0, None, ALU.mult))
            dve.sem_inc(S["g_free"], 1)
            base = link.n
            for turn in range(2):
                if turn:
                    dve.sem_inc(S["g_max"], 1)
                    dve.wait_ge(S["g_top"], 1)
                    dve.tensor_copy(top[:], den[:]).then_inc(S["g_zero"], 1)
                    dve.wait_ge(S["g_zero"], 1)
                    dve.memset(den[:], 0.0).then_inc(S["g_zero"], 1)
                    dve.memset(acc[:], 0.0).then_inc(S["g_zero"], 1)
                steps = 3 + 2 * CT if turn == 0 else 3 + 3 * CT
                with dve.Fori(0, NT) as i:
                    seen = NT * turn + i
                    n = base + steps * i
                    dve.wait_ge(S["g_row"], 16 * (seen + 1))
                    dve.wait_ge(S["g_mask"], 16 * (seen + 1))
                    dve.tensor_copy(split[:, 0, :, 0:3:2, :],
                                    nat[:, 0, :].rearrange("p (h c) -> p h c", c=HD).unsqueeze(2)
                                    .to_broadcast([P, NH, 2, HD])).then_inc(S["g_dv"], 1)
                    dve.wait_ge(S["g_dv"], n + 1)
                    dve.tensor_tensor(split[:, 0, :, 1, :], nat[:, 0, :].rearrange("p (h c) -> p h c", c=HD),
                                      split[:, 0, :, 0, :].bitcast(F32), ALU.subtract).then_inc(S["g_dv"], 1)
                    dve.wait_ge(S["g_dv"], n + 2)
                    dve.tensor_scalar(mbias[:], msk[:, 0, :], 0, MASKED, ALU.is_equal, ALU.mult)\
                       .then_inc(S["g_dv"], 1)
                    dve.wait_ge(S["g_dv"], n + 3)
                    dve.sem_inc(S["g_split"], 1)
                    k = n + 3
                    for g in range(CT):
                        dve.wait_ge(S["g_tr"], CT * seen + g + 1)
                        dve.tensor_copy(kst[0:STACK, 0, HG * g:HG * (g + 1), :], tr[0:STACK])\
                           .then_inc(S["g_ks"], 1)
                        dve.wait_ge(S["g_sc"], CT * seen + g + 1)
                        if turn and g:
                            dve.wait_ge(S["g_exp"], CT * i + g)
                        dve.tensor_tensor(tmp[:], sc[:, 0], mbias[:].unsqueeze(1).to_broadcast([P, HG, SQ]),
                                          ALU.add).then_inc(S["g_dv"], 1)
                        dve.wait_ge(S["g_dv"], k + 1)
                        if turn == 0:
                            dve.tensor_tensor(top[:, g], top[:, g], tmp[:], ALU.max).then_inc(S["g_dv"], 1)
                            dve.wait_ge(S["g_dv"], k + 2)
                            k = k + 2
                        else:
                            dve.tensor_tensor(tmp[:], tmp[:], top[:, g], ALU.subtract).then_inc(S["g_dv"], 1)
                            dve.wait_ge(S["g_dv"], k + 2)
                            dve.sem_inc(S["g_arg"], 1)
                            dve.wait_ge(S["g_exp"], CT * i + g + 1)
                            dve.tensor_tensor(den[:, g], den[:, g], probs[:, 0], ALU.add).then_inc(S["g_dv"], 1)
                            dve.wait_ge(S["g_dv"], k + 3)
                            k = k + 3
                    if turn:
                        dve.wait_ge(S["g_pv"], CT * (i + 1))
                    dve.sem_inc(S["g_free"], 1)
                base = base + steps * NT
            dve.wait_ge(S["g_fin"], 1)
            dve.tensor_copy(dsum[:], sc[:, 0]).then_inc(S["g_zero"], 1)
            dve.wait_ge(S["g_zero"], 4)

        @block.vector
        def _(dve):
            link = Chain(dve, S["dv"])
            dve.memset(acc[:], 0.0).then_inc(S["zero"], 1)
            dve.memset(psum[:], 0.0).then_inc(S["zero"], 1)
            dve.wait_ge(S["x_in"], 16)
            norm.vector(dve, link)
            dve.wait_ge(S["tokT"], 1)
            dve.tensor_copy(tok[:], sc[:, 0]).then_inc(S["tokE"], 1)
            dve.wait_ge(S["q1"], 1)
            dve.tensor_copy(tok2[:], sc[:, 1]).then_inc(S["q1E"], 1)
            for t in range(CT):
                heads = slice(HG * t, HG * (t + 1))
                dve.wait_ge(S["qr"], t + 1)
                link(dve.tensor_scalar(qst[0:STACK, heads, :], sc[0:STACK, t % 2], SCALE, None, ALU.mult))
                dve.scalar_tensor_tensor(qst[2 * HD:STACK, heads, :], sc[2 * HD:STACK, t % 2], SCALE,
                                         qst[2 * HD:STACK, heads, :].bitcast(F32), ALU.mult,
                                         ALU.subtract).then_inc(S["qs"], 1)
            dve.wait_ge(S["ones"], 1)
            link(dve.tensor_copy(ident_r[:], ident[:]))
            dve.sem_inc(S["ident_r"], 1)
            for b in range(2):
                link(dve.tensor_copy(kst[STACK:KROWS, b].rearrange("p h k -> p (h k)"),
                                     ones[STACK:KROWS, 0:1].to_broadcast([1, NH * P])))
            link(dve.tensor_scalar(qst[STACK:KROWS].rearrange("p h q -> p (h q)"),
                                   ones[STACK:KROWS, 0:1].to_broadcast([1, NH * SQ]), 0.0, None, ALU.mult))
            dve.sem_inc(S["rows_set"], 1)

            def row_hi(u, b, seen):
                dve.wait_ge(row_in[u], seen)
                dve.tensor_copy(split[:, b, :, 0:3:2, :],
                                nat[:, u, :].rearrange("p (h c) -> p h c", c=HD).unsqueeze(2)
                                .to_broadcast([P, NH, 2, HD])).then_inc(S["hi"], 1)

            def row_lo(u, b, tile):
                dve.wait_ge(S["hi"], tile + 1)
                dve.tensor_tensor(split[:, b, :, 1, :], nat[:, u, :].rearrange("p (h c) -> p h c", c=HD),
                                  split[:, b, :, 0, :].bitcast(F32), ALU.subtract).then_inc(S["split"], 1)

            def evacuate(b, g, tile):
                m = CT * tile + g
                dve.wait_ge(S["tr"], m + 1)
                wait(dve, S["score"], m - 2 * CT + 1)
                dve.tensor_copy(kst[0:STACK, b, HG * g:HG * (g + 1), :], tr[0:STACK])\
                   .then_inc(S["ks_dve"], 1)

            def look_at_mask(u, tile, seen):
                now, then = u % 2, (u + 1) % 2
                dve.wait_ge(mask_in[u], seen)
                wait(dve, S["exp"], CT * (tile - U + 1))
                dve.wait_ge(S["steps"], 2 * tile + 2)
                dve.tensor_scalar(bias[:, u:u + 1], msk[:, u, 0:1], 0.0, HIDE, ALU.is_equal, ALU.mult)\
                   .then_inc(S["bias"], 1)
                dve.scalar_tensor_tensor(steps_up[:, now:now + 1], msk[:, u, SQ - 1:SQ], msk[:, u, 0:1],
                                         steps_up[:, then:then + 1], ALU.subtract, ALU.max).then_inc(S["steps"], 1)
                dve.tensor_tensor_reduce(out=mbias[:, 1:SQ], in0=msk[:, u, 0:SQ - 1], in1=msk[:, u, 1:SQ],
                                         scale=1.0, scalar=steps_down[:, then:then + 1], op0=ALU.subtract,
                                         op1=ALU.max, accum_out=steps_down[:, now:now + 1])\
                   .then_inc(S["steps"], 1)

            for tile in range(2):
                row_hi(tile, tile, 16)
                row_lo(tile, tile, tile)
            evacuate(0, 0, 0)
            for g in range(CT):
                dve.wait_ge(S["probe_sc"], g + 1)
                dve.tensor_copy(probs[:, g], sc[:, g % 2]).then_inc(S["probe_cp"], 1)
            dve.wait_ge(S["shift"], 1)
            link(dve.tensor_scalar(qst[STACK:KROWS].rearrange("p h q -> p (h q)"),
                                   den[STACK:KROWS].rearrange("p g h q -> p (g h q)"), -1.0, None, ALU.mult))
            dve.sem_inc(S["shift_in"], 1)
            dve.memset(den[:, 0:3], 0.0).then_inc(S["den_dve"], 1)
            dve.memset(steps_up[:], 0.0).then_inc(S["steps"], 1)
            dve.memset(steps_down[:], 0.0).then_inc(S["steps"], 1)
            for tile in range(2):
                look_at_mask(tile, tile, 16)

            def add(tile, g):
                dve.wait_ge(S["exp"], CT * tile + g + 1)
                dve.wait_ge(S["den_dve"], 3 * tile + g + 1)
                dve.tensor_tensor(den[:, g], den[:, g], probs[:, g], ALU.add).then_inc(S["den_dve"], 1)

            def body(i):
                for u in range(U):
                    tile = U * i + u
                    b2, seen2 = (u + 2) % U, 16 * (i + 1 + (u + 2) // U)
                    more1 = not (last_turn(i) and u >= U - 1)
                    more2 = not (last_turn(i) and u >= U - 2)
                    if more1:
                        evacuate((u + 1) % 2, 0, tile + 1)
                    if more2:
                        dve.wait_ge(S["tr"], CT * (tile + 1))
                        row_hi(b2, u % 2, seen2)
                    add(tile, 0)
                    if more2:
                        row_lo(b2, u % 2, tile + 2)
                    add(tile, 1)
                    if more2:
                        look_at_mask(b2, tile + 2, seen2)
                    add(tile, 2)

            per_turn(body, dve)
            dve.wait_ge(S["den_sum"], 1)
            dve.wait_ge(S["pv"], NT * CT)
            count = Chain(dve, S["okrow"])
            count(dve.tensor_copy(dsum[:, 0:3], sc[:, 0, 0:3]))
            count(dve.tensor_copy(dsum[:, 3], psum[:]))
            count(dve.tensor_tensor(sums[:, 0:1], steps_up[:, 1:2], steps_down[:, 1:2], ALU.max))
            count(dve.tensor_scalar(sums[:, 0:1], sums[:, 0:1], 0.0, None, ALU.is_gt))
            count(dve.tensor_scalar(tmp[:], dsum[:], DEN_MIN, None, ALU.is_ge))
            count(dve.scalar_tensor_tensor(tmp[:], dsum[:], DEN_MAX, tmp[:], ALU.is_le, ALU.mult))
            count(dve.tensor_reduce(sums[:, 1:2], tmp[:], AXY, ALU.min))
            count(dve.tensor_scalar(sums[:, 2:3], sums[:, 1:2], 1.0, None, ALU.is_lt))
            count(dve.tensor_tensor(sums[:, 3:4], sums[:, 0:1], sums[:, 2:3], ALU.add))
            dve.wait_ge(S["oksum"], 1)
            dve.tensor_scalar(flag[:], tr[0:1, 0, 0:1], 0.5, None, ALU.is_gt).then_inc(S["flag"], 1)
            dve.wait_ge(S["flag"], 1)
            general = dve.value_load(flag[0:1, 0:1], min_val=0, max_val=1)
            with dve.If(general):
                general_vector(dve)
            with dve.Else():
                dve.nop()
            tail = Chain(dve, S["norm"])
            tail(dve.reciprocal(tmp[:], dsum[:]))
            tail(dve.tensor_tensor(tok[:], acc[:], tmp[:], ALU.mult))
            dve.wait_ge(S["vp"], 1)
            dve.tensor_copy(tok2[:], sc[:, 1]).then_inc(S["vpE"], 1)
            dve.wait_ge(S["wo_in"], 48)
            dve.wait_ge(S["proj"], 1)
            for m in range(QT):
                tail(dve.tensor_tensor(xres[:, m, :], xres[:, m, :], bo[:], ALU.add))
                tail(dve.tensor_tensor(xres[:, m, :], xres[:, m, :],
                                       sc[:, 0].rearrange("p h q -> p (h q)")[:, m * D:(m + 1) * D], ALU.add))

        @block.tensor
        def _(pe):
            scf = sc[:].rearrange("p s h q -> p s (h q)")
            pe.wait_ge(S["id"], 1)
            pe.wait_ge(norm.ready, QT)
            transpose_tokens(pe, sc[:, 0], xn, ident).then_inc(S["tokT"], 1)
            pe.wait_ge(S["small"], 32)
            pe.wait_ge(S["tokE"], 1)
            for t in range(CT):
                last = pe.matmul(sc[:, 1, t], bd_q[:], tok[:, t], start=True, stop=True)
            last.then_inc(S["q1"], 1)
            pe.wait_ge(S["q1E"], 1)
            for t in range(CT):
                wait(pe, S["qs"], t - 1)
                for j in range(HG):
                    last = pe.matmul(sc[0:STACK, t % 2, j], bd_k[:, j], tok2[:, t], start=True, stop=True)
                last.then_inc(S["qr"], 1)

            def transposes(b, g, tile):
                pe.wait_ge(S["split"], tile + 1)
                if g == 1:
                    pe.wait_ge(S["ks_dve"], tile + 1)
                else:
                    wait(pe, S["ks_act"], 3 * tile + max(g - 1, 0))
                for j in range(HG):
                    last = pe.matmul(tr[0:STACK, j], split[:, b, HG * g + j].rearrange("p s c -> p (s c)"),
                                     ident_r[:], start=True, stop=True)
                last.then_inc(S["tr"], 1)

            def scores(b, g, tile, signal):
                if g == 0:
                    pe.wait_ge(S["ks_dve"], tile + 1)
                else:
                    pe.wait_ge(S["ks_act"], 3 * tile + g)
                for j in range(HG):
                    h = HG * g + j
                    last = pe.matmul(sc[:, g % 2, j], kst[:, b, h], qst[:, h], start=True, stop=True)
                last.then_inc(signal, 1)

            def weighted(u, g, signal, src):
                for j in range(HG):
                    last = pe.matmul(acc[HD * j:HD * (j + 1), g], nat[:, u, (HG * g + j) * HD:(HG * g + j + 1) * HD],
                                     src[:, j], start=False, stop=True, skip_group_check=True,
                                     tile_position=(0, HD * j))
                if signal is S["pv"] and g == 3:
                    for j in range(HG):
                        last = pe.matmul(psum[HD * j:HD * (j + 1)], ones[:, 0:HD], src[:, j], start=False,
                                         stop=True, skip_group_check=True, tile_position=(0, HD * j))
                last.then_inc(signal, 1)

            pe.wait_ge(S["ident_r"], 1)
            for g in range(CT):
                transposes(0, g, 0)
            pe.wait_ge(S["qs"], CT)
            pe.wait_ge(S["rows_set"], 1)
            for g in range(CT):
                wait(pe, S["probe_cp"], g - 1)
                scores(0, g, 0, S["probe_sc"])
            pe.wait_ge(S["probe_cp"], CT)
            pe.wait_ge(S["shift_in"], 1)
            pe.wait_ge(S["zero"], 2)

            def body(i):
                for u in range(U):
                    tile = U * i + u
                    for g in range(CT):
                        n = CT * tile + g
                        if not (last_turn(i) and u == U - 1):
                            transposes((u + 1) % 2, g, tile + 1)
                        wait(pe, S["exp"], n - 1)
                        scores(u % 2, g, tile, S["score"])
                        if not (isinstance(i, int) and n < 2):
                            weighted((u if g >= 2 else u - 1) % U, (g - 2) % CT, S["pv"], probs[:, (g - 2) % CT])

            per_turn(body, pe)
            for g in (2, 3):
                pe.wait_ge(S["exp"], NT * CT - 3 + g)
                weighted(U - 1, g, S["pv"], probs[:, g])
            pe.wait_ge(S["den_dve"], 3 * NT + 1)
            pe.wait_ge(S["exp"], NT * CT)

            def total(groups, signal):
                for g in groups:
                    for j in range(HG):
                        last = pe.matmul(sc[HD * j:HD * (j + 1), 0, g], ones[:, 0:HD], den[:, g, j],
                                         start=True, stop=True, tile_position=(0, HD * j))
                last.then_inc(signal, 1)

            total(range(3), S["den_sum"])
            pe.wait_ge(S["okrow"], 9)
            pe.matmul(tr[0:1, 0, 0:1], sums[:, 3:4], ones[:, 0:1], start=True, stop=True).then_inc(S["oksum"], 1)
            pe.wait_ge(S["flag"], 1)
            general = pe.value_load(flag[0:1, 0:1], min_val=0, max_val=1)
            with pe.If(general):
                for turn in range(2):
                    if turn:
                        pe.wait_ge(S["g_zero"], 3)
                    with pe.Fori(0, NT) as i:
                        seen = NT * turn + i
                        pe.wait_ge(S["g_split"], seen + 1)
                        for g in range(CT):
                            for j in range(HG):
                                last = pe.matmul(tr[0:STACK, j],
                                                 split[:, 0, HG * g + j].rearrange("p s c -> p (s c)"),
                                                 ident_r[:], start=True, stop=True)
                            last.then_inc(S["g_tr"], 1)
                            pe.wait_ge(S["g_ks"], CT * seen + g + 1)
                            for j in range(HG):
                                h = HG * g + j
                                last = pe.matmul(sc[:, 0, j], kst[:, 0, h], qst[:, h], start=True, stop=True)
                            last.then_inc(S["g_sc"], 1)
                            if turn:
                                pe.wait_ge(S["g_exp"], CT * i + g + 1)
                                weighted(0, g, S["g_pv"], probs[:, 0])
                            else:
                                pe.wait_ge(S["g_dv"], 2 + (3 + 2 * CT) * i + 3 + 2 * (g + 1))
                pe.wait_ge(S["g_dv"], 2 + (6 + 5 * CT) * NT)
                total(range(CT), S["g_den"])
                pe.wait_ge(S["g_den"], 1)
                pe.sem_inc(S["g_fin"], 1)
            with pe.Else():
                pe.nop()
            pe.wait_ge(S["norm"], 2)
            pe.wait_ge(S["wo_in"], 48)
            for t in range(CT):
                last = pe.matmul(sc[:, 1, t], bd_v[:], tok[:, t], start=True, stop=True)
            last.then_inc(S["vp"], 1)
            pe.wait_ge(S["vpE"], 1)
            for m in range(QT):
                for t in range(CT):
                    last = pe.matmul(scf[:, 0, m * D:(m + 1) * D], tok2[:, t, m * P:(m + 1) * P], wo[:, t],
                                     start=t == 0, stop=t == CT - 1)
            last.then_inc(S["proj"], 1)


def self_attention(nc, mem, sem, a, ident, ones, xres, wr, past, past_ready):
    PAIRS = NH // 2
    NU_SELF = PAIRS
    UP = SP_ // P // 2
    NU_PAST = NP * PAIRS * UP
    NU_EXACT = NH * QT * NP
    KT = NP * SP_ // P
    weights = {n: mem.sb(f"w_{n}", [P, CT, D]) for n in ("q", "k", "v", "o")}
    wrk, wrv = wr[:, 0:CT], wr[:, CT:2 * CT]
    wrq = mem.sb("wrq", [P, CT, D])
    brk_c, brq_c, bq_c, bk_c, bo_c = (mem.sb(n, [P, CT]) for n in ("brk_c", "brq_c", "bq_c", "bk_c", "bo_c"))
    rk = mem.sb("rk", [P, CT, NP * SP_])
    rv = mem.sb("rv", [P, KT, D])
    row_bias = mem.sb("row_bias", [P, 4, D])
    h = mem.sb("b_h", [P, QT, D])
    ht = mem.sb("b_ht", [P, CT, SQ])
    qpad = mem.sb("qpad", [P, CT, HG, SQ])
    kt = mem.sb("b_kt", [P, CT, SQ])
    v = mem.sb("b_v", [P, QT, D])
    ex = mem.sb("b_ex", [P, 3, 1024])
    ct = mem.sb("b_ct", [P, CT, SQ])
    inv = mem.sb("b_inv", [P, CT, NP, SQ])
    term = mem.sb("b_term", [P, SQ])
    flag = mem.sb("b_flag", [1, 1], I32)
    few = mem.sb("b_few", [P, 2])
    nmax = mem.sb("nmax", [P, NU_EXACT])
    tot = mem.sb("tot", [P, NU_EXACT])
    sc = mem.ps("b_sc", [P, 2, 1024])
    tr = mem.ps("b_tr", [P, 8, P])
    acc = mem.ps("b_acc", [P, 2, D])
    accq = acc[:].rearrange("p b (t q) -> p (b t) q", q=SQ)
    shift = wr[:].rearrange("p (n t) c -> p n (t c)", t=1)
    top = h
    pr, pt = ex[:, 0:2], inv[:].rearrange("p t s (k q) -> p (t s k) q", q=P).rearrange("p (b n) q -> p b n q", b=2)
    wg = past
    o_t, o_nat = kt, v
    r_t, r_nat, gate = ct, h, ex

    norm = Norm("bnorm", mem, sem, xres, h)
    S = {n: sem("b_" + n) for n in (
        "past_lo", "past_hi", "w_in", "wrq_in", "bias_in", "wg_in", "pmm", "pev_act", "pev_dve", "dv", "hT",
        "hE", "q", "qE", "k", "kE", "v", "vE", "filled", "read", "shift", "exp", "pv", "taken", "okrow",
        "oksum", "flag", "g_dv", "g_sc", "g_max", "g_exp", "g_norm", "g_tr", "g_ev_dve", "g_ev_act", "g_pv",
        "accE", "o", "oT", "oE", "oTE", "rq", "rqE", "rT", "rE", "gmm", "z", "ez")}

    self_units = [(pair, 0, (0, 1), 0, 1) for pair in range(PAIRS)]
    past_units = [(pair, state, (2 * UP * state + 2 * c, 2 * UP * state + 2 * c + 1), c, UP)
                  for state in range(NP) for pair in range(PAIRS) for c in range(UP)]
    all_units = self_units + past_units

    def group(u):
        return all_units[u][0] + (0 if u < NU_SELF else PAIRS * (1 + all_units[u][1]))

    LEAD = 3

    def fillings(groups):
        order = [("probe", g) for g in groups[:LEAD]]
        for n, g in enumerate(groups):
            order += [("unit", u) for u in range(len(all_units)) if group(u) == g]
            order += [("probe", g2) for g2 in groups[n + LEAD:n + LEAD + 1]]
        return order

    SELF = fillings(range(PAIRS))
    PAST = fillings(range(PAIRS, PAIRS * (1 + NP)))
    at = {what: n for n, what in enumerate(SELF + PAST)}
    last_unit = {group(u): u for u in range(len(all_units))}
    first_unit = {g: u - all_units[u][4] + 1 for g, u in last_unit.items()}

    with nc.Block() as block:
        @block.sync
        def _(sp):
            pastv = [a["past_t"][p].rearrange("(t p) k -> p t k", p=P) for p in range(NP)]
            for dst, name in ((brk_c, "brk"), (brq_c, "brq"), (bq_c, "bq"), (bk_c, "bk"), (bo_c, "bo")):
                sp.dma_start(dst[:], a[name + "_c"]).then_inc(S["bias_in"], 16)
            for n, name in enumerate(("brv", "bv", "bo", "bg")):
                sp.dma_start(row_bias[:, n], a[name].partition_broadcast(P)).then_inc(S["bias_in"], 16)
            for n in ("q", "k", "v", "o"):
                sp.dma_start(weights[n][:], a["w" + n].rearrange("(t p) o -> p t o", p=P)).then_inc(S["w_in"], 16)
            sp.dma_start(wrq[:], a["wrq"].rearrange("(t p) o -> p t o", p=P)).then_inc(S["wrq_in"], 16)
            half = SP_ // 2
            sp.wait_ge(S["pmm"], 8)
            sp.dma_start(past[:, :, 0:half], pastv[1][:, :, 0:half]).then_inc(S["past_lo"], 16)
            sp.wait_ge(S["pmm"], 16)
            sp.dma_start(past[:, :, half:], pastv[1][:, :, half:]).then_inc(S["past_hi"], 16)
            sp.wait_ge(S["pmm"], 32)
            for n in range(2):
                sp.dma_start(wg[:, :, n * D:(n + 1) * D],
                             a["wg"][n * D:(n + 1) * D].rearrange("(t p) o -> p t o", p=P)).then_inc(S["wg_in"], 16)

        slots = [sc[:, n // 2, (n % 2) * D:(n % 2 + 1) * D] for n in range(4)]

        @block.gpsimd
        def _(pool):
            for g in range(PAIRS * (1 + NP)):
                pool.wait_ge(S["read"], at["probe", g] + 1)
                if g >= PAIRS:
                    pool.wait_ge(S["read"], at["unit", last_unit[g - PAIRS]] + 1)
                pool.partition_all_reduce(shift[:, g % PAIRS], top[:, g % 2], P, RMAX).then_inc(S["shift"], 1)

        @block.scalar
        def _(act):
            act.wait_ge(S["bias_in"], 9 * 16)
            for n in range(16):
                mt, c = (n % 8) % CT, 2 * (n // 8) + (n % 8) // CT
                act.wait_ge(S["pmm"], 2 * n + 1)
                act.activation(rk[:, mt, c * D:(c + 1) * D], slots[(2 * n) % 4], ACT.Identity,
                               bias=brk_c[:, mt:mt + 1]).then_inc(S["pev_act"], 1)
            norm.scalar(act)
            act.wait_ge(S["k"], 1)
            for t in range(CT):
                last = act.activation(kt[:, t], sc[:, 1, t * SQ:(t + 1) * SQ], ACT.Identity, bias=bk_c[:, t:t + 1])
            last.then_inc(S["kE"], 1)

            def attend(order):
                for kind, u in order:
                    if kind == "unit":
                        act.wait_ge(S["read"], at[kind, u] + 1)
                        act.activation(ex[:, u % 3], ex[:, u % 3], ACT.Exp).then_inc(S["exp"], 1)

            attend(SELF)
            act.wait_ge(S["oT"], 1)
            for t in range(CT):
                last = act.activation(o_t[:, t], sc[:, 1, t * SQ:(t + 1) * SQ], ACT.Identity, bias=bo_c[:, t:t + 1])
            last.then_inc(S["oTE"], 1)
            attend(PAST)
            act.wait_ge(S["flag"], 1)
            general = act.value_load(flag[0:1, 0:1], min_val=0, max_val=1)
            with act.If(general):
                for u in range(NU_EXACT + 2):
                    if u < NU_EXACT:
                        act.wait_ge(S["g_max"], u + 1)
                        wait(act, S["g_tr"], u - 1)
                        act.activation(pr[:, u % 2], sc[:, u % 2], ACT.Exp, bias=nmax[:, u:u + 1],
                                       accum_out=tot[:, u:u + 1]).then_inc(S["g_exp"], 1)
                    if u >= 2:
                        act.wait_ge(S["g_tr"], u - 1)
                        wait(act, S["g_pv"], u - 3)
                        act.activation(pt[:, u % 2, 4:8], tr[:, 4:8], ACT.Copy).then_inc(S["g_ev_act"], 1)
            with act.Else():
                act.nop()
            act.wait_ge(S["z"], 1)
            act.activation(gate[:, 1], gate[:, 0], ACT.Exp, scale=-1.0).then_inc(S["ez"], 1)

        @block.vector
        def _(dve):
            link = Chain(dve, S["dv"])
            dve.wait_ge(S["bias_in"], 9 * 16)
            for n in range(16):
                dve.wait_ge(S["pmm"], 2 * n + 2)
                dve.tensor_tensor(rv[:, n], slots[(2 * n + 1) % 4], row_bias[:, 0], ALU.add).then_inc(S["pev_dve"], 1)
            norm.vector(dve, link)
            link(dve.memset(qpad[:], 0.0))
            dve.wait_ge(S["hT"], 1)
            dve.tensor_copy(ht[:].rearrange("p t q -> p (t q)"), tr[:].rearrange("p a b -> p (a b)"))\
               .then_inc(S["hE"], 1)

            def pad(bias, src, done):
                for t in range(CT):
                    for j in range(HG):
                        part = slice(HD * j, HD * (j + 1))
                        last = dve.tensor_scalar(qpad[part, t, j], src[part, t * SQ:(t + 1) * SQ],
                                                 bias[part, t:t + 1], SCALE, ALU.add, ALU.mult)
                    last.then_inc(done, 1)

            dve.wait_ge(S["q"], 1)
            pad(bq_c, tr[:].rearrange("p a b -> p (a b)"), S["qE"])
            dve.wait_ge(S["v"], 1)
            for m in range(QT):
                last = dve.tensor_tensor(v[:, m], acc[:, m], row_bias[:, 1], ALU.add)
            last.then_inc(S["vE"], 1)

            def probe(g):
                n = at["probe", g]
                dve.wait_ge(S["filled"], n + 1)
                wait(dve, S["shift"], g - 1)
                dve.tensor_reduce(top[:, g % 2], sc[:, n % 2].rearrange("p (k c) -> p c k", k=2), AX,
                                  ALU.max).then_inc(S["read"], 1)

            def subtract(u):
                n, g = at["unit", u], group(u)
                dve.wait_ge(S["shift"], g + 1)
                dve.wait_ge(S["filled"], n + 1)
                wait(dve, S["pv"], u - 2)
                dve.tensor_tensor(ex[:, u % 3].rearrange("p (k c) -> p k c", k=2),
                                  sc[:, n % 2].rearrange("p (k c) -> p k c", k=2),
                                  shift[:, g % PAIRS][:, None, :].to_broadcast([P, 2, 2 * SQ]),
                                  ALU.subtract).then_inc(S["read"], 1)

            def take(g):
                pair, state, _, _, count = all_units[last_unit[g]]
                t = pair // 2
                dve.wait_ge(S["pv"], last_unit[g] + 1)
                for hh in range(2):
                    dst = slice(HD * (2 * (pair % 2) + hh), HD * (2 * (pair % 2) + hh + 1))
                    num, den = (acc[64 * hh + HD * n:64 * hh + HD * (n + 1), g % 2, 0:SQ] for n in range(2))
                    dve.tensor_copy(term[dst] if state else ct[dst, t], num).then_inc(S["taken"], 1)
                    dve.tensor_copy(inv[dst, t, state], den).then_inc(S["taken"], 1)
                if pair % 2:
                    dve.wait_ge(S["taken"], 4 * (g + 1))
                    link(dve.reciprocal(inv[:, t, state], inv[:, t, state]))
                    factor = 1.0 if count == 1 else 1.0 / NP
                    raw = term[:] if state else ct[:, t]
                    link(dve.scalar_tensor_tensor(raw, raw, factor, inv[:, t, state], ALU.mult, ALU.mult))
                    if state:
                        link(dve.tensor_tensor(r_t[:, t], r_t[:, t], raw, ALU.add))

            def attend(order):
                first = at[order[0]]
                for n in range(first, first + len(order) + 3):
                    if n < first + len(order):
                        kind, what = order[n - first]
                        probe(what) if kind == "probe" else subtract(what)
                    kind, what = order[n - first - 3] if n >= first + 3 else ("", 0)
                    if kind == "unit" and last_unit[group(what)] == what:
                        take(group(what))

            attend(SELF)
            dve.sem_inc(S["accE"], 1)
            dve.wait_ge(S["o"], 1)
            for m in range(QT):
                last = dve.tensor_tensor(o_nat[:, m], sc[:, 0, m * D:(m + 1) * D], row_bias[:, 2], ALU.add)
            last.then_inc(S["oE"], 1)
            dve.wait_ge(S["rq"], 1)
            pad(brq_c, tr[:].rearrange("p a b -> p (a b)"), S["rqE"])
            attend(PAST)
            ok = ex[:, 0:2].rearrange("p a b -> p (a b)")
            invf = inv[:].rearrange("p t s q -> p (t s q)")
            count = Chain(dve, S["okrow"])
            count(dve.tensor_scalar(ok, invf, 1.0 / DEN_MAX, None, ALU.is_ge))
            count(dve.scalar_tensor_tensor(ok, invf, 1.0 / DEN_MIN, ok, ALU.is_le, ALU.mult))
            count(dve.tensor_reduce(few[:, 0:1], ok, AX, ALU.min))
            count(dve.tensor_scalar(few[:, 1:2], few[:, 0:1], 1.0, None, ALU.is_lt))
            dve.wait_ge(S["oksum"], 1)
            dve.tensor_scalar(flag[:], tr[0:1, 0, 0:1], 0.5, None, ALU.is_gt).then_inc(S["flag"], 1)
            dve.wait_ge(S["flag"], 1)
            general = dve.value_load(flag[0:1, 0:1], min_val=0, max_val=1)
            with dve.If(general):
                here = Chain(dve, S["g_dv"])
                for u in range(NU_EXACT + 2):
                    if u < NU_EXACT:
                        dve.wait_ge(S["g_sc"], u + 1)
                        dve.tensor_reduce(nmax[:, u:u + 1], sc[:, u % 2], AX, ALU.max, negate=True)\
                           .then_inc(S["g_max"], 1)
                    if 0 < u <= NU_EXACT:
                        x = u - 1
                        dve.wait_ge(S["g_exp"], x + 1)
                        here(dve.reciprocal(tot[:, x:x + 1], tot[:, x:x + 1]))
                        dve.tensor_scalar(pr[:, x % 2], pr[:, x % 2], tot[:, x:x + 1], 1.0 / NP, ALU.mult,
                                          ALU.mult).then_inc(S["g_norm"], 1)
                    if u >= 2:
                        dve.wait_ge(S["g_tr"], u - 1)
                        wait(dve, S["g_pv"], u - 3)
                        dve.tensor_copy(pt[:, u % 2, 0:4], tr[:, 0:4]).then_inc(S["g_ev_dve"], 1)
                dve.wait_ge(S["g_pv"], NU_EXACT)
                here(dve.tensor_copy(r_t[:], accq))
            with dve.Else():
                dve.nop()
            dve.sem_inc(S["accE"], 1)
            dve.wait_ge(S["rT"], 1)
            for m in range(QT):
                last = dve.tensor_copy(r_nat[:, m], tr[:, 4 * m:4 * m + 4].rearrange("p a b -> p (a b)"))
            last.then_inc(S["rE"], 1)
            dve.wait_ge(S["gmm"], 1)
            for m in range(QT):
                link(dve.tensor_tensor(gate[:, 0, m * D:(m + 1) * D], sc[:, 0, m * D:(m + 1) * D], row_bias[:, 3],
                                       ALU.add))
            dve.sem_inc(S["z"], 1)
            g = gate[:, 1].rearrange("p (m c) -> p m c", m=QT)
            dve.wait_ge(S["ez"], 1)
            link(dve.tensor_scalar(g, g, 1.0, None, ALU.add))
            link(dve.reciprocal(g, g))
            link(dve.tensor_tensor(r_nat[:], r_nat[:], o_nat[:], ALU.subtract))
            link(dve.tensor_tensor(r_nat[:], r_nat[:], g, ALU.mult))
            link(dve.tensor_tensor(r_nat[:], r_nat[:], o_nat[:], ALU.add))
            link(dve.tensor_tensor(xres[:], xres[:], r_nat[:], ALU.add))

        @block.tensor
        def _(pe):
            pe.wait_ge(past_ready, 48)
            for n in range(32):
                state, k = n // 16, (n % 16) // 2
                if n in (16, 24):
                    pe.wait_ge(S["past_lo"] if n == 16 else S["past_hi"], 16)
                wait(pe, S["pev_dve"] if n % 2 else S["pev_act"], n // 2 - 1)
                for c in range(CT):
                    if n % 2:
                        lhs, rhs = past[:, c, k * P:(k + 1) * P], wrv[:, c]
                    else:
                        lhs, rhs = wrk[:, c, (k % CT) * P:(k % CT + 1) * P], past[:, c, (k // CT) * D:(k // CT + 1) * D]
                    last = pe.matmul(slots[n % 4], lhs, rhs, start=c == 0, stop=c == CT - 1)
                last.then_inc(S["pmm"], 1)
            pe.wait_ge(norm.ready, QT)
            transpose_tokens(pe, tr[:].rearrange("p a b -> p (a b)").rearrange("p (t q) -> p t q", q=SQ), h, ident)\
                .then_inc(S["hT"], 1)
            pe.wait_ge(S["w_in"], 64)
            pe.wait_ge(S["hE"], 1)
            pe.wait_ge(S["pev_dve"], 16)
            pe.wait_ge(S["pev_act"], 16)

            def project_t(dst, w, src):
                for mt in range(CT):
                    for c in range(CT):
                        last = pe.matmul(dst[:, mt * SQ:(mt + 1) * SQ], w[:, c, mt * P:(mt + 1) * P], src[:, c],
                                         start=c == 0, stop=c == CT - 1)
                return last

            def project(dst, w, src):
                for m in range(QT):
                    for c in range(CT):
                        last = pe.matmul(dst[:, m * D:(m + 1) * D], src[:, c, m * P:(m + 1) * P], w[:, c],
                                         start=c == 0, stop=c == CT - 1)
                return last

            trf = tr[:].rearrange("p a b -> p (a b)")
            accf = acc[:].rearrange("p a b -> p (a b)")
            project_t(trf, weights["q"], ht).then_inc(S["q"], 1)
            project_t(sc[:, 1], weights["k"], ht).then_inc(S["k"], 1)
            project(accf, weights["v"], ht).then_inc(S["v"], 1)
            def fill(n, keys, pair, tiles):
                wait(pe, S["read"], n - 1)
                for k in range(2):
                    last = pe.matmul(sc[:, n % 2, k * D:(k + 1) * D],
                                     keys[:, pair // 2, tiles[k] * P:(tiles[k] + 1) * P],
                                     qpad[:, pair // 2, 2 * (pair % 2):2 * (pair % 2) + 2], start=True, stop=True)
                last.then_inc(S["filled"], 1)

            def weighted(x, values):
                pair, _, tiles, c, count = all_units[x]
                g = group(x)
                pe.wait_ge(S["exp"], x + 1)
                if c == 0:
                    wait(pe, S["taken"], 4 * (g - 1))
                for k in range(2):
                    for hh in range(2):
                        head = 2 * pair + hh
                        for n, lhs in enumerate((values[:, tiles[k], head * HD:(head + 1) * HD], ones[:, 0:HD])):
                            to = 64 * hh + HD * n
                            last = pe.matmul(acc[to:to + HD, g % 2, 0:SQ], lhs,
                                             ex[:, x % 3, k * D + hh * SQ:k * D + (hh + 1) * SQ],
                                             start=c == 0 and k == 0, stop=c == count - 1 and k == 1,
                                             skip_group_check=True, tile_position=(0, to))
                last.then_inc(S["pv"], 1)

            def attend(order, keys, values, queries, values_ready):
                first = at[order[0]]
                for n in range(first, first + len(order) + 2):
                    if n < first + len(order):
                        kind, what = order[n - first]
                        g = what if kind == "probe" else group(what)
                        pair, _, tiles, _, _ = all_units[first_unit[g] if kind == "probe" else what]
                        if kind == "probe":
                            pe.wait_ge(queries, pair // 2 + 1)
                        fill(n, keys, pair, tiles)
                    kind, what = order[n - first - 2] if n >= first + 2 else ("", 0)
                    if kind == "unit":
                        if what == 0:
                            pe.wait_ge(values_ready, 1)
                        weighted(what, values)

            pe.wait_ge(S["kE"], 1)
            attend(SELF, kt, v, S["qE"], S["vE"])
            pe.wait_ge(S["accE"], 1)
            project_t(sc[:, 1], weights["o"], ct).then_inc(S["oT"], 1)
            project(sc[:, 0], weights["o"], ct).then_inc(S["o"], 1)
            pe.wait_ge(S["oTE"], 1)
            pe.wait_ge(S["wrq_in"], 16)
            project_t(trf, wrq, o_t).then_inc(S["rq"], 1)
            pe.wait_ge(S["oE"], 1)
            attend(PAST, rk, rv, S["rqE"], None)
            pe.wait_ge(S["okrow"], 4)
            pe.matmul(tr[0:1, 0, 0:1], few[:, 1:2], ones[:, 0:1], start=True, stop=True).then_inc(S["oksum"], 1)
            pe.wait_ge(S["flag"], 1)
            general = pe.value_load(flag[0:1, 0:1], min_val=0, max_val=1)
            with pe.If(general):
                for u in range(NU_EXACT + 2):
                    if u < NU_EXACT:
                        head, m, state = u // (QT * NP), u // NP % QT, u % NP
                        wait(pe, S["g_exp"], u - 1)
                        for n in range(SP_ // D):
                            key = state * SP_ + n * D
                            last = pe.matmul(sc[:, u % 2, n * D:(n + 1) * D],
                                             qpad[:, head // HG, head % HG, m * P:(m + 1) * P],
                                             rk[:, head // HG, key:key + D], start=True, stop=True)
                        last.then_inc(S["g_sc"], 1)
                    if 0 < u <= NU_EXACT:
                        pe.wait_ge(S["g_norm"], u)
                        wait(pe, S["g_ev_dve"], u - 1)
                        wait(pe, S["g_ev_act"], u - 1)
                        for b in range(8):
                            last = pe.transpose(tr[:, b], pr[:, (u - 1) % 2, b * P:(b + 1) * P], ident[:])
                        last.then_inc(S["g_tr"], 1)
                    if u >= 2:
                        x = u - 2
                        head, m, state = x // (QT * NP), x // NP % QT, x % NP
                        t, j = head // HG, head % HG
                        pe.wait_ge(S["g_ev_dve"], x + 1)
                        pe.wait_ge(S["g_ev_act"], x + 1)
                        for k in range(8):
                            last = pe.matmul(accq[HD * j:HD * (j + 1), t, m * P:(m + 1) * P],
                                             rv[:, 8 * state + k, head * HD:(head + 1) * HD], pt[:, x % 2, k],
                                             start=state == 0 and k == 0, stop=state == NP - 1 and k == 7,
                                             skip_group_check=True, tile_position=(0, HD * j))
                        last.then_inc(S["g_pv"], 1)
            with pe.Else():
                pe.nop()
            pe.wait_ge(S["accE"], 2)
            for m in range(QT):
                for t in range(CT):
                    last = pe.transpose(tr[:, 4 * m + t], r_t[:, t, m * P:(m + 1) * P], ident[:])
            last.then_inc(S["rT"], 1)
            pe.wait_ge(S["wg_in"], 32)
            for m in range(QT):
                for c in range(2 * CT):
                    src = (o_t if c < CT else r_t)[:, c % CT, m * P:(m + 1) * P]
                    last = pe.matmul(sc[:, 0, m * D:(m + 1) * D], src, wg[:, c % CT, (c // CT) * D:(c // CT + 1) * D],
                                     start=c == 0, stop=c == 2 * CT - 1)
            last.then_inc(S["gmm"], 1)


def experts(nc, mem, sem, a, ident, ones, xres, out):
    MORE = (2 * SQ - NE) // P
    w1 = mem.sb("w1", [P, 2, CT, FF])
    w2 = mem.sb("w2", [P, 2, FT, D])
    h = mem.sb("c_h", [P, QT, D])
    ht = mem.sb("c_ht", [P, CT, SQ])
    gw = mem.sb("gw", [P, CT, NE])
    b1 = mem.sb("b1", [P, NE, FT])
    b2 = mem.sb("b2", [NE, D])
    iota = mem.sb("iota", [P, NE])
    prob = mem.sb("prob", [P, QT, NE])
    share = mem.sb("share", [P, QT, NE])
    share_t = mem.sb("share_t", [NE, SQ])
    best = mem.sb("best", [P, QT, 8])
    which = mem.sb("which", [P, QT, 8], U32)
    whichf = mem.sb("whichf", [P, QT, 8])
    pick = mem.sb("pick", [P, QT, 2, NE])
    one = mem.sb("one", [P, QT, 4])
    hid = mem.sb("hid", [P, 2, FT, P])
    count_to = mem.sb("count_to", [P, P])
    row_no = mem.sb("row_no", [P, 1])
    before = mem.sb("before", [P, P])
    chosen = mem.sb("chosen", [P, QT, NE])
    place = mem.sb("place", [P, QT, NE])
    place2 = mem.sb("place2", [P, QT, NE])
    over = mem.sb("over", [NE, 2])
    second = mem.sb("second", [NE, MORE])
    extra = mem.sb("extra", [1, 2 * MORE], I32)
    ident_r = mem.sb("c_ident_r", [P, P], F32R)
    h_hi = mem.sb("h_hi", [P, QT, D], F32R)
    h_lo = mem.sb("h_lo", [P, QT, D], F32R)
    to_place = mem.sb("to_place", [P, 2, QT, P], F32R)
    from_place = mem.sb("from_place", [P, 2, SQ], F32R)
    mine = mem.sb("mine", [P, 2, CT, P])
    y_hi = mem.sb("y_hi", [P, D], F32R)
    y_lo = mem.sb("y_lo", [P, D], F32R)
    total = mem.sb("total", [P, QT, D])
    up = mem.ps("up", [P, 2, 4 * P])
    mine_ps = mem.ps("mine_ps", [P, CT * P])
    back_ps = mem.ps("back_ps", [P, D])
    down = mem.ps("down", [P, 2, D])
    small = mem.ps("c_small", [P, D])
    y = mem.ps("c_y", [P, D])

    norm = Norm("cnorm", mem, sem, xres, h)
    S = {n: sem("c_" + n) for n in (
        "gate_in", "b_in", "iota", "dv", "hT", "hE", "logit", "nmax", "p", "share", "chosen", "counted", "over",
        "extra", "split", "sel", "gathered", "mine", "back", "y", "y_hi", "y_lo", "scattered", "shT", "shE",
        "b2", "up", "gelu", "down", "added", "out", "done")}
    w1_in = [sem(f"w1_in{b}") for b in range(2)]
    w2_in = [sem(f"w2_in{b}") for b in range(2)]
    w1v = a["w1"].rearrange("e (t p) f -> e p t f", p=P)
    w2v = a["w2"].rearrange("e (t p) f -> e p t f", p=P)
    PAIRS = NE // 2
    C_SHARE = 64
    C_PLACE = C_SHARE + SQ
    C_EXTRA = 2

    def second_jobs(eng):
        eng.wait_ge(S["extra"], 1)
        for n in range(MORE):
            yield (NE + n, n % 2, eng.value_load(extra[0:1, n:n + 1], min_val=0, max_val=NE - 1),
                   eng.value_load(extra[0:1, MORE + n:MORE + n + 1], min_val=0, max_val=1))

    def last_pair(i):
        return isinstance(i, int) and i == PAIRS - 1

    with nc.Block() as block:
        @block.sync
        def _(sp):
            sp.dma_start(gw[:], a["gate_t"].rearrange("(t p) e -> p t e", p=P)).then_inc(S["gate_in"], 16)
            for b in range(2):
                sp.dma_start(w1[:, b], w1v[b]).then_inc(w1_in[b], 16)
                sp.dma_start(w2[:, b], w2v[b]).then_inc(w2_in[b], 16)
            sp.dma_start(b1[:], a["b1_c"]).then_inc(S["b_in"], 16)
            sp.dma_start(b2[:], a["b2"]).then_inc(S["b_in"], 16)

            def load(job, e, b):
                sp.wait_ge(S["up"], 2 * (job - 1))
                sp.dma_start(w1[:, b], w1v[e]).then_inc(w1_in[b], 16)
                sp.wait_ge(S["y"], job - 1)
                sp.dma_start(w2[:, b], w2v[e]).then_inc(w2_in[b], 16)

            with sp.Fori(1, PAIRS) as i:
                for b in range(2):
                    load(2 * i + b, 2 * i + b, b)
            for job, b, e, wanted in second_jobs(sp):
                with sp.If(wanted):
                    load(job, e, b)
                with sp.Else():
                    sp.nop()
            sp.wait_ge(S["out"], 1)
            sp.dma_start(out.rearrange("(t p) c -> p t c", p=P), total[:]).then_inc(S["done"], 16)
            sp.wait_ge(S["done"], 16)

        @block.gpsimd
        def _(pool):
            pool.iota(iota[:], [[1, NE]], base=0, channel_multiplier=0,
                      allow_small_or_imprecise_dtypes=True).then_inc(S["iota"], 1)
            pool.iota(count_to[:], [[1, P]], base=0, channel_multiplier=0,
                      allow_small_or_imprecise_dtypes=True).then_inc(S["iota"], 1)
            pool.iota(row_no[:], [[0, 1]], base=0, channel_multiplier=1,
                      allow_small_or_imprecise_dtypes=True).then_inc(S["iota"], 1)

        @block.scalar
        def _(act):
            norm.scalar(act)
            for m in range(QT):
                act.wait_ge(S["nmax"], 1)
                act.activation(prob[:, m], small[:, m * NE:(m + 1) * NE], ACT.Exp, bias=one[:, m, 0:1],
                               accum_out=one[:, m, 1:2]).then_inc(S["p"], 1)
            act.wait_ge(S["b_in"], 32)

            def own_tokens(e, b):
                act.wait_ge(S["gathered"], e + 1)
                wait(act, S["up"], 2 * (e - 1))
                act.activation(mine[:, b], mine_ps[:].rearrange("p (c k) -> p c k", k=P), ACT.Copy)\
                   .then_inc(S["mine"], 1)

            def job(n, e, b):
                for s in range(2):
                    act.wait_ge(S["up"], 2 * n + s + 1)
                    wait(act, S["y"], n - 1)
                    for f in range(4):
                        last = act.activation(hid[:, b, 4 * s + f], up[:, s, f * P:(f + 1) * P], ACT.Gelu,
                                              bias=b1[:, bass.ds(e, 1), 4 * s + f])
                    last.then_inc(S["gelu"], 1)

            def result(n):
                act.wait_ge(S["y"], n + 1)
                act.activation(y_hi[:], y[:], ACT.Copy).then_inc(S["y_hi"], 1)

            def pair(i):
                for b in range(2):
                    e = 2 * i + b
                    job(e, e, b)
                    if not last_pair(i) or b == 0:
                        own_tokens(e + 1, 1 - b)
                    result(e)

            own_tokens(0, 0)
            pair(0)
            with act.Fori(1, PAIRS - 1) as i:
                pair(i)
            pair(PAIRS - 1)
            for n, b, e, wanted in second_jobs(act):
                with act.If(wanted):
                    own_tokens(n, b)
                    job(n, e, b)
                    result(n)
                with act.Else():
                    act.nop()

        @block.vector
        def _(dve):
            link = Chain(dve, S["dv"])
            norm.vector(dve, link)
            dve.wait_ge(S["hT"], 1)
            dve.tensor_copy(ht[:], down[:].rearrange("p m (t q) -> p (m t) q", q=SQ)).then_inc(S["hE"], 1)
            dve.wait_ge(S["logit"], 1)
            dve.tensor_reduce(one[:, :, 0], small[:, 0:QT * NE].rearrange("p (m e) -> p m e", m=QT), AX, ALU.max,
                              negate=True).then_inc(S["nmax"], 1)
            link(dve.tensor_copy(ident_r[:], ident[:]))
            link(dve.tensor_copy(h_hi[:], h[:]))
            link(dve.tensor_tensor(h_lo[:], h[:], h_hi[:].bitcast(F32), ALU.subtract))
            dve.wait_ge(S["iota"], 3)
            link(dve.tensor_scalar(before[:], count_to[:], row_no[:, 0:1], None, ALU.is_gt))
            dve.sem_inc(S["split"], 1)
            def each(ap):
                return ap.to_broadcast([P, QT, NE])

            dve.wait_ge(S["p"], QT)
            link(dve.reciprocal(one[:, :, 2], one[:, :, 1]))
            link(dve.tensor_tensor(prob[:], prob[:], each(one[:, :, 2:3]), ALU.mult))
            for m in range(QT):
                link(dve.max(best[:, m], prob[:, m]))
                link(dve.max_index(which[:, m], best[:, m], prob[:, m]))
            link(dve.tensor_copy(whichf[:], which[:]))
            for n in range(2):
                link(dve.tensor_tensor(pick[:, :, n], iota[:][:, None, :].to_broadcast([P, QT, NE]),
                                       each(whichf[:, :, n:n + 1]), ALU.is_equal))
            dve.tensor_tensor(chosen[:], pick[:, :, 0], pick[:, :, 1], ALU.add).then_inc(S["chosen"], 1)
            dve.wait_ge(S["chosen"], 1)
            link(dve.tensor_scalar(place[:], chosen[:], -2.0 * SQ, 2.0 * SQ, ALU.mult, ALU.add))
            dve.wait_ge(S["counted"], 1)
            link(dve.tensor_tensor(place[:], place[:],
                                   small[:, C_PLACE:C_PLACE + QT * NE].rearrange("p (m e) -> p m e", m=QT), ALU.add))

            def shares():
                link(dve.tensor_tensor(one[:, :, 3], best[:, :, 0], best[:, :, 1], ALU.add))
                link(dve.tensor_scalar(one[:, :, 3], one[:, :, 3], 1e-10, None, ALU.max))
                link(dve.reciprocal(one[:, :, 3], one[:, :, 3]))
                for n in range(2):
                    link(dve.tensor_tensor(pick[:, :, n], pick[:, :, n], each(best[:, :, n:n + 1]), ALU.mult))
                link(dve.tensor_tensor(share[:], pick[:, :, 0], pick[:, :, 1], ALU.add))
                link(dve.tensor_tensor(share[:], share[:], each(one[:, :, 3:4]), ALU.mult))
                dve.sem_inc(S["share"], 1)
                dve.wait_ge(S["shT"], 1)
                dve.tensor_copy(share_t[:], small[0:NE, C_SHARE:C_SHARE + SQ]).then_inc(S["shE"], 1)
                dve.wait_ge(S["b2"], 1)
                for m in range(QT):
                    dve.tensor_tensor(total[:, m], h[:, m], down[:, m], ALU.add).then_inc(S["added"], 1)

            def second_jobs_list():
                over_jobs = Chain(dve, S["over"])
                over_jobs(dve.tensor_scalar(over[:, 0:1], y[0:NE, 0:1], P + 0.5, None, ALU.is_gt))
                link(dve.tensor_scalar(place2[:], place[:], -float(P), None, ALU.add))
                dve.wait_ge(S["counted"], 2)
                over_jobs(dve.tensor_copy(over[:, 1:2], y[0:NE, 1:2]))
                dve.tensor_scalar(second[:], count_to[0:NE, 0:MORE], over[:, 1:2], over[:, 0:1], ALU.is_equal,
                                  ALU.mult).then_inc(S["over"], 1)
                dve.wait_ge(S["counted"], 3)
                dve.tensor_copy(extra[:], y[0:1, C_EXTRA:C_EXTRA + 2 * MORE]).then_inc(S["extra"], 1)

            def select(n, e, b, place=place):
                wait(dve, S["gathered"], n - 1)
                for m in range(QT):
                    last = dve.tensor_scalar(to_place[:, b, m], count_to[:], place[:, m, bass.ds(e, 1)], None,
                                             ALU.is_equal)
                last.then_inc(S["sel"], 1)

            def back(e, b):
                dve.wait_ge(S["gathered"], e + 1)
                wait(dve, S["scattered"], e - 1)
                dve.tensor_copy(from_place[:, b], back_ps[:, 0:SQ]).then_inc(S["back"], 1)

            def add(n, e):
                dve.wait_ge(S["scattered"], n + 1)
                dve.wait_ge(S["added"], QT * (n + 1))
                for m in range(QT):
                    dve.scalar_tensor_tensor(total[:, m], down[:, m], share[:, m, bass.ds(e, 1)], total[:, m],
                                             ALU.mult, ALU.add).then_inc(S["added"], 1)

            def result(n):
                dve.wait_ge(S["y_hi"], n + 1)
                dve.tensor_tensor(y_lo[:], y[:], y_hi[:].bitcast(F32), ALU.subtract).then_inc(S["y_lo"], 1)

            def pair(i):
                for b in range(2):
                    e = 2 * i + b
                    if not last_pair(i) or b == 0:
                        select(e + 1, e + 1, 1 - b)
                        back(e + 1, 1 - b)
                    if isinstance(e, int) and e == 0:
                        shares()
                    else:
                        add(e - 1, e - 1)
                    result(e)

            select(0, 0, 0)
            second_jobs_list()
            back(0, 0)
            pair(0)
            with dve.Fori(1, PAIRS - 1) as i:
                pair(i)
            pair(PAIRS - 1)
            add(NE - 1, NE - 1)
            dve.wait_ge(S["added"], QT * (NE + 1))
            for n, b, e, wanted in second_jobs(dve):
                with dve.If(wanted):
                    select(n, e, b, place2)
                    back(n, b)
                    result(n)
                    add(n, e)
                    dve.wait_ge(S["added"], QT * (n + 2))
                with dve.Else():
                    dve.nop()
            link(dve.tensor_scalar(total[:], total[:], -100.0, 100.0, ALU.max, ALU.min))
            dve.tensor_tensor(total[:], total[:], xres[:], ALU.add).then_inc(S["out"], 1)

        @block.tensor
        def _(pe):
            pe.wait_ge(norm.ready, QT)
            transpose_tokens(pe, down[:].rearrange("p m (t q) -> p (m t) q", q=SQ), h, ident).then_inc(S["hT"], 1)
            pe.wait_ge(S["gate_in"], 16)
            pe.wait_ge(S["hE"], 1)
            for m in range(QT):
                for c in range(CT):
                    last = pe.matmul(small[:, m * NE:(m + 1) * NE], ht[:, c, m * P:(m + 1) * P], gw[:, c],
                                     start=c == 0, stop=c == CT - 1)
            last.then_inc(S["logit"], 1)
            pe.wait_ge(S["chosen"], 1)
            pe.wait_ge(S["split"], 1)
            for m in range(QT):
                to = C_PLACE + m * NE
                pe.matmul(small[:, to:to + NE], before[:], chosen[:, m], start=True, stop=m == 0)
                if m:
                    pe.matmul(small[:, to:to + NE], ones[:], chosen[:, 0], start=False, stop=True)
            for m in range(QT):
                last = pe.matmul(y[0:NE, 0:1], chosen[:, m], ones[:, 0:1], start=m == 0, stop=m == QT - 1)
            last.then_inc(S["counted"], 1)

            def gather(e, b):
                pe.wait_ge(S["sel"], e + 1)
                wait(pe, S["mine"], e)
                wait(pe, S["back"], e)
                for c in range(CT):
                    for m in range(QT):
                        for part in (h_hi, h_lo):
                            pe.matmul(mine_ps[:, c * P:(c + 1) * P], part[:, m, c * P:(c + 1) * P], to_place[:, b, m],
                                      start=m == 0 and part is h_hi, stop=m == QT - 1 and part is h_lo)
                for m in range(QT):
                    last = pe.matmul(back_ps[:, m * P:(m + 1) * P], to_place[:, b, m], ident_r[:],
                                     start=True, stop=True)
                last.then_inc(S["gathered"], 1)

            def scatter(e, b):
                pe.wait_ge(S["y_lo"], e + 1)
                pe.wait_ge(S["back"], e + 1)
                pe.wait_ge(S["added"], QT * (e + 1))
                for m in range(QT):
                    for part in (y_hi, y_lo):
                        last = pe.matmul(down[:, m], from_place[:, b, m * P:(m + 1) * P], part[:],
                                         start=part is y_hi, stop=part is y_lo)
                last.then_inc(S["scattered"], 1)

            def first_product(n, b, seen):
                pe.wait_ge(w1_in[b], seen)
                pe.wait_ge(S["mine"], n + 1)
                for s in range(2):
                    wait(pe, S["gelu"], 2 * n + s - 1)
                    for f in range(4):
                        for c in range(CT):
                            last = pe.matmul(up[:, s, f * P:(f + 1) * P],
                                             w1[:, b, c, (4 * s + f) * P:(4 * s + f + 1) * P],
                                             mine[:, b, c], start=c == 0, stop=c == CT - 1)
                    last.then_inc(S["up"], 1)

            def second_product(n, b, seen):
                pe.wait_ge(w2_in[b], seen)
                pe.wait_ge(S["gelu"], 2 * n + 2)
                for f in range(FT):
                    last = pe.matmul(y[:], hid[:, b, f], w2[:, b, f], start=f == 0, stop=f == FT - 1)
                last.then_inc(S["y"], 1)

            def pair(i):
                for b in range(2):
                    e = 2 * i + b
                    first_product(e, b, 16 * (i + 1))
                    if not last_pair(i) or b == 0:
                        gather(e + 1, 1 - b)
                    if isinstance(e, int) and e == 0:
                        biases()
                    else:
                        scatter(e - 1, 1 - b)
                    second_product(e, b, 16 * (i + 1))

            def biases():
                pe.wait_ge(S["share"], 1)
                for m in range(QT):
                    last = pe.transpose(small[0:NE, C_SHARE + m * P:C_SHARE + (m + 1) * P], share[:, m], ident[:])
                last.then_inc(S["shT"], 1)
                pe.wait_ge(S["b_in"], 32)
                pe.wait_ge(S["shE"], 1)
                for m in range(QT):
                    last = pe.matmul(down[:, m], share_t[:, m * P:(m + 1) * P], b2[:], start=True, stop=True)
                last.then_inc(S["b2"], 1)

            gather(0, 0)
            pe.wait_ge(S["over"], 1)
            pe.matmul(y[0:NE, 1:2], before[0:NE, 0:NE], over[:, 0:1], start=True, stop=True)\
              .then_inc(S["counted"], 1)
            pe.wait_ge(S["over"], 3)
            for n, lhs in enumerate((row_no, ones)):
                last = pe.matmul(y[0:1, C_EXTRA + n * MORE:C_EXTRA + (n + 1) * MORE], lhs[0:NE, 0:1], second[:],
                                 start=True, stop=True)
            last.then_inc(S["counted"], 1)
            pair(0)
            with pe.Fori(1, PAIRS - 1) as i:
                pair(i)
            pair(PAIRS - 1)
            scatter(NE - 1, 1)
            for n, b, e, wanted in second_jobs(pe):
                with pe.If(wanted):
                    gather(n, b)
                    first_product(n, b, 16 * (n // 2 + 1))
                    second_product(n, b, 16 * (n // 2 + 1))
                    scatter(n, b)
                with pe.Else():
                    pe.nop()


INPUTS = {"x": [SQ, D], "ctx": [SK, D], "mask_t": [SK, SQ], "bd_wq_t": [P, P], "bd_wk": [P, HG, STACK],
          "bd_wv_t": [P, P], "x_wo_t": [D, D], "x_bo": [D], "wq": [D, D], "wk": [D, D], "wv": [D, D], "wo": [D, D],
          "past_t": [NP, D, SP_], "wrk": [D, D], "wrv": [D, D], "wrq": [D, D], "wg": [2 * D, D],
          "brk_c": [P, CT], "brq_c": [P, CT], "bq_c": [P, CT], "bk_c": [P, CT], "bo_c": [P, CT],
          "brv": [D], "bv": [D], "bo": [D], "bg": [D],
          "gate_t": [D, NE], "w1": [NE, D, FF], "w2": [NE, FF, D], "b1_c": [P, NE, FT], "b2": [NE, D]}


def kernel(**inputs):
    import concourse.bacc as bacc
    from concourse.bass_utils import run_bass_kernel_spmd

    given = {k: np.asarray(v) for k, v in inputs.items()}

    def blocks(w):
        m = np.zeros((P, P), w.dtype)
        for j in range(HG):
            m[HD * j:HD * (j + 1), HD * j:HD * (j + 1)] = w
        return m

    arrays = {
        "x": given["x"][0], "ctx": given["ctx_1024"][0], "mask_t": given["mask_Bx1xSxS2_ik1"][0, 0].T,
        "bd_wq_t": blocks(given["L0_xattn_Wq"].T), "bd_wv_t": blocks(given["L0_xattn_Wv"].T),
        "bd_wk": np.concatenate([blocks(given["L0_xattn_Wk"]).reshape(P, HG, HD)] * 3, axis=2),
        "x_wo_t": given["L0_xattn_Wo"].T, "x_bo": given["L0_xattn_bo"],
        "past_t": given["L0_attn_past_states"][:, 0, :SP_].transpose(0, 2, 1),
        "gate_t": given["L0_ffn_gate_w"].T, "w1": given["L0_ffn_w1"], "w2": given["L0_ffn_w2"],
        "b1_c": given["L0_ffn_b1"].reshape(NE, FT, P).transpose(2, 0, 1), "b2": given["L0_ffn_b2"],
        "wq": given["L0_attn_Wq"], "wk": given["L0_attn_Wk"], "wv": given["L0_attn_Wv"], "wo": given["L0_attn_Wo"],
    }
    arrays |= {n.lower(): given["L0_attn_" + n] for n in ("Wrk", "Wrv", "Wrq", "Wg", "brv", "bv", "bo", "bg")}
    arrays |= {n + "_c": given["L0_attn_" + n].reshape(CT, P).T for n in ("brk", "brq", "bq", "bk", "bo")}
    arrays = {"in_" + k: np.ascontiguousarray(v) for k, v in arrays.items()}
    nc = bacc.Bacc("TRN2", target_bir_lowering=False, num_devices=1)
    aps = {}
    for name, shape in INPUTS.items():
        assert list(arrays["in_" + name].shape) == shape, name
        aps[name] = nc.dram_tensor("in_" + name, shape, mybir.dt.from_np(arrays["in_" + name].dtype), kind="ExternalInput").ap()
    out = nc.dram_tensor("out", [SQ, D], F32, kind="ExternalOutput").ap()
    build(nc, aps, out)
    result = run_bass_kernel_spmd(nc, [arrays], core_ids=[0])
    return result.results[0]["out"][None]
```
